# Optimizing a Trainium2 kernel written in Bass

```python
import numpy as np
import jax
import jax.numpy as jnp

def _softmax(x, axis=-1):
    return jax.nn.softmax(x, axis=axis)

def _gelu(x):
    return jax.nn.gelu(x, approximate=True)

def _silu(x):
    return jax.nn.silu(x)

def _sigmoid(x):
    return jax.nn.sigmoid(x)

def _layernorm(x, axis=-1, eps=1e-05):
    m = jnp.mean(x, axis=axis, keepdims=True)
    v = jnp.var(x, axis=axis, keepdims=True)
    return (x - m) / jnp.sqrt(v + eps)

def _scatter_add(tgt, idx, src, axis=0):
    return tgt.at[idx].add(src)

def _segment_sum(src, seg, n):
    return jax.ops.segment_sum(src, seg, n)
kernel_name = 'mk_seq_postln_d2_jaxref_r8_8be355'

def setup_inputs(seed: int=0):
    np.random.seed(seed)
    _w = jnp.asarray

    def _L0_attn_setup():
        import jax, jax.numpy as jnp
        import numpy as np
        N_HEAD = 16

        def _rope_cache(T, head_dim):
            half = head_dim // 2
            inv_freq = 1.0 / 10000.0 ** (jnp.arange(half, dtype=jnp.float32) / half)
            t = jnp.arange(T, dtype=jnp.float32)
            freqs = jnp.einsum('i,j->ij', t, inv_freq)
            cos = jnp.repeat(jnp.cos(freqs), 2, axis=-1)
            sin = jnp.repeat(jnp.sin(freqs), 2, axis=-1)
            return (cos, sin)

        def _apply_rope(x, cos, sin):
            x1 = x[..., ::2]
            x2 = x[..., 1::2]
            x_rot = jnp.stack([-x2, x1], axis=-1).reshape(x.shape)
            return x * cos[None, None] + x_rot * sin[None, None]
        key = jax.random.key(seed)
        k1, k2, k3 = jax.random.split(key, 3)
        B, T, C = (2, 256, 128)
        x = jax.random.normal(k1, (B, T, C), dtype=jnp.float32)
        Wqkv = jax.random.normal(k2, (C, 3 * C), dtype=jnp.float32) * 0.02
        Wo = jax.random.normal(k3, (C, C), dtype=jnp.float32) * 0.02
        bo = jnp.zeros((C,), dtype=jnp.float32)
        return {'x': x, 'Wqkv': Wqkv, 'Wo': Wo, 'bo': bo}
    _L0_attn_in = _L0_attn_setup()

    def _L0_ffn_setup():
        import jax, jax.numpy as jnp
        import numpy as np
        B, S, H, E, I, K = (2, 256, 128, 8, 128, 2)
        ALPHA, LIMIT = (1.702, 7.0)
        key = jax.random.key(seed)
        ks = jax.random.split(key, 5)
        sc = 0.02
        return {'hidden_states': jax.random.normal(ks[0], (B, S, H), jnp.float32), 'router_weight': jax.random.normal(ks[1], (H, E), jnp.float32) * sc, 'gate_up_proj': jax.random.normal(ks[2], (E, H, 2 * I), jnp.float32) * sc, 'gate_up_proj_bias': jnp.zeros((E, 2 * I), jnp.float32), 'down_proj': jax.random.normal(ks[3], (E, I, H), jnp.float32) * sc, 'down_proj_bias': jnp.zeros((E, H), jnp.float32)}
    _L0_ffn_in = _L0_ffn_setup()

    def _L1_attn_setup():
        import jax, jax.numpy as jnp
        import numpy as np
        import math
        FEATURE_DIM = 16
        NUM_HEADS = 16
        HIDDEN = 128
        HEAD_DIM = HIDDEN // NUM_HEADS
        EPS = 1e-12
        IU, JU = np.triu_indices(FEATURE_DIM, 1)
        RD = math.sqrt(FEATURE_DIM)
        RRD = math.sqrt(RD)
        R2 = math.sqrt(2.0)

        def taylor_feature_map(x):
            x2 = x[..., :, None] * x[..., None, :]
            off = x2[..., IU, JU]
            diag = jnp.square(x)
            ones = jnp.ones_like(x[..., :1])
            return jnp.concatenate([ones, x / RRD, diag / (RD * R2), off / RD], axis=-1)
        key = jax.random.key(seed)
        k0, k1, k2, k3, k4 = jax.random.split(key, 5)
        b, t = (2, 64)
        s = 1.0 / math.sqrt(HIDDEN)
        return {'hidden_states': jax.random.normal(k0, (b, t, HIDDEN), jnp.float32), 'Wq': jax.random.normal(k1, (NUM_HEADS * FEATURE_DIM, HIDDEN), jnp.float32) * s, 'Wk': jax.random.normal(k2, (NUM_HEADS * FEATURE_DIM, HIDDEN), jnp.float32) * s, 'Wv': jax.random.normal(k3, (HIDDEN, HIDDEN), jnp.float32) * s, 'Wo': jax.random.normal(k4, (HIDDEN, HIDDEN), jnp.float32) * s}
    _L1_attn_in = _L1_attn_setup()

    def _L1_ffn_setup():
        import jax, jax.numpy as jnp
        import numpy as np
        EMBED_DIM = 128
        MLP_RATIO = 4
        NUM_EXPERTS = 8
        CAPACITY = 1.0
        LN_EPS = 1e-05

        def _layernorm(y, gamma, beta):
            mu = jnp.mean(y, axis=-1, keepdims=True)
            var = jnp.mean(jnp.square(y - mu), axis=-1, keepdims=True)
            return (y - mu) * jax.lax.rsqrt(var + LN_EPS) * gamma + beta
        key = jax.random.key(seed)
        k0, k1, k2, k3, k4, k5 = jax.random.split(key, 6)
        d = EMBED_DIM
        dd = EMBED_DIM * MLP_RATIO
        n = NUM_EXPERTS
        x = jax.random.normal(k0, (4, 256, d), dtype=jnp.float32)
        gate_w = jax.random.normal(k1, (n, d), dtype=jnp.float32) * 0.02
        ln_gamma = jnp.ones((d,), dtype=jnp.float32)
        ln_beta = jnp.zeros((d,), dtype=jnp.float32)
        fc1s = jax.random.normal(k2, (n, dd, d), dtype=jnp.float32) * (1.0 / np.sqrt(d))
        b1s = jax.random.normal(k3, (n, dd), dtype=jnp.float32) * 0.02
        fc2s = jax.random.normal(k4, (n, d, dd), dtype=jnp.float32) * (1.0 / np.sqrt(dd))
        b2s = jax.random.normal(k5, (n, d), dtype=jnp.float32) * 0.02
        return {'x': x, 'gate_w': gate_w, 'ln_gamma': ln_gamma, 'ln_beta': ln_beta, 'fc1s': fc1s, 'b1s': b1s, 'fc2s': fc2s, 'b2s': b2s}
    _L1_ffn_in = _L1_ffn_setup()
    _d = {'L0_attn_x': _L0_attn_in['x'], 'L0_attn_Wqkv': _L0_attn_in['Wqkv'], 'L0_attn_Wo': _L0_attn_in['Wo'], 'L0_attn_bo': _L0_attn_in['bo'], 'L0_ffn_router_weight': _L0_ffn_in['router_weight'], 'L0_ffn_gate_up_proj': _L0_ffn_in['gate_up_proj'], 'L0_ffn_gate_up_proj_bias': _L0_ffn_in['gate_up_proj_bias'], 'L0_ffn_down_proj': _L0_ffn_in['down_proj'], 'L0_ffn_down_proj_bias': _L0_ffn_in['down_proj_bias'], 'L1_attn_Wq': _L1_attn_in['Wq'], 'L1_attn_Wk': _L1_attn_in['Wk'], 'L1_attn_Wv': _L1_attn_in['Wv'], 'L1_attn_Wo': _L1_attn_in['Wo'], 'L1_ffn_gate_w': _L1_ffn_in['gate_w'], 'L1_ffn_ln_gamma': _L1_ffn_in['ln_gamma'], 'L1_ffn_ln_beta': _L1_ffn_in['ln_beta'], 'L1_ffn_fc1s': _L1_ffn_in['fc1s'], 'L1_ffn_b1s': _L1_ffn_in['b1s'], 'L1_ffn_fc2s': _L1_ffn_in['fc2s'], 'L1_ffn_b2s': _L1_ffn_in['b2s']}
    _x0 = _d['L0_attn_x']
    _d['L0_attn_x'] = jax.random.normal(jax.random.fold_in(jax.random.key(seed), 1), (16, 256, 128), dtype=_x0.dtype)
    del _x0
    return _d

def reference(L0_attn_x, L0_attn_Wqkv, L0_attn_Wo, L0_attn_bo, L0_ffn_router_weight, L0_ffn_gate_up_proj, L0_ffn_gate_up_proj_bias, L0_ffn_down_proj, L0_ffn_down_proj_bias, L1_attn_Wq, L1_attn_Wk, L1_attn_Wv, L1_attn_Wo, L1_ffn_gate_w, L1_ffn_ln_gamma, L1_ffn_ln_beta, L1_ffn_fc1s, L1_ffn_b1s, L1_ffn_fc2s, L1_ffn_b2s):

    def _L0_attn_ref(x, Wqkv, Wo, bo):
        import jax, jax.numpy as jnp
        import numpy as np
        N_HEAD = 16

        def _rope_cache(T, head_dim):
            half = head_dim // 2
            inv_freq = 1.0 / 10000.0 ** (jnp.arange(half, dtype=jnp.float32) / half)
            t = jnp.arange(T, dtype=jnp.float32)
            freqs = jnp.einsum('i,j->ij', t, inv_freq)
            cos = jnp.repeat(jnp.cos(freqs), 2, axis=-1)
            sin = jnp.repeat(jnp.sin(freqs), 2, axis=-1)
            return (cos, sin)

        def _apply_rope(x, cos, sin):
            x1 = x[..., ::2]
            x2 = x[..., 1::2]
            x_rot = jnp.stack([-x2, x1], axis=-1).reshape(x.shape)
            return x * cos[None, None] + x_rot * sin[None, None]
        B, T, C = x.shape
        H = N_HEAD
        D = C // H
        scale = D ** (-0.5)
        qkv = x @ Wqkv
        qkv = qkv.reshape(B, T, 3, H, D).transpose(2, 0, 3, 1, 4)
        q, k, v = (qkv[0], qkv[1], qkv[2])
        cos, sin = _rope_cache(T, D)
        q = _apply_rope(q, cos, sin)
        k = _apply_rope(k, cos, sin)
        att = jnp.einsum('bhqd,bhkd->bhqk', q, k) * scale
        causal = jnp.tril(jnp.ones((T, T), dtype=bool))
        att = jnp.where(causal[None, None], att, -jnp.inf)
        att = jax.nn.softmax(att, axis=-1)
        out = jnp.einsum('bhqk,bhkd->bhqd', att, v)
        out = out.transpose(0, 2, 1, 3).reshape(B, T, C)
        return out @ Wo + bo

    def _L0_ffn_ref(hidden_states, router_weight, gate_up_proj, gate_up_proj_bias, down_proj, down_proj_bias):
        import jax, jax.numpy as jnp
        import numpy as np
        B, S, H, E, I, K = (2, 256, 128, 8, 128, 2)
        ALPHA, LIMIT = (1.702, 7.0)
        Bt, St, Ht = hidden_states.shape
        x = hidden_states.reshape(-1, Ht)
        T = x.shape[0]
        logits = x @ router_weight
        top_vals, top_idx = jax.lax.top_k(logits, K)
        scores = jax.nn.softmax(top_vals, axis=-1)
        w = jnp.zeros((T, E), x.dtype).at[jnp.arange(T)[:, None], top_idx].set(scores)
        gu = jnp.einsum('th,ehf->tef', x, gate_up_proj) + gate_up_proj_bias
        gate = gu[..., ::2]
        up = gu[..., 1::2]
        gate = jnp.minimum(gate, LIMIT)
        up = jnp.clip(up, -LIMIT, LIMIT)
        glu = gate * jax.nn.sigmoid(gate * ALPHA)
        act = (up + 1.0) * glu
        down = jnp.einsum('tei,eih->teh', act, down_proj) + down_proj_bias
        out = jnp.einsum('te,teh->th', w, down)
        return out.reshape(Bt, St, Ht)

    def _L1_attn_ref(hidden_states, Wq, Wk, Wv, Wo):
        import jax, jax.numpy as jnp
        import numpy as np
        import math
        FEATURE_DIM = 16
        NUM_HEADS = 16
        HIDDEN = 128
        HEAD_DIM = HIDDEN // NUM_HEADS
        EPS = 1e-12
        IU, JU = np.triu_indices(FEATURE_DIM, 1)
        RD = math.sqrt(FEATURE_DIM)
        RRD = math.sqrt(RD)
        R2 = math.sqrt(2.0)

        def taylor_feature_map(x):
            x2 = x[..., :, None] * x[..., None, :]
            off = x2[..., IU, JU]
            diag = jnp.square(x)
            ones = jnp.ones_like(x[..., :1])
            return jnp.concatenate([ones, x / RRD, diag / (RD * R2), off / RD], axis=-1)
        b, t, _ = hidden_states.shape
        q = (hidden_states @ Wq.T).reshape(b, t, NUM_HEADS, FEATURE_DIM).transpose(0, 2, 1, 3)
        k = (hidden_states @ Wk.T).reshape(b, t, NUM_HEADS, FEATURE_DIM).transpose(0, 2, 1, 3)
        v = (hidden_states @ Wv.T).reshape(b, t, NUM_HEADS, HEAD_DIM).transpose(0, 2, 1, 3)
        q = taylor_feature_map(q)
        k = taylor_feature_map(k)
        kv = jnp.cumsum(k[..., None, :] * v[..., :, None], axis=2)
        y = jnp.einsum('bhtD,bhtdD->bhtd', q, kv)
        z = jnp.cumsum(k, axis=2)
        denom = jnp.sum(q * z, axis=-1, keepdims=True) + EPS
        y = y / denom
        y = y.transpose(0, 2, 1, 3).reshape(b, t, NUM_HEADS * HEAD_DIM)
        return y @ Wo.T

    def _L1_ffn_ref(x, gate_w, ln_gamma, ln_beta, fc1s, b1s, fc2s, b2s):
        import jax, jax.numpy as jnp
        import numpy as np
        EMBED_DIM = 128
        MLP_RATIO = 4
        NUM_EXPERTS = 8
        CAPACITY = 1.0
        LN_EPS = 1e-05

        def _layernorm(y, gamma, beta):
            mu = jnp.mean(y, axis=-1, keepdims=True)
            var = jnp.mean(jnp.square(y - mu), axis=-1, keepdims=True)
            return (y - mu) * jax.lax.rsqrt(var + LN_EPS) * gamma + beta
        og_shape = x.shape
        d = og_shape[-1]
        xf = x.reshape(-1, d)
        bs = xf.shape[0]
        n = gate_w.shape[0]
        k = int(bs * CAPACITY) // n
        scores = xf @ gate_w.T
        scores = (jnp.tanh(scores) + 1.0) * 0.5
        vals, idx = jax.lax.top_k(scores.T, k)
        kept_w = vals.T
        flat_idx = idx.T.reshape(-1)
        y = xf[flat_idx].reshape(k, n, d)
        y = _layernorm(y, ln_gamma, ln_beta)
        h = jnp.einsum('knd,nfd->knf', y, fc1s) + b1s
        h = jax.nn.gelu(h, approximate=True)
        o = jnp.einsum('knf,ndf->knd', h, fc2s) + b2s
        o = o * kept_w[:, :, None]
        out = xf.at[flat_idx].add(o.reshape(k * n, d))
        return out.reshape(og_shape)
    x = L0_attn_x
    x = _layernorm(x + _L0_attn_ref(x, L0_attn_Wqkv, L0_attn_Wo, L0_attn_bo), axis=-1)
    x = _layernorm(x + _L0_ffn_ref(x, L0_ffn_router_weight, L0_ffn_gate_up_proj, L0_ffn_gate_up_proj_bias, L0_ffn_down_proj, L0_ffn_down_proj_bias), axis=-1)
    x = _layernorm(x + _L1_attn_ref(x, L1_attn_Wq, L1_attn_Wk, L1_attn_Wv, L1_attn_Wo), axis=-1)
    x = _layernorm(x + _L1_ffn_ref(x, L1_ffn_gate_w, L1_ffn_ln_gamma, L1_ffn_ln_beta, L1_ffn_fc1s, L1_ffn_b1s, L1_ffn_fc2s, L1_ffn_b2s), axis=-1)
    return x

_drawn_inputs = setup_inputs


def setup_inputs(seed=0):
    import zlib

    import numpy as np

    out = dict(_drawn_inputs(seed))
    spreads = {'L0_attn_bo': (0.0, 0.1),
     'L0_ffn_gate_up_proj_bias': (0.0, 0.365),
     'L0_ffn_down_proj_bias': (0.0, 0.1),
     'L1_ffn_ln_gamma': (1.0, 0.2),
     'L1_ffn_ln_beta': (0.0, 0.381)}
    factors = {'L1_ffn_b1s': 8.0, 'L1_ffn_b2s': 8.0}
    for name, (base, spread) in spreads.items():
        noise = np.random.default_rng([zlib.crc32(name.encode()), seed]).standard_normal(out[name].shape)
        drawn = base * np.exp(spread * noise) if base else spread * noise
        out[name] = jnp.asarray(drawn.astype(out[name].dtype))
    for name, factor in factors.items():
        out[name] = (out[name] * factor).astype(out[name].dtype)
    return out
```

```python
from contextlib import ExitStack

import concourse.bass as bass
from concourse import mybir

F32 = mybir.dt.float32
BF16 = mybir.dt.bfloat16
ALU = mybir.AluOpType
ACT = mybir.ActivationFunctionType
I32 = mybir.dt.int32
AX_X = mybir.AxisListType.X

P = 128
NB, T, C = 16, 256, 128
NTOK = NB * T
NTILE = NTOK // P
H, HD = 16, 8
HV = HD + 1
VW = 32
CH = 512
NCH = NTOK // CH
FD = 16
E = 8
ALPHA, LIMIT = 1.702, 7.0
CAP = NTOK // E
BITS = 26
DEN_EPS = 1e-12
NSLOT = 6
SLOT_RUNS = ((0, 3, 0), (3, 2, 1), (5, 1, 2))
UH = 8
NU = NB * H // UH
EPS = 1e-5
BIG = 1e30


def after(eng, sem, n):
    if isinstance(n, int) and n <= 0:
        return
    eng.wait_ge(sem, n)


class Semaphores:

    def __init__(self, nc):
        self.nc, self.taken = nc, []

    def __enter__(self):
        return self

    def take(self, name):
        self.taken.append(self.nc.alloc_semaphore(name))
        return self.taken[-1]

    def __exit__(self, *exc):
        if exc[0] is None:
            self.nc.clear_and_free_semaphores(self.taken)
            self.nc.all_engine_barrier()


def settled(eng, sem, n, gate):
    after(eng, sem, n)
    if not isinstance(n, int):
        eng.sem_inc(gate, 1)


def layer0_attention(nc, io, xn, stats, consts):
    scratch = [nc.dram_tensor(f"scratch0_{n}", [NCH, NSLOT, P, CH], BF16, kind="Internal").ap() for n in "qk"]
    with ExitStack() as keep:
        v_all = keep.enter_context(nc.sbuf_tensor("v_all0", [P, NTILE, H, HV], F32))
        wo = keep.enter_context(nc.sbuf_tensor("wo0", [P, P], F32))
        bo = keep.enter_context(nc.sbuf_tensor("bo0", [P, 1, C], F32))
        project_layer0(nc, io, scratch, v_all, wo, bo, xn, consts)
        attend(nc, "a0", scratch, 6 * HD, v_all, xn, stats, consts, wo, bo, softmax=True)


def project_layer0(nc, io, scratch, v_all, wo, bo, xn, consts):
    with ExitStack() as ctx:
        def sb(name, shape, dt=F32):
            return ctx.enter_context(nc.sbuf_tensor(name, shape, dt))

        def ps(name, shape, dt=F32):
            return ctx.enter_context(nc.psum_tensor(name, shape, dt))

        phase = ctx.enter_context(Semaphores(nc))

        def sem(name):
            return phase.take(name)

        ident, ident_bf, ones_row = consts["ident"], consts["ident_bf"], consts["ones_row"]
        tri4, upper, ones_sq = consts["tri4"], consts["upper"], consts["ones_sq"]
        xc = sb("xc", [P, 2, CH])
        wqk = sb("wqk", [P, 4, P])
        wv = sb("wv", [P, P])
        rot = sb("rot", [P, 2, 1, T])
        tri_f = sb("tri_f", [P, P])
        term = sb("term", [P, 2, 2, CH])
        roped = sb("roped", [P, 2, CH])
        resid = sb("resid", [P, 2, CH])
        parts = sb("parts", [P, 4, 3, CH], BF16)

        ps_b = [ps(f"ps_b{i}", [P, 1024]) for i in range(2)]
        ps_a = [ps(f"ps_a{i}", [P, 512]) for i in range(2)]
        ps_qk = [[ps_b[j][:, 512 * i:512 * i + 512] for i in range(2)] for j in range(2)]
        ps_v = ps_a[0]

        s_w = sem("weights_loaded")
        s_xn = sem("xn_loaded")
        s_xc = [sem(f"xc_loaded{i}") for i in range(2)]
        s_zero = sem("stacks_cleared")
        s_tri = sem("tri_ready")
        s_proj = sem("qk_projected")
        s_rot = sem("qk_psum_read")
        s_rope = sem("qk_roped")
        s_hi = sem("hi_done")
        s_r1 = sem("residual_done")
        s_mid = sem("mid_done")
        s_lo = sem("lo_done")
        s_store = [sem(f"parts_stored{i}") for i in range(4)]
        s_vp = sem("v_projected")
        s_vc = sem("v_copied")

        with nc.Block() as block:
            @block.sync
            def _(sp):
                for dst, src in ((wqk[:, :, :], io["wqk"]), (rot[:, :, 0, :], io["rot"]), (wv[:, :], io["wv"])):
                    sp.dma_start(dst, src).then_inc(s_w, 16)

                def load(c, u):
                    sp.dma_start(xc[:, u, :], io["xT"][:, bass.ds(c * CH, CH)]).then_inc(s_xc[u], 16)

                def store(c, u):
                    for j in range(2):
                        n = 2 * c + j
                        sp.wait_ge(s_lo, n + 1)
                        src = parts[:, 2 * u + j, :, :]
                        dst = scratch[j][bass.ds(c, 1), :, :, :].rearrange("c s p t -> p (c s) t")
                        for s0, m, part in SLOT_RUNS:
                            if j == 0:
                                sp.dma_start(dst[:, s0:s0 + m, :], src[:, 0:m, :]).then_inc(s_store[2 * u + j], 16)
                            else:
                                sp.dma_start(dst[:, s0:s0 + m, :],
                                             src[:, part:part + 1, :].to_broadcast([P, m, CH])).then_inc(s_store[2 * u + j], 16)

                for u in range(2):
                    load(u, u)
                for dst, src in ((wo[:, :], io["wo"]), (bo[:, 0, :], io["bo"]), (tri_f[:, :], io["tri"]), (upper[:, :], io["upper"])):
                    sp.dma_start(dst, src).then_inc(s_w, 16)
                sp.dma_start(xn[:, :, :], io["x"].rearrange("(t p) c -> p t c", p=P)).then_inc(s_xn, 16)
                with sp.Fori(0, NCH // 2 - 1) as k:
                    for u in range(2):
                        store(2 * k + u, u)
                        sp.wait_ge(s_vp, 2 * k + u + 1)
                        load(2 * k + u + 2, u)
                for u in range(2):
                    store(NCH - 2 + u, u)
                for n in range(4):
                    sp.wait_ge(s_store[n], 48 * (NCH // 2))
                sp.wait_ge(s_xn, 16)

            @block.tensor
            def _(pe):
                pe.wait_ge(s_w, 48)

                def chunk(k, u):
                    c = 2 * k + u
                    pe.wait_ge(s_xc[u], 16 * k + 16)
                    for j in range(2):
                        after(pe, s_rot, 2 * c + j - 1)
                        for i in range(2):
                            last = nc.tensor.matmul(ps_qk[j][i], wqk[:, 2 * j + i, :], xc[:, u, :], start=True, stop=True)
                        last.then_inc(s_proj, 1)
                    after(pe, s_vc, c)
                    for t in range(4):
                        last = nc.tensor.matmul(ps_v[:, t * P:(t + 1) * P], xc[:, u, t * P:(t + 1) * P], wv[:, :],
                                                start=True, stop=True)
                    last.then_inc(s_vp, 1)

                for u in range(2):
                    chunk(0, u)
                with pe.Fori(1, NCH // 2) as k:
                    for u in range(2):
                        chunk(k, u)

            @block.vector
            def _(ve):
                nc.vector.memset(v_all[:, :, :, HD:HV], 1.0).then_inc(s_zero, 1)
                nc.vector.memset(ones_row[:, :], 1.0).then_inc(s_zero, 1)
                nc.vector.memset(ones_sq[:, :], 1.0).then_inc(s_zero, 1)
                ve.wait_ge(s_w, 112)
                for i in range(4):
                    nc.vector.tensor_copy(tri4[:, i, :], tri_f[:, :]).then_inc(s_tri, 1)
                nc.vector.tensor_copy(ident_bf[:, :], ident[:, :]).then_inc(s_tri, 1)

                def item(c, j):
                    n = 2 * c + j
                    ve.wait_ge(s_proj, n + 1)
                    for i in range(2):
                        last = nc.vector.tensor_tensor(
                            term[:, j, i, :].rearrange("p (b t) -> p b t", b=2),
                            ps_qk[j][i].rearrange("p (b t) -> p b t", b=2),
                            rot[:, i, :, :].to_broadcast([P, 2, T]), ALU.mult)
                    last.then_inc(s_rot, 1)
                    ve.wait_ge(s_rot, n + 1)
                    after(ve, s_r1, n - 1)
                    nc.vector.tensor_tensor(roped[:, j, :], term[:, j, 0, :], term[:, j, 1, :], ALU.add).then_inc(s_rope, 1)

                for j in range(2):
                    item(0, j)
                with ve.Fori(1, NCH) as c:
                    for j in range(2):
                        item(c, j)

            @block.scalar
            def _(act):
                act.wait_ge(s_zero, 1)

                def chunk(k, u):
                    c = 2 * k + u
                    for j in range(2):
                        n = 2 * c + j
                        act.wait_ge(s_rope, n + 1)
                        after(act, s_store[2 * u + j], 48 * k)
                        nc.scalar.activation(parts[:, 2 * u + j, 0, :], roped[:, j, :], ACT.Copy).then_inc(s_hi, 1)
                        act.wait_ge(s_r1, n + 1)
                        nc.scalar.activation(parts[:, 2 * u + j, 1, :], resid[:, j, :], ACT.Copy).then_inc(s_mid, 1)
                    act.wait_ge(s_vp, c + 1)
                    nc.scalar.activation(v_all[:, bass.ds(4 * c, 4), :, 0:HD],
                                         ps_v[:, :].rearrange("p (t h d) -> p t h d", t=4, h=H), ACT.Copy).then_inc(s_vc, 1)

                for u in range(2):
                    chunk(0, u)
                with act.Fori(1, NCH // 2) as k:
                    for u in range(2):
                        chunk(k, u)

            @block.gpsimd
            def _(pool):
                def item(k, u, j):
                    n = 4 * k + 2 * u + j
                    pool.wait_ge(s_hi, n + 1)
                    after(pool, s_mid, n - 1)
                    nc.gpsimd.tensor_tensor(resid[:, j, :], roped[:, j, :], parts[:, 2 * u + j, 0, :], ALU.subtract).then_inc(s_r1, 1)
                    pool.wait_ge(s_mid, n + 1)
                    nc.gpsimd.tensor_tensor(parts[:, 2 * u + j, 2, :], resid[:, j, :], parts[:, 2 * u + j, 1, :],
                                            ALU.subtract).then_inc(s_lo, 1)

                for u in range(2):
                    for j in range(2):
                        item(0, u, j)
                with pool.Fori(1, NCH // 2) as k:
                    for u in range(2):
                        for j in range(2):
                            item(k, u, j)


def attend(nc, tag, scratch, rows, v_all, xn, stats, consts, wo, bo, softmax):
    depth = 67 if softmax else rows
    scale = HD ** -0.5 if softmax else FD ** -0.5
    ident, ident_bf, ones_row = consts["ident"], consts["ident_bf"], consts["ones_row"]
    tri4, upper, ones_sq = consts["tri4"], consts["upper"], consts["ones_sq"]
    with ExitStack() as ctx:
        def sb(name, shape, dt=F32):
            return ctx.enter_context(nc.sbuf_tensor(f"{tag}_{name}", shape, dt))

        def ps(name, shape, dt=F32):
            return ctx.enter_context(nc.psum_tensor(f"{tag}_{name}", shape, dt))

        phase = ctx.enter_context(Semaphores(nc))

        def sem(name):
            return phase.take(f"{tag}_{name}")

        v_now = sb("v_now", [P, 2, 2, H, VW])
        qst = sb("qst", [P, 4, UH, T], BF16)
        kst = sb("kst", [P, 4, UH, T], BF16)
        prob = sb("prob", [P, 6, 1024])
        mx = sb("mx", [P, 2, UH, 2])
        mres = sb("mres", [P, 2, 16])
        mparts = sb("mparts", [P, 2, 3, 16], BF16)
        mT = sb("mT", [48, 2, P], BF16)
        outT = sb("outT", [P, 2, 2, T])
        vsum = sb("vsum", [P, 2, 2, H, HV])
        total = sb("total", [P, 2, 2, 4, HV])
        rden = sb("rden", [P, 2, 2, 4, 1])
        att = sb("att", [P, 2, H, HD])
        attT = sb("attT", [P, 2, P])
        bns = sb("bns", [P, NTILE, 6])
        den = sb("den", [P, 2, 2, 4, 1])
        ps_b = [ps(f"ps_b{i}", [P, 1024]) for i in range(2)]
        ps_a = [ps(f"ps_a{i}", [P, 512]) for i in range(2)]
        ps_pv = ps("ps_pv", [P, 512])
        ps_m = ps("ps_m", [P, 512])

        s_st = [sem(f"stack_loaded{i}") for i in range(4)]
        s_mrow = [sem(f"max_rows_loaded{i}") for i in range(2)]
        s_gate_pe, s_gate_pool = sem("gate_pe"), sem("gate_pool")
        s_af = sem("max_scores_ready")
        s_mx = sem("max_taken")
        s_mh = sem("max_hi_done")
        s_mr = sem("max_residual_done")
        s_mm = sem("max_mid_done")
        s_mp = sem("max_parts_done")
        s_mT = sem("max_transposed")
        s_mTc = sem("max_rows_copied")
        s_b = sem("scores_ready")
        s_e = sem("exp_done")
        s_k = sem("causal_masked")
        s_pv = sem("weighted_v_done")
        s_vn = sem("v_now_ready")
        s_vz = sem("v_now_cleared")
        s_ev = sem("out_rows_copied")
        s_tp = sem("out_transposed")
        s_vs = sem("v_summed")
        s_vsc = sem("v_sums_copied")
        s_tot = sem("v_sums_added")
        s_bias = sem("bias_added")
        s_rd = sem("denominator_inverted")
        s_on = sem("out_normalised")
        s_aT = sem("attention_transposed")
        s_aTc = sem("attention_rows_copied")
        s_o = sem("output_projected")
        s_y = sem("residual_added")
        s_bn = sem("row_stats_taken")
        s_ag = sem("row_stats_merged")
        s_clear = sem("stacks_cleared")
        s_zero = sem("stack_rows_set")
        s_de = sem("denominator_guarded")

        with nc.Block() as block:
            @block.sync
            def _(sp):
                sp.wait_ge(s_clear, 1)

                def load(c, s):
                    h0, t0 = UH * (s % 2), T * (s // 2)
                    for st, sc in ((qst, scratch[0]), (kst, scratch[1])):
                        src = sc[bass.ds(c, 1), :, :, :].rearrange("c s (d h) t -> (c s d) h t", h=H)[:, h0:h0 + UH, t0:t0 + T]
                        sp.dma_start(st[0:rows, s, :, :], src).then_inc(s_st[s], 16)

                def max_rows(k, s):
                    sp.wait_ge(s_mTc, 4 * k + s + 1)
                    for p in range(3):
                        dst = qst[64 + p:65 + p, s % 4, :, :].rearrange("p h (x q) -> p (h x) q", q=P)
                        sp.dma_start(dst, mT[16 * p:16 * p + 16, s % 2, :]).then_inc(s_mrow[s % 2], 16)

                for s in range(4):
                    load(0, s)
                if softmax:
                    max_rows(0, 0)

                def slot(k, s, next_max=softmax, more=True):
                    if next_max:
                        max_rows(k, s + 1)
                    if more:
                        sp.wait_ge(s_b, 12 * k + 3 * s + 3)
                        load(k + 1, s)

                with sp.Fori(0, NU // 4 - 1) as k:
                    for s in range(4):
                        slot(k, s)
                for s in range(4):
                    slot(NU // 4 - 1, s, next_max=softmax and s < 3, more=False)

            @block.tensor
            def _(pe):
                pe.wait_ge(s_clear, 1)

                def fill(k, s, f):
                    g = 24 * k + 6 * s + f
                    after(pe, s_mx, g - 1)
                    if f >= 4:
                        after(pe, s_on, 2 * (4 * k + s - 3) + f - 3)
                    s = s % 4
                    out = ps_a[f % 2]
                    if f < 4:
                        for i in range(2):
                            nc.tensor.matmul(out[:, 256 * i:256 * i + 256], qst[0:48, s, 2 * f + i, P:2 * P],
                                             kst[0:48, s, 2 * f + i, :], start=i == 0, stop=False, skip_group_check=True)
                        o = out[:, :].rearrange("p (h k) -> p h k", h=2)[:, :, P:2 * P]
                        nc.tensor.matmul(o, ident_bf[:, :], tri4[:, 0:2, :], start=False, stop=True,
                                         skip_group_check=True).then_inc(s_af, 1)
                    else:
                        for i in range(4):
                            h = 4 * (f - 4) + i
                            nc.tensor.matmul(out[:, P * i:P * i + P], qst[0:48, s, h, 0:P], kst[0:48, s, h, 0:P],
                                             start=i == 0, stop=False, skip_group_check=True)
                        nc.tensor.matmul(out[:, :], ident_bf[:, :], tri4[:, :, :], start=False, stop=True,
                                         skip_group_check=True).then_inc(s_af, 1)

                def stack_ready(k, s):
                    pe.wait_ge(s_st[s % 4], 32 * (k + s // 4) + 32)

                def scores(k, s, j):
                    r = 12 * k + 3 * s + j
                    after(pe, s_e, r - 1)
                    out = ps_b[(3 * s + j) % 2]
                    if j < 2:
                        for i in range(4):
                            last = nc.tensor.matmul(out[:, 256 * i:256 * i + 256], kst[0:depth, s, 4 * j + i, 0:P],
                                                    qst[0:depth, s, 4 * j + i, :], start=True, stop=True)
                    else:
                        for i in range(8):
                            last = nc.tensor.matmul(out[:, P * i:P * i + P], kst[0:depth, s, i, P:2 * P],
                                                    qst[0:depth, s, i, P:2 * P], start=True, stop=True)
                    last.then_inc(s_b, 1)

                def weighted(k, s, j):
                    r = 12 * k + 3 * s + j
                    u = 4 * k + s
                    pe.wait_ge(s_k, r + 1)
                    if j == 0:
                        after(pe, s_ev, u)
                        if s % 2 == 0:
                            pe.wait_ge(s_vn, 2 * k + s // 2 + 1)
                    h0, par = UH * (s % 2), s // 2
                    reg = prob[:, (3 * s + j) % 6, :]
                    for i in range(4 if j < 2 else UH):
                        part = slice(VW * (i % 4), VW * (i % 4) + VW)
                        if j < 2:
                            last = nc.tensor.matmul(ps_pv[part, T * j:T * j + T], v_now[:, par, 0, h0 + 4 * j + i, :],
                                                    reg[:, T * i:T * i + T], start=j == 0, stop=False, skip_group_check=True)
                        else:
                            q0 = T * (i // 4) + P
                            last = nc.tensor.matmul(ps_pv[part, q0:q0 + P], v_now[:, par, 1, h0 + i, :],
                                                    reg[:, P * i:P * i + P], start=False, stop=True, skip_group_check=True)
                    last.then_inc(s_pv, 1)

                def turn_out(k, s, fills):
                    w = 4 * k + s
                    after(pe, s_ev, w + 1)
                    for i in range(2):
                        if softmax:
                            pe.wait_ge(s_mx, 6 * (w + 3) + 3 + i if fills else 6 * NU)
                        after(pe, s_on, 2 * w + i - 1)
                        for q in range(2):
                            last = nc.tensor.transpose(ps_a[i][:, q * P:q * P + P], outT[:, s % 2, i, q * P:q * P + P], ident[:, :])
                        last.then_inc(s_tp, 1)

                def sum_v(b, par):
                    pe.wait_ge(s_vn, b + 1)
                    after(pe, s_y, b - 1)
                    vt = [v_now[:, par, t, :, 0:HV] for t in range(2)]
                    out = [ps_m[:, H * HV * t:H * HV * (t + 1)].rearrange("p (h d) -> p h d", h=H) for t in range(2)]
                    nc.tensor.matmul(out[0], upper[:, :], vt[0], start=True, stop=False, skip_group_check=True)
                    nc.tensor.matmul(out[1], ones_sq[:, :], vt[0], start=False, stop=False, skip_group_check=True)
                    nc.tensor.matmul(out[1], upper[:, :], vt[1], start=False, stop=True, skip_group_check=True).then_inc(s_vs, 1)

                def transpose_max(n, s):
                    settled(pe, s_mp, n + 1, s_gate_pe)
                    nc.tensor.transpose(ps_m[0:48, 0:64].bitcast(BF16), mparts[:, s % 2, :, :].rearrange("p a b -> p (a b)"),
                                        ident_bf[:, :]).then_inc(s_mT, 1)

                def transpose_att(b):
                    pe.wait_ge(s_on, 4 * b + 4)
                    for q in range(2):
                        last = nc.tensor.transpose(ps_m[:, q * P:q * P + P], att[:, q, :, :].rearrange("p h d -> p (h d)"),
                                                   ident[:, :])
                    last.then_inc(s_aT, 1)

                def project(b):
                    pe.wait_ge(s_aTc, b + 1)
                    for q in range(2):
                        o = ps_m[:, q * P:q * P + P]
                        last = nc.tensor.matmul(o, attT[:, q, :], wo[:, :], start=q == 0, stop=True, skip_group_check=True)
                    last.then_inc(s_o, 1)

                def slot(k, s, fills=softmax, tr=softmax, prev=True):
                    u = 4 * k + s
                    b = 2 * k + s // 2
                    if softmax:
                        pe.wait_ge(s_mrow[s % 2], 48 * (2 * k + s // 2) + 48)
                    else:
                        stack_ready(k, s)
                    prev1 = prev or s > 0
                    w = (k - 1, 3) if s == 0 else (k, s - 1)
                    for j in range(3):
                        scores(k, s, j)
                        if j > 0 and fills:
                            fill(k, s + 2, 2 * j)
                            fill(k, s + 2, 2 * j + 1)
                        if j > 0:
                            weighted(k, s, j - 1)
                        elif prev1:
                            weighted(*w, 2)
                        if j == 0 and fills:
                            stack_ready(k, s + 2)
                            fill(k, s + 2, 0)
                            fill(k, s + 2, 1)
                        if j == 0 and tr:
                            if s % 2 == 0:
                                after(pe, s_y, b - 1)
                            else:
                                after(pe, s_aTc, b)
                            transpose_max(u + 1, s + 1)
                        if j == 0 and not softmax and s % 2 == 0:
                            sum_v(b, s // 2)
                        if j == 1 and prev1:
                            turn_out(*w, fills)
                        if j == 1 and s % 2 == 1 and (prev or s > 1):
                            if softmax:
                                pe.wait_ge(s_mTc, u + (2 if tr else 1))
                            project(b - 1)
                        if j == 2 and s % 2 == 0 and (prev or s > 1):
                            if softmax:
                                pe.wait_ge(s_mTc, u + (2 if tr else 1))
                            else:
                                pe.wait_ge(s_vsc, b + 1)
                            transpose_att(b - 1)

                if softmax:
                    for s in range(2):
                        stack_ready(0, s)
                        for f in range(6):
                            fill(0, s, f)
                    transpose_max(0, 0)
                    pe.wait_ge(s_mTc, 1)
                for s in range(4):
                    slot(0, s, prev=False)
                with pe.Fori(1, NU // 4 - 1) as k:
                    for s in range(4):
                        slot(k, s)
                for s in range(4):
                    slot(NU // 4 - 1, s, fills=softmax and s < 2, tr=softmax and s < 3)
                weighted(NU // 4 - 1, 3, 2)
                turn_out(NU // 4 - 1, 3, False)
                pe.wait_ge(s_y, NB - 1)
                transpose_att(NB - 1)
                project(NB - 1)

            @block.vector
            def _(ve):
                if softmax:
                    nc.vector.memset(qst[32:64, :, :, :], 0.0).then_inc(s_zero, 1)
                    nc.vector.memset(kst[32:64, :, :, :], 0.0).then_inc(s_zero, 1)
                    nc.vector.memset(kst[64:96, :, :, :], -1.0).then_inc(s_zero, 1)
                    ve.wait_ge(s_zero, 3)
                nc.vector.memset(v_now[:, :, :, :, :], 0.0).then_inc(s_vz, 1)
                nc.vector.memset(den[:, :, :, :, :], 0.0).then_inc(s_clear, 1)
                if bo is not None:
                    nc.vector.tensor_tensor(xn[:, :, :], xn[:, :, :], bo[:, :, :].to_broadcast([P, NTILE, C]),
                                            ALU.add).then_inc(s_bias, 1)
                    ve.wait_ge(s_bias, 1)

                def reduce(k, s, f):
                    g = 24 * k + 6 * s + f
                    if f == 0:
                        after(ve, s_mp, 4 * k + s - 1)
                    ve.wait_ge(s_af, g + 1)
                    if f < 4:
                        nc.vector.reduce_max(mx[:, s % 2, 2 * f:2 * f + 2, 1:2],
                                             ps_a[f % 2][:, :].rearrange("p (h k) -> p h k", h=2), AX_X).then_inc(s_mx, 1)
                    else:
                        h = 4 * (f - 4)
                        nc.vector.reduce_max(mx[:, s % 2, h:h + 4, 0:1],
                                             ps_a[f % 2][:, :].rearrange("p (h k) -> p h k", h=4), AX_X).then_inc(s_mx, 1)

                def normalise(k, s):
                    w = 4 * k + s
                    for i in range(2):
                        src = ps_a[i][:, 0:2 * P].rearrange("p (q h d) -> p q h d", q=2, h=4)
                        h = UH * (s % 2) + 4 * i
                        ve.wait_ge(s_tp, 2 * w + i + 1)
                        if softmax:
                            out, d = src[:, :, :, 0:HD], src[:, :, :, HD:HV]
                        else:
                            tot = total[:, i, :, :, :]
                            out, d = tot[:, :, :, 0:HD], den[:, i, :, :, :]
                            if i == 0 and s % 2 == 0:
                                ve.wait_ge(s_vsc, 2 * k + s // 2 + 1)
                            for q in range(2):
                                last = nc.vector.tensor_tensor(tot[:, q, :, :], src[:, q, :, 0:HV], vsum[:, s // 2, q, h:h + 4, :], ALU.add)
                            last.then_inc(s_tot, 1)
                            ve.wait_ge(s_tot, 2 * w + i + 1)
                            nc.vector.tensor_scalar(d, tot[:, :, :, HD:HV], 2.0 * DEN_EPS, None, ALU.add).then_inc(s_de, 1)
                            ve.wait_ge(s_de, 2 * w + i + 1)
                        nc.vector.reciprocal(rden[:, i, :, :, :], d).then_inc(s_rd, 1)
                        ve.wait_ge(s_rd, 2 * w + i + 1)
                        if i == 0 and s % 2 == 0:
                            after(ve, s_aT, 2 * k + s // 2)
                        for q in range(2):
                            last = nc.vector.tensor_tensor(att[:, q, h:h + 4, :], out[:, q, :, :],
                                                           rden[:, i, q, :, :].to_broadcast([P, 4, HD]), ALU.mult)
                        last.then_inc(s_on, 1)

                def add_residual(b):
                    ve.wait_ge(s_o, b + 1)
                    y = xn[:, bass.ds(2 * b, 2), :]
                    nc.vector.tensor_tensor(y, ps_m[:, 0:2 * P].rearrange("p (t c) -> p t c", t=2), y, ALU.add).then_inc(s_y, 1)
                    ve.wait_ge(s_clear, 1)
                    ve.wait_ge(s_y, b + 1)
                    for q in range(2):
                        nc.vector.bn_stats(bns[:, bass.ds(2 * b + q, 1), :], xn[:, bass.ds(2 * b + q, 1), :]).then_inc(s_bn, 1)

                def slot(k, s, fills=softmax, prev=True):
                    b = 2 * k + s // 2
                    for j in range(3):
                        if fills:
                            reduce(k, s + 2, 2 * j)
                            reduce(k, s + 2, 2 * j + 1)
                        if j == 1 and (prev or s > 0):
                            normalise(*((k - 1, 3) if s == 0 else (k, s - 1)))
                        if j == 1 and s % 2 == 1 and (prev or s > 1):
                            add_residual(b - 1)

                if softmax:
                    for s in range(2):
                        for f in range(6):
                            reduce(0, s, f)
                for s in range(4):
                    slot(0, s, prev=False)
                with ve.Fori(1, NU // 4 - 1) as k:
                    for s in range(4):
                        slot(k, s)
                for s in range(4):
                    slot(NU // 4 - 1, s, fills=softmax and s < 2)
                normalise(NU // 4 - 1, 3)
                add_residual(NB - 1)
                merge_stats(nc, ve, stats, bns, s_bn, s_ag)

            @block.scalar
            def _(act):
                def copy_max(n, s):
                    act.wait_ge(s_mT, n + 1)
                    nc.scalar.activation(mT[:, s % 2, :], ps_m[0:48, 0:64].bitcast(BF16), ACT.Copy).then_inc(s_mTc, 1)

                def copy_att(b):
                    act.wait_ge(s_aT, b + 1)
                    after(act, s_o, b)
                    nc.scalar.activation(attT[:, :, :], ps_m[:, 0:2 * P].rearrange("p (t c) -> p t c", t=2),
                                         ACT.Copy).then_inc(s_aTc, 1)

                def copy_out(w, s):
                    act.wait_ge(s_pv, 3 * w + 3)
                    after(act, s_tp, 2 * w - 2)
                    nc.scalar.activation(outT[:, s % 2, :, :], ps_pv[:, :].rearrange("p (i q) -> p i q", i=2),
                                         ACT.Copy).then_inc(s_ev, 1)

                def copy_vsum(b, par):
                    act.wait_ge(s_vs, b + 1)
                    after(act, s_on, 4 * b - 4)
                    nc.scalar.activation(vsum[:, par, :, :, :].rearrange("p t h d -> p (t h d)"), ps_m[:, 0:2 * H * HV],
                                         ACT.Copy).then_inc(s_vsc, 1)

                def slot(k, s, tr=softmax, prev=True):
                    b = 2 * k + s // 2
                    for j in range(3):
                        r = 12 * k + 3 * s + j
                        act.wait_ge(s_b, r + 1)
                        after(act, s_pv, r - 5)
                        nc.scalar.activation(prob[:, (3 * s + j) % 6, :], ps_b[(3 * s + j) % 2][:, :],
                                             ACT.Exp if softmax else ACT.Square, scale=scale,
                                             bias=0.0 if softmax else 1.0).then_inc(s_e, 1)
                        if j == 0 and (prev or s > 0):
                            copy_out(4 * k + s - 1, (s - 1) % 4)
                        if j == 0 and tr:
                            copy_max(4 * k + s + 1, s + 1)
                        if j == 0 and not softmax and s % 2 == 0:
                            copy_vsum(b, s // 2)
                        if j == 2 and s % 2 == 0 and (prev or s > 1):
                            copy_att(b - 1)

                if softmax:
                    copy_max(0, 0)
                for s in range(4):
                    slot(0, s, prev=False)
                with act.Fori(1, NU // 4 - 1) as k:
                    for s in range(4):
                        slot(k, s)
                for s in range(4):
                    slot(NU // 4 - 1, s, tr=softmax and s < 3)
                copy_out(NU - 1, 3)
                copy_att(NB - 1)

            @block.gpsimd
            def _(pool):
                def mask(k, s, j):
                    r = 12 * k + 3 * s + j
                    settled(pool, s_e, r + 1, s_gate_pool)
                    reg = prob[:, (3 * s + j) % 6, :]
                    if j < 2:
                        blk, n = reg.rearrange("p (h q) -> p h q", h=4)[:, :, 0:P], 4
                    else:
                        blk, n = reg.rearrange("p (h q) -> p h q", h=8), 8
                    nc.gpsimd.affine_select(out=blk, in_=blk, compare_op=ALU.is_ge, fill=0.0, base=0,
                                            pattern=[[0, n], [1, P]], channel_multiplier=-1).then_inc(s_k, 1)

                def split_max(n, s):
                    after(pool, s_mT, n - 1)
                    settled(pool, s_mx, 6 * n + 6, s_gate_pool)
                    m = mx[:, s % 2, :, :].rearrange("p h q -> p (h q)")
                    nc.gpsimd.tensor_copy(mparts[:, s % 2, 0, :], m).then_inc(s_mh, 1)
                    pool.wait_ge(s_mh, n + 1)
                    nc.gpsimd.tensor_tensor(mres[:, s % 2, :], m, mparts[:, s % 2, 0, :], ALU.subtract).then_inc(s_mr, 1)
                    settled(pool, s_mr, n + 1, s_gate_pool)
                    nc.gpsimd.tensor_copy(mparts[:, s % 2, 1, :], mres[:, s % 2, :]).then_inc(s_mm, 1)
                    pool.wait_ge(s_mm, n + 1)
                    nc.gpsimd.tensor_tensor(mparts[:, s % 2, 2, :], mres[:, s % 2, :], mparts[:, s % 2, 1, :],
                                            ALU.subtract).then_inc(s_mp, 1)

                def slot(k, s, fills=softmax):
                    b = 2 * k + s // 2
                    if s % 2 == 0:
                        settled(pool, s_pv, 6 * b - 6, s_gate_pool)
                        nc.gpsimd.tensor_copy(v_now[:, s // 2, :, :, 0:HV], v_all[:, bass.ds(2 * b, 2), :, :]).then_inc(s_vn, 1)
                    mask(k, s, 0)
                    mask(k, s, 1)
                    if fills:
                        split_max(4 * k + s + 2, s)
                    mask(k, s, 2)

                pool.wait_ge(s_vz, 1)
                if softmax:
                    for s in range(2):
                        split_max(s, s)
                for s in range(4):
                    slot(0, s)
                with pool.Fori(1, NU // 4 - 1) as k:
                    for s in range(4):
                        slot(k, s)
                for s in range(4):
                    slot(NU // 4 - 1, s, fills=softmax and s < 2)


def expert_layer0(nc, io, xn, stats, norm, consts):
    ident, ident_bf = consts["ident"], consts["ident_bf"]
    with ExitStack() as ctx:
        def sb(name, shape, dt=F32):
            return ctx.enter_context(nc.sbuf_tensor(f"m0_{name}", shape, dt))

        def ps(name, shape, dt=F32):
            return ctx.enter_context(nc.psum_tensor(f"m0_{name}", shape, dt))

        phase = ctx.enter_context(Semaphores(nc))

        def sem(name):
            return phase.take(f"m0_{name}")

        wr = sb("wr", [P, E])
        wgu = sb("wgu", [P, E, 2, P])
        bgu = sb("bgu", [P, E, 2])
        bup = sb("bup", [P, E])
        wd = sb("wd", [P, E, C])
        wdh = sb("wdh", [P, E, C])
        bd = sb("bd", [E, C])
        sel_f = sb("sel_f", [32, E, P])
        sel = sb("sel", [32, E, P], BF16)
        desc = sb("desc", [P, 1, E])
        x1 = sb("x1", [P, 2, 4, C])
        x1T = sb("x1T", [P, 2, CH])
        ra = [sb(f"route{i}", [P, 4, E]) for i in range(6)]
        rs = [sb(f"pick{i}", [P, 4, 1]) for i in range(8)]
        wt = sb("wt", [P, 2, 4, E])
        wtr = sb("wtr", [P, 4, E])
        wtp = sb("wtp", [P, 2, 4, 32], BF16)
        wT = sb("wT", [E, 2, CH])
        wTp = sb("wTp", [32, 2, CH], BF16)
        gate = sb("gate", [P, 2, CH])
        up = sb("up", [P, 2, CH])
        upc = sb("upc", [P, 2, CH])
        th = sb("th", [P, 2, CH])
        prod = sb("prod", [P, 2, CH])
        glu = sb("glu", [P, 2, CH])
        act = sb("act", [P, 2, CH])
        bns = sb("bns", [P, NTILE, 6])
        ps_g = [ps(f"ps_g{i}", [P, CH]) for i in range(2)]
        ps_u = [ps(f"ps_u{i}", [P, CH]) for i in range(2)]
        ps_w = ps("ps_w", [P, CH])
        ps_d = ps("ps_d", [P, CH])
        ps_x = ps("ps_x", [P, CH])
        ps_r = ps("ps_r", [P, CH])
        logits = ps_r[:, 0:4 * E].rearrange("p (t e) -> p t e", t=4)

        s_w = sem("weights_loaded")
        s_c = sem("constants_ready")
        s_x1 = sem("tile_normalised")
        s_xp = sem("x_transposed")
        s_xT = sem("x_rows_copied")
        s_lg = sem("logits_ready")
        s_rt = sem("routing_step")
        s_ra = sem("routing_exp_done")
        s_wtp = sem("weights_transposed")
        s_wT = sem("weight_rows_copied")
        s_wx = sem("weights_transposed_f32")
        s_g = sem("gate_ready")
        s_u = sem("up_ready")
        s_bc = sem("weight_broadcast")
        s_gc = sem("gate_clipped")
        s_uc = sem("up_copied")
        s_ucl = sem("up_clipped")
        s_th = sem("tanh_done")
        s_pr = sem("product_done")
        s_gl = sem("glu_done")
        s_act = sem("activation_weighted")
        s_dn = sem("expert_summed")
        s_y = sem("residual_added")
        s_bn = sem("row_stats_taken")
        s_ag = sem("row_stats_merged")
        s_gate = sem("gate_pe")
        NR = 22
        NEXP = NCH * E

        with nc.Block() as block:
            @block.sync
            def _(sp):
                for dst, src in ((wr[:, :], io["wr"]), (sel_f[:, :, :], io["sel"]), (desc[:, 0, :], io["desc"]),
                                 (bgu[:, :, :], io["bgu"]), (wgu[:, :, :, :], io["wgu"]), (wd[:, :, :], io["wd0"]),
                                 (bd[:, :], io["bd0"])):
                    sp.dma_start(dst, src).then_inc(s_w, 16)
                sp.wait_ge(s_w, 112)

            @block.tensor
            def _(pe):
                pe.wait_ge(s_c, 3)

                def transpose_x(c, u):
                    after(pe, s_xT, c)
                    pe.wait_ge(s_x1, 4 * c + 4)
                    for t in range(4):
                        last = nc.tensor.transpose(ps_x[:, t * P:(t + 1) * P], x1[:, u, t, :], ident[:, :])
                    last.then_inc(s_xp, 1)

                def route(c, u):
                    pe.wait_ge(s_xT, c + 1)
                    after(pe, s_wT, 2 * c)
                    for t in range(4):
                        last = nc.tensor.matmul(logits[:, t, :], x1T[:, u, t * P:(t + 1) * P], wr[:, :], start=True, stop=True)
                    last.then_inc(s_lg, 1)

                def transpose_w(c, u):
                    pe.wait_ge(s_rt, NR * c + NR)
                    for t in range(4):
                        last = nc.tensor.transpose(ps_r[0:32, 64 * t:64 * t + 64].bitcast(BF16), wtp[:, u, t, :], ident_bf[:, :])
                    last.then_inc(s_wtp, 1)
                    pe.wait_ge(s_wT, 2 * c + 1)
                    for t in range(4):
                        last = nc.tensor.transpose(ps_r[0:E, t * P:(t + 1) * P], wt[:, u, t, :], ident[:, :])
                    last.then_inc(s_wx, 1)

                def expand(c, u, e):
                    n = E * c + e
                    after(pe, s_gc, n - 1)
                    nc.tensor.matmul(ps_g[e % 2][:, :], wgu[:, e, 0, :], x1T[:, u, :], start=True, stop=True).then_inc(s_g, 1)
                    after(pe, s_uc, n - 1)
                    nc.tensor.matmul(ps_u[e % 2][:, :], wgu[:, e, 1, :], x1T[:, u, :], start=True, stop=True).then_inc(s_u, 1)

                def broadcast(c, u, e):
                    n = E * c + e
                    after(pe, s_act, n)
                    nc.tensor.matmul(ps_w[:, :], sel[0:32, e, :], wTp[0:32, u, :], start=True, stop=True).then_inc(s_bc, 1)

                def reduce(c, u, e):
                    n = E * c + e
                    if e == 0:
                        after(pe, s_y, c)
                        for t in range(4):
                            nc.tensor.matmul(ps_d[:, t * P:(t + 1) * P], wT[:, u, t * P:(t + 1) * P], bd[:, :],
                                             start=t == 0, stop=False, skip_group_check=True)
                    pe.wait_ge(s_act, n + 1)
                    for t in range(4):
                        last = nc.tensor.matmul(ps_d[:, t * P:(t + 1) * P], act[:, e % 2, t * P:(t + 1) * P], wdh[:, e, :],
                                                start=False, stop=e == E - 1, skip_group_check=True)
                    last.then_inc(s_dn, 1)

                def chunk(c, u, prev=True, nxt=True):
                    for e in range(E):
                        if e == 0:
                            pe.wait_ge(s_wT, 2 * c + 2)
                        expand(c, u, e)
                        if e >= 2:
                            reduce(c, u, e - 2)
                        elif prev:
                            reduce(c - 1, 1 - u, E + e - 2)
                        broadcast(c, u, e)
                        if nxt:
                            if e == 4:
                                transpose_x(c + 1, 1 - u)
                            if e == 5:
                                route(c + 1, 1 - u)
                            if e == 7:
                                transpose_w(c + 1, 1 - u)

                transpose_x(0, 0)
                route(0, 0)
                transpose_w(0, 0)
                chunk(0, 0, prev=False)
                chunk(1, 1)
                with pe.Fori(1, NCH // 2 - 1) as k:
                    for u in range(2):
                        chunk(2 * k + u, u)
                chunk(NCH - 2, 0)
                chunk(NCH - 1, 1, nxt=False)
                for e in (E - 2, E - 1):
                    reduce(NCH - 1, 1, e)

            @block.vector
            def _(ve):
                nc.vector.memset(wtp[:, :, :, :], 0.0).then_inc(s_c, 1)
                ve.wait_ge(s_w, 112)
                nc.vector.tensor_scalar(bup[:, :], bgu[:, :, 1], 1.0, None, ALU.add).then_inc(s_c, 1)
                nc.vector.tensor_copy(sel[:, :, :], sel_f[:, :, :]).then_inc(s_c, 1)
                nc.vector.tensor_scalar(wdh[:, :, :], wd[:, :, :], 0.5, None, ALU.mult).then_inc(s_c, 1)
                ve.wait_ge(s_c, 4)

                def normalise(c, u):
                    after(ve, s_y, c - 1)
                    for t in range(4):
                        nc.vector.tensor_scalar(x1[:, u, t, :], xn[:, bass.ds(4 * c + t, 1), :],
                                                stats[:, bass.ds(4 * c + t, 1), 0:1], norm.rstd[:, bass.ds(4 * c + t, 1)],
                                                ALU.subtract, ALU.mult).then_inc(s_x1, 1)

                def route(c, u):
                    done = [0]

                    def step(ins):
                        done[0] += 1
                        ins.then_inc(s_rt, 1)
                        ve.wait_ge(s_rt, NR * c + done[0])

                    def wide(x):
                        return x[:, :, :].to_broadcast([P, 4, E])

                    order = desc[:, :, :].to_broadcast([P, 4, E])
                    m1, k1, m2, k2, d, s, r, p2 = rs
                    ve.wait_ge(s_lg, c + 1)
                    after(ve, s_wx, c - 1)
                    step(nc.vector.reduce_max(m1[:, :, :], logits, AX_X))
                    step(nc.vector.tensor_tensor(ra[0][:, :, :], logits, wide(m1), ALU.is_ge))
                    step(nc.vector.tensor_tensor(ra[0][:, :, :], ra[0][:, :, :], order, ALU.mult))
                    step(nc.vector.reduce_max(k1[:, :, :], ra[0][:, :, :], AX_X))
                    step(nc.vector.tensor_tensor(ra[1][:, :, :], ra[0][:, :, :], wide(k1), ALU.is_equal))
                    step(nc.vector.scalar_tensor_tensor(ra[2][:, :, :], ra[1][:, :, :], -BIG, logits, ALU.mult, ALU.add))
                    step(nc.vector.reduce_max(m2[:, :, :], ra[2][:, :, :], AX_X))
                    step(nc.vector.tensor_tensor(d[:, :, :], m2[:, :, :], m1[:, :, :], ALU.subtract))
                    step(nc.vector.tensor_tensor(ra[3][:, :, :], ra[2][:, :, :], wide(m2), ALU.is_ge))
                    step(nc.vector.tensor_tensor(ra[3][:, :, :], ra[3][:, :, :], order, ALU.mult))
                    step(nc.vector.reduce_max(k2[:, :, :], ra[3][:, :, :], AX_X))
                    step(nc.vector.tensor_tensor(ra[4][:, :, :], ra[3][:, :, :], wide(k2), ALU.is_equal))
                    ve.wait_ge(s_ra, c + 1)
                    step(nc.vector.tensor_scalar(s[:, :, :], d[:, :, :], 1.0, None, ALU.add))
                    step(nc.vector.reciprocal(r[:, :, :], s[:, :, :]))
                    step(nc.vector.tensor_tensor(p2[:, :, :], d[:, :, :], r[:, :, :], ALU.mult))
                    step(nc.vector.tensor_tensor(ra[5][:, :, :], ra[1][:, :, :], wide(r), ALU.mult))
                    step(nc.vector.tensor_tensor(ra[4][:, :, :], ra[4][:, :, :], wide(p2), ALU.mult))
                    step(nc.vector.tensor_tensor(wt[:, u, :, :], ra[5][:, :, :], ra[4][:, :, :], ALU.add))
                    step(nc.vector.tensor_copy(wtp[:, u, :, 0:E], wt[:, u, :, :]))
                    step(nc.vector.tensor_tensor(wtr[:, :, :], wt[:, u, :, :], wtp[:, u, :, 0:E], ALU.subtract))
                    step(nc.vector.tensor_copy(wtp[:, u, :, E:2 * E], wtr[:, :, :]))
                    step(nc.vector.tensor_tensor(wtp[:, u, :, 2 * E:3 * E], wtr[:, :, :], wtp[:, u, :, E:2 * E], ALU.subtract))
                    assert done[0] == NR

                def clip(c, e):
                    n = E * c + e
                    ve.wait_ge(s_g, n + 1)
                    after(ve, s_gl, n - 1)
                    nc.vector.tensor_scalar(gate[:, e % 2, :], ps_g[e % 2][:, :], bgu[:, e, 0:1], LIMIT, ALU.add, ALU.min)\
                        .then_inc(s_gc, 1)
                    ve.wait_ge(s_uc, n + 1)
                    nc.vector.tensor_scalar(upc[:, e % 2, :], up[:, e % 2, :], LIMIT + 1.0, 1.0 - LIMIT, ALU.min, ALU.max)\
                        .then_inc(s_ucl, 1)

                def weigh(c, e):
                    n = E * c + e
                    ve.wait_ge(s_th, n + 1)
                    ve.wait_ge(s_pr, n + 1)
                    nc.vector.scalar_tensor_tensor(glu[:, e % 2, :], th[:, e % 2, :], 1.0, prod[:, e % 2, :],
                                                   ALU.add, ALU.mult).then_inc(s_gl, 1)
                    ve.wait_ge(s_gl, n + 1)
                    ve.wait_ge(s_bc, n + 1)
                    after(ve, s_dn, n - 1)
                    nc.vector.tensor_tensor(act[:, e % 2, :], ps_w[:, :], glu[:, e % 2, :], ALU.mult).then_inc(s_act, 1)

                def add_residual(c, u):
                    ve.wait_ge(s_dn, E * c + E)
                    nc.vector.tensor_tensor(xn[:, bass.ds(4 * c, 4), :], ps_d[:, :].rearrange("p (t c) -> p t c", t=4),
                                            x1[:, u, :, :], ALU.add).then_inc(s_y, 1)
                    ve.wait_ge(s_c, 4)
                    ve.wait_ge(s_y, c + 1)
                    for t in range(4):
                        nc.vector.bn_stats(bns[:, bass.ds(4 * c + t, 1), :], xn[:, bass.ds(4 * c + t, 1), :]).then_inc(s_bn, 1)

                def chunk(c, u, prev=True, nxt=True):
                    for e in range(E):
                        clip(c, e)
                        if e >= 1:
                            weigh(c, e - 1)
                        elif prev:
                            weigh(c - 1, E - 1)
                        if e == 2 and prev:
                            add_residual(c - 1, 1 - u)
                        if nxt:
                            if e == 3:
                                normalise(c + 1, 1 - u)
                            if e == 5:
                                route(c + 1, 1 - u)

                normalise(0, 0)
                route(0, 0)
                chunk(0, 0, prev=False)
                chunk(1, 1)
                with ve.Fori(1, NCH // 2 - 1) as k:
                    for u in range(2):
                        chunk(2 * k + u, u)
                chunk(NCH - 2, 0)
                chunk(NCH - 1, 1, nxt=False)
                weigh(NCH - 1, E - 1)
                add_residual(NCH - 1, 1)
                merge_stats(nc, ve, stats, bns, s_bn, s_ag)

            @block.scalar
            def _(act_e):
                act_e.wait_ge(s_c, 4)

                def prepare(c, u, what):
                    if what == 0:
                        act_e.wait_ge(s_xp, c + 1)
                        nc.scalar.activation(x1T[:, u, :], ps_x[:, :], ACT.Copy).then_inc(s_xT, 1)
                    elif what == 1:
                        act_e.wait_ge(s_rt, NR * c + 8)
                        nc.scalar.activation(rs[4][:, :, :], rs[4][:, :, :], ACT.Exp).then_inc(s_ra, 1)
                    else:
                        act_e.wait_ge(s_wtp, c + 1)
                        for t in range(4):
                            last = nc.scalar.activation(wTp[:, u, t * P:(t + 1) * P], ps_r[0:32, 64 * t:64 * t + 64].bitcast(BF16), ACT.Copy)
                        last.then_inc(s_wT, 1)
                        act_e.wait_ge(s_wx, c + 1)
                        nc.scalar.activation(wT[:, u, :], ps_r[0:E, :], ACT.Copy).then_inc(s_wT, 1)

                def expert(c, e):
                    n = E * c + e
                    act_e.wait_ge(s_u, n + 1)
                    after(act_e, s_ucl, n - 1)
                    nc.scalar.activation(up[:, e % 2, :], ps_u[e % 2][:, :], ACT.Identity, bias=bup[:, e:e + 1]).then_inc(s_uc, 1)
                    act_e.wait_ge(s_gc, n + 1)
                    after(act_e, s_gl, n - 1)
                    nc.scalar.activation(th[:, e % 2, :], gate[:, e % 2, :], ACT.Tanh, scale=ALPHA / 2).then_inc(s_th, 1)

                def chunk(c, u, nxt=True):
                    for e in range(E):
                        expert(c, e)
                        if nxt:
                            if e == 4:
                                prepare(c + 1, 1 - u, 0)
                            if e == 5:
                                prepare(c + 1, 1 - u, 1)
                            if e == 7:
                                prepare(c + 1, 1 - u, 2)

                for what in range(3):
                    prepare(0, 0, what)
                chunk(0, 0)
                chunk(1, 1)
                with act_e.Fori(1, NCH // 2 - 1) as k:
                    for u in range(2):
                        chunk(2 * k + u, u)
                chunk(NCH - 2, 0)
                chunk(NCH - 1, 1, nxt=False)

            @block.gpsimd
            def _(pool):
                def product(n, e):
                    after(pool, s_gl, n - 1)
                    pool.wait_ge(s_ucl, n + 1)
                    nc.gpsimd.tensor_tensor(prod[:, e % 2, :], upc[:, e % 2, :], gate[:, e % 2, :], ALU.mult).then_inc(s_pr, 1)

                for e in range(E):
                    product(e, e)
                with pool.Fori(1, NCH) as c:
                    for e in range(E):
                        product(E * c + e, e)


def layer1_attention(nc, io, xn, stats, norm, consts):
    scratch = [nc.dram_tensor(f"scratch1_{n}", [NCH, NSLOT, 2 * P, CH], BF16, kind="Internal").ap() for n in "qk"]
    with ExitStack() as keep:
        v_all = keep.enter_context(nc.sbuf_tensor("v_all1", [P, NTILE, H, HV], F32))
        wo = keep.enter_context(nc.sbuf_tensor("wo1", [P, P], F32))
        project_layer1(nc, io, scratch, v_all, wo, xn, stats, norm, consts)
        attend(nc, "a1", scratch, 6 * FD, v_all, xn, stats, consts, wo, None, softmax=False)


def project_layer1(nc, io, scratch, v_all, wo, xn, stats, norm, consts):
    ident = consts["ident"]
    with ExitStack() as ctx:
        def sb(name, shape, dt=F32):
            return ctx.enter_context(nc.sbuf_tensor(f"p1_{name}", shape, dt))

        def ps(name, shape, dt=F32):
            return ctx.enter_context(nc.psum_tensor(f"p1_{name}", shape, dt))

        phase = ctx.enter_context(Semaphores(nc))

        def sem(name):
            return phase.take(f"p1_{name}")

        wqk = sb("wqk", [P, 4, P])
        wv = sb("wv", [P, P])
        x2 = sb("x2", [P, 2, 4, C])
        x2T = sb("x2T", [P, 2, CH])
        resid = sb("resid", [P, 2, CH])
        parts = sb("parts", [P, 8, 3, CH], BF16)
        ps_qk = [ps(f"ps_qk{i}", [P, CH]) for i in range(4)]
        ps_x = [ps(f"ps_x{i}", [P, CH]) for i in range(2)]
        ps_v = ps("ps_v", [P, CH])

        s_w = sem("weights_loaded")
        s_ones = sem("ones_set")
        s_x2 = sem("tile_normalised")
        s_back = sem("x2_kept")
        s_xp = sem("x_transposed")
        s_xT = sem("x_rows_copied")
        s_proj = sem("qk_projected")
        s_hi = sem("hi_done")
        s_r1 = sem("residual_done")
        s_mid = sem("mid_done")
        s_lo = sem("lo_done")
        s_store = [sem(f"parts_stored{i}") for i in range(8)]
        s_vp = sem("v_projected")
        s_vc = sem("v_copied")
        s_gate = sem("gate_pool")

        with nc.Block() as block:
            @block.sync
            def _(sp):
                for dst, src in ((wqk[:, :, :], io["wqk1"]), (wv[:, :], io["wv1"]), (wo[:, :], io["wo1"])):
                    sp.dma_start(dst, src).then_inc(s_w, 16)

                def store(c, u):
                    for i in range(4):
                        sp.wait_ge(s_lo, 4 * c + i + 1)
                        src = parts[:, 4 * u + i, :, :]
                        half = P * (i % 2)
                        dst = scratch[i // 2][bass.ds(c, 1), :, half:half + P, :].rearrange("c s p t -> p (c s) t")
                        for s0, m, part in SLOT_RUNS:
                            if i < 2:
                                sp.dma_start(dst[:, s0:s0 + m, :], src[:, 0:m, :]).then_inc(s_store[4 * u + i], 16)
                            else:
                                sp.dma_start(dst[:, s0:s0 + m, :],
                                             src[:, part:part + 1, :].to_broadcast([P, m, CH])).then_inc(s_store[4 * u + i], 16)

                with sp.Fori(0, NCH // 2) as k:
                    for u in range(2):
                        store(2 * k + u, u)
                for n in range(8):
                    sp.wait_ge(s_store[n], 48 * (NCH // 2))

            @block.tensor
            def _(pe):
                pe.wait_ge(s_w, 48)

                def chunk(c, u):
                    pe.wait_ge(s_x2, 4 * c + 4)
                    after(pe, s_xT, c - 1)
                    for t in range(4):
                        last = nc.tensor.transpose(ps_x[u][:, t * P:(t + 1) * P], x2[:, u, t, :], ident[:, :])
                    last.then_inc(s_xp, 1)
                    pe.wait_ge(s_xT, c + 1)
                    for i in range(4):
                        after(pe, s_r1, 4 * c + i - 3)
                        nc.tensor.matmul(ps_qk[i][:, :], wqk[:, i, :], x2T[:, u, :], start=True, stop=True).then_inc(s_proj, 1)
                    after(pe, s_vc, c)
                    for t in range(4):
                        last = nc.tensor.matmul(ps_v[:, t * P:(t + 1) * P], x2T[:, u, t * P:(t + 1) * P], wv[:, :],
                                                start=True, stop=True)
                    last.then_inc(s_vp, 1)

                for u in range(2):
                    chunk(u, u)
                with pe.Fori(1, NCH // 2) as k:
                    for u in range(2):
                        chunk(2 * k + u, u)

            @block.vector
            def _(ve):
                nc.vector.memset(v_all[:, :, :, HD:HV], 1.0).then_inc(s_ones, 1)

                def normalise(c, u):
                    after(ve, s_xp, c - 1)
                    after(ve, s_back, c - 1)
                    for t in range(4):
                        nc.vector.tensor_scalar(x2[:, u, t, :], xn[:, bass.ds(4 * c + t, 1), :],
                                                stats[:, bass.ds(4 * c + t, 1), 0:1], norm.rstd[:, bass.ds(4 * c + t, 1)],
                                                ALU.subtract, ALU.mult).then_inc(s_x2, 1)

                def residuals(c, u):
                    for i in range(4):
                        n = 4 * c + i
                        ve.wait_ge(s_hi, n + 1)
                        after(ve, s_lo, n - 1)
                        nc.vector.tensor_tensor(resid[:, i % 2, :], ps_qk[i][:, :], parts[:, 4 * u + i, 0, :],
                                                ALU.subtract).then_inc(s_r1, 1)

                normalise(0, 0)
                normalise(1, 1)
                residuals(0, 0)
                with ve.Fori(1, NCH // 2) as k:
                    for u in range(2):
                        normalise(2 * k + u, u)
                        residuals(2 * k + u - 1, 1 - u)
                residuals(NCH - 1, 1)

            @block.scalar
            def _(act):
                act.wait_ge(s_ones, 1)

                def copy_x(c, u):
                    act.wait_ge(s_xp, c + 1)
                    after(act, s_vp, c - 1)
                    nc.scalar.activation(x2T[:, u, :], ps_x[u][:, :], ACT.Copy).then_inc(s_xT, 1)

                def chunk(c, k, u):
                    copy_x(c, u)
                    for i in range(4):
                        n = 4 * c + i
                        act.wait_ge(s_proj, n + 1)
                        after(act, s_store[4 * u + i], 48 * k)
                        nc.scalar.activation(parts[:, 4 * u + i, 0, :], ps_qk[i][:, :], ACT.Copy).then_inc(s_hi, 1)
                        act.wait_ge(s_r1, n + 1)
                        nc.scalar.activation(parts[:, 4 * u + i, 1, :], resid[:, i % 2, :], ACT.Copy).then_inc(s_mid, 1)
                    act.wait_ge(s_vp, c + 1)
                    nc.scalar.activation(v_all[:, bass.ds(4 * c, 4), :, 0:HD],
                                         ps_v[:, :].rearrange("p (t h d) -> p t h d", t=4, h=H), ACT.Copy).then_inc(s_vc, 1)

                for u in range(2):
                    chunk(u, 0, u)
                with act.Fori(1, NCH // 2) as k:
                    for u in range(2):
                        chunk(2 * k + u, k, u)

            @block.gpsimd
            def _(pool):
                def chunk(c, u):
                    settled(pool, s_x2, 4 * c + 4, s_gate)
                    nc.gpsimd.tensor_copy(xn[:, bass.ds(4 * c, 4), :], x2[:, u, :, :]).then_inc(s_back, 1)
                    for i in range(4):
                        pool.wait_ge(s_mid, 4 * c + i + 1)
                        nc.gpsimd.tensor_tensor(parts[:, 4 * u + i, 2, :], resid[:, i % 2, :], parts[:, 4 * u + i, 1, :],
                                                ALU.subtract).then_inc(s_lo, 1)

                for u in range(2):
                    chunk(u, u)
                with pool.Fori(1, NCH // 2) as k:
                    for u in range(2):
                        chunk(2 * k + u, u)


def score_tokens(nc, io, xn, stats, stats_y, norm, gate_act, consts):
    ident = consts["ident"]
    with ExitStack() as ctx:
        def sb(name, shape, dt=F32):
            return ctx.enter_context(nc.sbuf_tensor(f"g_{name}", shape, dt))

        phase = ctx.enter_context(Semaphores(nc))

        def sem(name):
            return phase.take(f"g_{name}")

        wg = sb("wg", [P, E])
        x3 = sb("x3", [P, 2, 4, C])
        x3T = sb("x3T", [P, 2, CH])
        bns = sb("bns", [P, NTILE, 6])
        ps_x = [ctx.enter_context(nc.psum_tensor(f"g_ps_x{i}", [P, CH], F32)) for i in range(2)]
        ps_s = [ctx.enter_context(nc.psum_tensor(f"g_ps_s{i}", [P, CH], F32)) for i in range(2)]
        s_w = sem("weights_loaded")
        s_x3 = sem("tile_normalised")
        s_back = sem("x3_kept")
        s_xp = sem("x_transposed")
        s_xT = sem("x_rows_copied")
        s_sc = sem("scores_ready")
        s_th = sem("tanh_done")
        s_bn = sem("row_stats_taken")
        s_ag = sem("row_stats_merged")
        s_gate = sem("gate_pool")
        with nc.Block() as block:
            @block.sync
            def _(sp):
                sp.dma_start(wg[:, :], io["wg1"]).then_inc(s_w, 16)

            @block.tensor
            def _(pe):
                pe.wait_ge(s_w, 16)

                def chunk(c, u):
                    pe.wait_ge(s_x3, 4 * c + 4)
                    after(pe, s_xT, c - 1)
                    for t in range(4):
                        last = nc.tensor.transpose(ps_x[u][:, t * P:(t + 1) * P], x3[:, u, t, :], ident[:, :])
                    last.then_inc(s_xp, 1)

                def score(c, u):
                    pe.wait_ge(s_xT, c + 1)
                    after(pe, s_th, c - 1)
                    for t in range(4):
                        last = nc.tensor.matmul(ps_s[u][:, t * E:(t + 1) * E], x3T[:, u, t * P:(t + 1) * P], wg[:, :],
                                                start=True, stop=True)
                    last.then_inc(s_sc, 1)

                chunk(0, 0)
                chunk(1, 1)
                score(0, 0)
                with pe.Fori(1, NCH // 2) as k:
                    for u in range(2):
                        chunk(2 * k + u, u)
                        score(2 * k + u - 1, 1 - u)
                score(NCH - 1, 1)

            @block.vector
            def _(ve):
                ve.wait_ge(s_w, 16)

                def chunk(c, u):
                    after(ve, s_xp, c - 1)
                    after(ve, s_back, c - 1)
                    for t in range(4):
                        nc.vector.tensor_scalar(x3[:, u, t, :], xn[:, bass.ds(4 * c + t, 1), :],
                                                stats[:, bass.ds(4 * c + t, 1), 0:1], norm.rstd[:, bass.ds(4 * c + t, 1)],
                                                ALU.subtract, ALU.mult).then_inc(s_x3, 1)
                    ve.wait_ge(s_w, 16)
                    ve.wait_ge(s_x3, 4 * c + 4)
                    for t in range(4):
                        nc.vector.bn_stats(bns[:, bass.ds(4 * c + t, 1), :], x3[:, u, t, :]).then_inc(s_bn, 1)

                for u in range(2):
                    chunk(u, u)
                with ve.Fori(1, NCH // 2) as k:
                    for u in range(2):
                        chunk(2 * k + u, u)
                merge_stats(nc, ve, stats_y, bns, s_bn, s_ag)

            @block.scalar
            def _(act):
                def chunk(c, u):
                    act.wait_ge(s_xp, c + 1)
                    after(act, s_sc, c - 1)
                    nc.scalar.activation(x3T[:, u, :], ps_x[u][:, :], ACT.Copy).then_inc(s_xT, 1)
                    act.wait_ge(s_sc, c + 1)
                    nc.scalar.activation(gate_act[:, :, bass.ds(4 * c, 4)],
                                         ps_s[u][:, 0:4 * E].rearrange("p (t e) -> p e t", t=4), ACT.Tanh).then_inc(s_th, 1)

                chunk(0, 0)
                chunk(1, 1)
                with act.Fori(1, NCH // 2) as k:
                    for u in range(2):
                        chunk(2 * k + u, u)

            @block.gpsimd
            def _(pool):
                def chunk(c, u):
                    settled(pool, s_x3, 4 * c + 4, s_gate)
                    nc.gpsimd.tensor_copy(xn[:, bass.ds(4 * c, 4), :], x3[:, u, :, :]).then_inc(s_back, 1)

                for u in range(2):
                    chunk(u, u)
                with pool.Fori(1, NCH // 2) as k:
                    for u in range(2):
                        chunk(2 * k + u, u)


def choose_tokens(nc, io, xn, stats_y, norm_y, gate_act, picked, kept, sum_d, norm_d, consts):
    ident, upper, ones_sq = consts["ident"], consts["upper"], consts["ones_sq"]
    NT, NV = NTILE, 5
    with ExitStack() as ctx:
        def sb(name, shape, dt=F32):
            return ctx.enter_context(nc.sbuf_tensor(f"c_{name}", shape, dt))

        phase = ctx.enter_context(Semaphores(nc))

        def sem(name):
            return phase.take(f"c_{name}")

        score = sb("score", [P, E, NT])
        hit = sb("hit", [P, E, NT])
        more = sb("more", [P, E, NT])
        equal = sb("equal", [P, E, NT])
        sel = sb("sel", [P, E, NT])
        pos = sb("pos", [P, E, NT])
        total = sb("total", [P, E, NT])
        running = sb("running", [P, E, NT])
        quarter = sb("quarter", [P, E, NT])
        in_q = [sb(f"in_q{i}", [P, E, NT]) for i in range(4)]
        wpart = [sb(f"wpart{i}", [P, E, NT], BF16) for i in range(3)]
        wres = sb("wres", [P, E, NT])
        vals = sb("vals", [P, E, NT, NV, 4], BF16)
        onehot = sb("onehot", [P, 2, NT, P], BF16)
        iota = sb("iota", [P, 1, P])
        tile0 = sb("tile0", [P, 1, NT])
        not0 = sb("not0", [P, E * NT])
        row = sb("row", [P, 1])
        strict = sb("strict", [P, P])
        count = sb("count", [P, E, 1])
        thr, cand, base, step_, half, take, held, need = [sb(n, [P, E, 1]) for n in
                                                    ("thr", "cand", "base", "step", "half", "take", "held", "need")]
        found = sb("found", [P, E, NV, 4])
        yn = sb("yn", [P, NT, C])
        twice = sb("twice", [P, NT, C])
        ps_c = ctx.enter_context(nc.psum_tensor("c_ps_c", [P, 512], F32))
        ps_p = ctx.enter_context(nc.psum_tensor("c_ps_p", [P, 512], F32))
        ps_t = ctx.enter_context(nc.psum_tensor("c_ps_t", [P, 512], F32))
        ps_f = ctx.enter_context(nc.psum_tensor("c_ps_f", [P, 512], F32))
        tot8 = ps_c[:, 0:E].rearrange("p (e o) -> p e o", o=1)
        before = ps_p[:, 0:E * NT].rearrange("p (e t) -> p e t", e=E)
        tiles = ps_t[:, 0:E * NT].rearrange("p (e t) -> p e t", e=E)
        hits = ps_f[:, 0:E * NV * 4].rearrange("p (e v a) -> p e v a", e=E, v=NV)

        s_w = sem("constants_loaded")
        s_st = sem("vector_step")
        s_cnt = sem("rows_counted")
        s_tot = sem("tokens_counted")
        s_src = sem("flags_ready")
        s_pre = sem("prefixes_ready")
        s_oh = sem("onehot_ready")
        s_used = sem("onehot_used")
        s_y = sem("tile_normalised")
        s_two = sem("x3_doubled")
        s_d = sem("rows_stored")

        def flat(x):
            return x[:, :, :].rearrange("p e t -> p (e t)")

        with nc.Block() as block:
            @block.sync
            def _(sp):
                for dst, src in ((iota[:, 0, :], io["iota"]), (tile0[:, 0, :], io["tile0"]), (not0[:, :], io["not0"]),
                                 (row[:, :], io["row"])):
                    sp.dma_start(dst, src).then_inc(s_w, 16)
                sp.wait_ge(s_two, 1)
                sp.dma_start(sum_d.rearrange("(t p) c -> p t c", p=P), twice[:, :, :]).then_inc(s_d, 16)
                sp.wait_ge(s_y, NT)
                sp.dma_start(norm_d.rearrange("(t p) c -> p t c", p=P), yn[:, :, :]).then_inc(s_d, 16)
                sp.wait_ge(s_d, 32)

            @block.scalar
            def _(act):
                nc.scalar.activation(twice[:, :, :], xn[:, :, :], ACT.Copy, scale=2.0).then_inc(s_two, 1)

            @block.gpsimd
            def _(pool):
                for t in range(NT):
                    nc.gpsimd.tensor_scalar(yn[:, t, :], xn[:, t, :], stats_y[:, t, 0:1], norm_y.rstd[:, t:t + 1],
                                            ALU.subtract, ALU.mult).then_inc(s_y, 1)

            @block.tensor
            def _(pe):
                with pe.Fori(0, BITS) as i:
                    pe.wait_ge(s_cnt, i + 1)
                    nc.tensor.matmul(ps_c[:, 0:E], ones_sq[:, :], count[:, :, 0], start=True, stop=True).then_inc(s_tot, 1)
                pe.wait_ge(s_cnt, BITS + 1)
                nc.tensor.matmul(ps_c[:, 0:E], ones_sq[:, :], count[:, :, 0], start=True, stop=True).then_inc(s_tot, 1)
                for n, src in enumerate((equal, sel)):
                    pe.wait_ge(s_src, n + 1)
                    nc.tensor.matmul(ps_t[:, 0:E * NT], ones_sq[:, :], flat(src), start=True, stop=True).then_inc(s_pre, 1)
                    nc.tensor.matmul(ps_p[:, 0:E * NT], strict[:, :], flat(src), start=True, stop=True).then_inc(s_pre, 1)
                for e in range(E):
                    pe.wait_ge(s_oh, e + 1)
                    for t in range(NT):
                        last = nc.tensor.matmul(hits[:, e, :, :], onehot[:, e % 2, t, :], vals[:, e, t, :, :],
                                                start=e == 0 and t == 0, stop=t == NT - 1, skip_group_check=True)
                    last.then_inc(s_used, 1)

            @block.vector
            def _(ve):
                done = [0]

                def step(ins):
                    done[0] += 1
                    ins.then_inc(s_st, 1)
                    ve.wait_ge(s_st, done[0])

                def wide(x):
                    return x[:, :, :].to_broadcast([P, E, NT])

                v = nc.vector
                ve.wait_ge(s_w, 64)
                step(v.tensor_scalar(score[:, :, :], gate_act[:, :, :], 1.0, 0.5, ALU.add, ALU.mult))
                step(v.memset(thr[:, :, :], 0.0))
                step(v.memset(cand[:, :, :], 1.0))
                step(v.memset(step_[:, :, :], 1.0))
                step(v.tensor_tensor(strict[:, :], upper[:, :], ident[:, :], ALU.subtract))
                base0, per = done[0], 8
                with ve.Fori(0, BITS) as i:
                    n = [0]

                    def bit(ins, wait=True):
                        n[0] += 1
                        ins.then_inc(s_st, 1)
                        if wait:
                            ve.wait_ge(s_st, per * i + (base0 + n[0]))

                    bit(v.tensor_tensor(hit[:, :, :], score[:, :, :], wide(cand), ALU.is_ge))
                    v.reduce_sum(count[:, :, :], hit[:, :, :], AX_X).then_inc(s_cnt, 1)
                    bit(v.tensor_scalar(half[:, :, :], step_[:, :, :], 0.5, None, ALU.mult))
                    bit(v.tensor_tensor(base[:, :, :], cand[:, :, :], half[:, :, :], ALU.subtract))
                    ve.wait_ge(s_tot, i + 1)
                    bit(v.scalar_tensor_tensor(take[:, :, :], tot8, CAP - 0.5, step_[:, :, :], ALU.is_ge, ALU.mult))
                    bit(v.scalar_tensor_tensor(held[:, :, :], tot8, CAP - 0.5, cand[:, :, :], ALU.is_ge, ALU.mult))
                    bit(v.tensor_tensor(cand[:, :, :], base[:, :, :], take[:, :, :], ALU.add), wait=False)
                    bit(v.tensor_tensor(thr[:, :, :], thr[:, :, :], held[:, :, :], ALU.max), wait=False)
                    bit(v.tensor_copy(step_[:, :, :], half[:, :, :]))
                    assert n[0] == per
                done[0] = base0 + per * BITS

                step(v.tensor_tensor(more[:, :, :], score[:, :, :], wide(thr), ALU.is_gt))
                v.reduce_sum(count[:, :, :], more[:, :, :], AX_X).then_inc(s_cnt, 1)
                v.tensor_tensor(equal[:, :, :], score[:, :, :], wide(thr), ALU.is_equal).then_inc(s_src, 1)
                ve.wait_ge(s_tot, BITS + 1)
                step(v.tensor_scalar(need[:, :, :], tot8, -1.0, float(CAP), ALU.mult, ALU.add))

                def prefix(n):
                    ve.wait_ge(s_pre, 2 * n + 1)
                    step(v.tensor_copy(total[:, :, :], tiles))
                    step(v.tensor_tensor_scan(flat(running), not0[:, :], flat(total), 0.0, ALU.mult, ALU.add))
                    step(v.tensor_tensor(running[:, :, :], running[:, :, :], total[:, :, :], ALU.subtract))
                    ve.wait_ge(s_pre, 2 * n + 2)
                    step(v.tensor_tensor(pos[:, :, :], before, running[:, :, :], ALU.add))

                prefix(0)
                step(v.tensor_tensor(sel[:, :, :], pos[:, :, :], wide(need), ALU.is_lt))
                step(v.tensor_tensor(sel[:, :, :], sel[:, :, :], equal[:, :, :], ALU.mult))
                v.tensor_tensor(sel[:, :, :], sel[:, :, :], more[:, :, :], ALU.add).then_inc(s_src, 1)
                step(v.tensor_copy(wpart[0][:, :, :], score[:, :, :]))
                step(v.tensor_tensor(wres[:, :, :], score[:, :, :], wpart[0][:, :, :], ALU.subtract))
                step(v.tensor_copy(wpart[1][:, :, :], wres[:, :, :]))
                step(v.tensor_tensor(wpart[2][:, :, :], wres[:, :, :], wpart[1][:, :, :], ALU.subtract))
                prefix(1)
                step(v.tensor_scalar(quarter[:, :, :], pos[:, :, :], float(P), None, ALU.is_ge))
                for q in (2, 3):
                    step(v.scalar_tensor_tensor(quarter[:, :, :], pos[:, :, :], float(q * P), quarter[:, :, :], ALU.is_ge, ALU.add))
                for q in range(4):
                    step(v.scalar_tensor_tensor(in_q[q][:, :, :], quarter[:, :, :], float(q), sel[:, :, :], ALU.is_equal, ALU.mult))
                step(v.scalar_tensor_tensor(pos[:, :, :], quarter[:, :, :], -float(P), pos[:, :, :], ALU.mult, ALU.add))
                for q in range(4):
                    step(v.tensor_tensor(vals[:, :, :, 0, q], in_q[q][:, :, :], tile0[:, :, :].to_broadcast([P, E, NT]), ALU.mult))
                    step(v.tensor_scalar(vals[:, :, :, 1, q], in_q[q][:, :, :], row[:, 0:1], None, ALU.mult))
                    for i in range(3):
                        step(v.tensor_tensor(vals[:, :, :, 2 + i, q], in_q[q][:, :, :], wpart[i][:, :, :], ALU.mult))
                for e in range(E):
                    after(ve, s_used, e - 1)
                    v.tensor_tensor(onehot[:, e % 2, :, :], iota[:, :, :].to_broadcast([P, NT, P]),
                                    pos[:, e, :].rearrange("p (t o) -> p t o", o=1).to_broadcast([P, NT, P]),
                                    ALU.is_equal).then_inc(s_oh, 1)
                ve.wait_ge(s_used, E)
                step(v.tensor_copy(found[:, :, :, :], hits))
                step(v.tensor_tensor(picked[:, :, :], found[:, :, 0, :], found[:, :, 1, :], ALU.add))
                step(v.tensor_tensor(kept[:, :, :], found[:, :, 2, :], found[:, :, 3, :], ALU.add))
                step(v.tensor_tensor(kept[:, :, :], kept[:, :, :], found[:, :, 4, :], ALU.add))


def expert_layer1(nc, io, picked, kept, sum_d, norm_d, consts):
    ident, ones_row = consts["ident"], consts["ones_row"]
    F = 4 * P
    with ExitStack() as ctx:
        def sb(name, shape, dt=F32):
            return ctx.enter_context(nc.sbuf_tensor(f"m1_{name}", shape, dt))

        phase = ctx.enter_context(Semaphores(nc))

        def sem(name):
            return phase.take(f"m1_{name}")

        w = sb("w", [P, 2, 2 * F + 4])
        b2 = sb("b2", [1, 2, C])
        gb = sb("gb", [P, 2])
        idx = sb("idx", [P, 2, 4], I32)
        kw = sb("kw", [P, 2, 4, 1])
        y = sb("y", [P, 2, 4, C])
        yT = sb("yT", [P, 2, CAP])
        hT = sb("hT", [P, 2, 4, CAP])
        o = sb("o", [P, 2, 4, C])
        ps_x = ctx.enter_context(nc.psum_tensor("m1_ps_x", [P, CAP], F32))
        ps_h = [ctx.enter_context(nc.psum_tensor(f"m1_ps_h{i}", [P, CAP], F32)) for i in range(2)]
        ps_o = [ctx.enter_context(nc.psum_tensor(f"m1_ps_o{i}", [P, CAP], F32)) for i in range(2)]
        s_c = sem("norm_weights_loaded")
        s_w = [sem(f"weights_loaded{i}") for i in range(2)]
        s_ix = sem("indices_ready")
        s_kw = sem("scores_ready")
        s_y = [sem(f"rows_gathered{i}") for i in range(2)]
        s_yp = sem("rows_transposed")
        s_yT = sem("rows_scaled")
        s_h = sem("hidden_ready")
        s_g = sem("gelu_done")
        s_o = sem("output_ready")
        s_ow = sem("output_weighted")
        s_sc = sem("rows_added")
        s_gate = sem("gate_pool")

        with nc.Block() as block:
            @block.sync
            def _(sp):
                sp.dma_start(gb[:, :], io["gb1"]).then_inc(s_c, 16)

                def load(e, u):
                    sp.dma_start(w[:, u, :], io["w1"][bass.ds(e, 1), :, :].rearrange("e p f -> (e p) f")).then_inc(s_w[u], 16)
                    sp.dma_start(b2[:, u, :], io["b2"][bass.ds(e, 1), :]).then_inc(s_w[u], 16)

                for u in range(2):
                    load(u, u)
                with sp.Fori(1, E // 2) as k:
                    for u in range(2):
                        sp.wait_ge(s_o, 2 * k + u - 1)
                        load(2 * k + u, u)

            @block.gpsimd
            def _(pool):
                def gather(e, k, u):
                    settled(pool, s_ix, e + 1, s_gate)
                    settled(pool, s_yp, e - 1, s_gate)
                    for a in range(4):
                        nc.gpsimd.indirect_dma_start(out=y[:, u, a, :], out_offset=None, in_=norm_d,
                                                     in_offset=bass.IndirectOffsetOnAxis(ap=idx[:, u, a:a + 1], axis=0))\
                            .then_inc(s_y[u], 16)

                def scatter(e, u):
                    settled(pool, s_ow, e + 1, s_gate)
                    for a in range(4):
                        settled(pool, s_sc, 64 * e + 16 * a, s_gate)
                        nc.gpsimd.indirect_dma_start(out=sum_d, out_offset=bass.IndirectOffsetOnAxis(ap=idx[:, u, a:a + 1], axis=0),
                                                     in_=o[:, u, a, :], in_offset=None, compute_op=ALU.add)\
                            .then_inc(s_sc, 16)

                def pair(k, more=True):
                    gather(2 * k + 1, k, 1)
                    scatter(2 * k, 0)
                    if more:
                        gather(2 * k + 2, k + 1, 0)
                    scatter(2 * k + 1, 1)

                gather(0, 0, 0)
                pair(0)
                with pool.Fori(1, E // 2 - 1) as k:
                    pair(k)
                pair(E // 2 - 1, more=False)
                pool.wait_ge(s_sc, 64 * E)

            @block.tensor
            def _(pe):
                def transpose(e, k, u):
                    pe.wait_ge(s_y[u], 64 * k + 64)
                    after(pe, s_yT, e)
                    for a in range(4):
                        last = nc.tensor.transpose(ps_x[:, a * P:(a + 1) * P], y[:, u, a, :], ident[:, :])
                    last.then_inc(s_yp, 1)

                def expand(e, k, u):
                    pe.wait_ge(s_w[u], 32 * k + 32)
                    pe.wait_ge(s_yT, e + 1)
                    for f in range(4):
                        after(pe, s_g, 4 * e + f - 1)
                        nc.tensor.matmul(ps_h[f % 2][:, :], w[:, u, f * P:(f + 1) * P], yT[:, u, :], start=True, stop=True)\
                            .then_inc(s_h, 1)

                def reduce(e, u):
                    after(pe, s_ow, e - 1)
                    pe.wait_ge(s_g, 4 * e + 4)
                    for a in range(4):
                        out = ps_o[u][:, a * P:(a + 1) * P]
                        nc.tensor.matmul(out, ones_row[0:1, :], b2[0:1, u, :], start=a == 0, stop=False, skip_group_check=True)
                        for f in range(4):
                            last = nc.tensor.matmul(out, hT[:, u, f, a * P:(a + 1) * P], w[:, u, F + f * P:F + (f + 1) * P],
                                                    start=False, stop=f == 3, skip_group_check=True)
                    last.then_inc(s_o, 1)

                def pair(k, more=True):
                    expand(2 * k, k, 0)
                    transpose(2 * k + 1, k, 1)
                    reduce(2 * k, 0)
                    expand(2 * k + 1, k, 1)
                    if more:
                        transpose(2 * k + 2, k + 1, 0)
                    reduce(2 * k + 1, 1)

                transpose(0, 0, 0)
                pair(0)
                with pe.Fori(1, E // 2 - 1) as k:
                    pair(k)
                pair(E // 2 - 1, more=False)

            @block.scalar
            def _(act):
                def gelu(e, k, u):
                    after(act, s_o, e - 1)
                    for f in range(4):
                        act.wait_ge(s_h, 4 * e + f + 1)
                        nc.scalar.activation(hT[:, u, f, :], ps_h[f % 2][:, :], ACT.Gelu_apprx_tanh,
                                             bias=w[:, u, 2 * F + f:2 * F + f + 1]).then_inc(s_g, 1)

                for u in range(2):
                    gelu(u, 0, u)
                with act.Fori(1, E // 2) as k:
                    for u in range(2):
                        gelu(2 * k + u, k, u)

            @block.vector
            def _(ve):
                ve.wait_ge(s_c, 16)

                def indices(e, u):
                    nc.vector.tensor_copy(idx[:, u, :], picked[:, bass.ds(e, 1), :]).then_inc(s_ix, 1)
                    nc.vector.tensor_copy(kw[:, u, :, 0], kept[:, bass.ds(e, 1), :]).then_inc(s_kw, 1)

                def scale(e, u):
                    ve.wait_ge(s_yp, e + 1)
                    after(ve, s_h, 4 * (e - 1))
                    nc.vector.tensor_scalar(yT[:, u, :], ps_x[:, :], gb[:, 0:1], gb[:, 1:2], ALU.mult, ALU.add).then_inc(s_yT, 1)

                def weigh(e, u):
                    ve.wait_ge(s_o, e + 1)
                    ve.wait_ge(s_kw, e + 1)
                    nc.vector.tensor_tensor(o[:, u, :, :], ps_o[u][:, :].rearrange("p (a c) -> p a c", a=4),
                                            kw[:, u, :, :].to_broadcast([P, 4, C]), ALU.mult).then_inc(s_ow, 1)

                def turn(e, u, last=False):
                    ve.wait_ge(s_sc, 64 * (e - 1))
                    indices(e, u)

                indices(0, 0)
                indices(1, 1)
                scale(0, 0)
                scale(1, 1)
                weigh(0, 0)
                with ve.Fori(1, E // 2) as k:
                    turn(2 * k, 0)
                    scale(2 * k, 0)
                    weigh(2 * k - 1, 1)
                    turn(2 * k + 1, 1)
                    scale(2 * k + 1, 1)
                    weigh(2 * k, 0)
                weigh(E - 1, 1)


def write_output(nc, io, xn, stats, norm, sum_d):
    with ExitStack() as ctx:
        phase = ctx.enter_context(Semaphores(nc))

        def sem(name):
            return phase.take(f"w_{name}")

        bns = ctx.enter_context(nc.sbuf_tensor("w_bns", [P, NTILE, 6], F32))
        s_x = [sem(f"sum_loaded{i}") for i in range(4)]
        s_bn = sem("row_stats_taken")
        s_ag = sem("row_stats_merged")
        s_n = sem("tile_normalised")
        s_out = sem("output_stored")
        part = NTILE // 4
        src = sum_d.rearrange("(t p) c -> p t c", p=P)
        dst = io["out"].rearrange("(t p) c -> p t c", p=P)
        with nc.Block() as block:
            @block.sync
            def _(sp):
                for i in range(4):
                    sp.dma_start(xn[:, i * part:(i + 1) * part, :], src[:, i * part:(i + 1) * part, :]).then_inc(s_x[i], 16)

            @block.vector
            def _(ve):
                for t in range(NTILE):
                    if t % part == 0:
                        ve.wait_ge(s_x[t // part], 16)
                    nc.vector.bn_stats(bns[:, t, :], xn[:, t, :]).then_inc(s_bn, 1)
                merge_stats(nc, ve, stats, bns, s_bn, s_ag)
                norm.vector(ve)
                for t in range(NTILE):
                    nc.vector.tensor_scalar(xn[:, t, :], xn[:, t, :], stats[:, t, 0:1], norm.rstd[:, t:t + 1],
                                            ALU.subtract, ALU.mult).then_inc(s_n, 1)

            @block.scalar
            def _(act):
                norm.scalar(act)
                for i in range(4):
                    act.wait_ge(s_n, part * (i + 1))
                    act.dma_start(dst[:, i * part:(i + 1) * part, :], xn[:, i * part:(i + 1) * part, :]).then_inc(s_out, 16)
                act.wait_ge(s_out, 64)


def merge_stats(nc, ve, stats, bns, s_bn, s_ag):
    ve.wait_ge(s_bn, NTILE)
    for t in range(NTILE):
        nc.vector.bn_aggr(stats[:, t, :], bns[:, t, :]).then_inc(s_ag, 1)
    ve.wait_ge(s_ag, NTILE)


def invert_spread(nc, norm):
    with nc.Block() as block:
        @block.vector
        def _(ve):
            norm.vector(ve)

        @block.scalar
        def _(act):
            norm.scalar(act)


class Norm:

    def __init__(self, nc, ctx, name, stats, n=NTILE):
        self.nc, self.stats, self.n, self.name = nc, stats, n, name
        self.ve = ctx.enter_context(nc.sbuf_tensor(f"{name}_ve", [P, n], F32))
        self.sq = ctx.enter_context(nc.sbuf_tensor(f"{name}_sq", [P, n], F32))
        self.t = ctx.enter_context(nc.sbuf_tensor(f"{name}_t", [P, n], F32))
        self.rstd = ctx.enter_context(nc.sbuf_tensor(f"{name}_rstd", [P, n], F32))
        phase = ctx.enter_context(Semaphores(nc))
        self.s_v = phase.take(f"{name}_variance")
        self.s_q = phase.take(f"{name}_root")
        self.s_r = phase.take(f"{name}_rstd")

    def vector(self, ve, base=0):
        nc = self.nc
        steps = [0]

        def step(ins):
            steps[0] += 1
            ins.then_inc(self.s_r, 1)
            ve.wait_ge(self.s_r, steps[0])

        nc.vector.tensor_scalar(self.ve[:, :], self.stats[:, :, 1], EPS, None, ALU.add).then_inc(self.s_v, 1)
        ve.wait_ge(self.s_q, 1)
        step(nc.vector.reciprocal(self.rstd[:, :], self.sq[:, :]))
        step(nc.vector.tensor_tensor(self.t[:, :], self.rstd[:, :], self.rstd[:, :], ALU.mult))
        step(nc.vector.tensor_tensor(self.t[:, :], self.t[:, :], self.ve[:, :], ALU.mult))
        step(nc.vector.tensor_scalar(self.t[:, :], self.t[:, :], -0.5, 1.5, ALU.mult, ALU.add))
        step(nc.vector.tensor_tensor(self.rstd[:, :], self.rstd[:, :], self.t[:, :], ALU.mult))

    STEPS = 5

    def scalar(self, act):
        act.wait_ge(self.s_v, 1)
        self.nc.scalar.activation(self.sq[:, :], self.ve[:, :], ACT.Sqrt).then_inc(self.s_q, 1)


def program(nc, io):
    with ExitStack() as ctx:
        def sb(name, shape, dt=F32):
            return ctx.enter_context(nc.sbuf_tensor(name, shape, dt))

        phase = ctx.enter_context(Semaphores(nc))

        def sem(name):
            return phase.take(name)

        xn = sb("xn", [P, NTILE, C])
        stats = sb("stats", [P, NTILE, 2])
        consts = {"ident": sb("ident", [P, P]), "ident_bf": sb("ident_bf", [P, P], BF16), "ones_row": sb("ones_row", [1, P]),
                  "tri4": sb("tri4", [P, 4, P], BF16), "upper": sb("upper", [P, P]), "ones_sq": sb("ones_sq", [P, P])}
        s_id = sem("ident_loaded")
        with nc.Block() as block:
            @block.sync
            def _(sp):
                sp.dma_start(consts["ident"][:, :], io["ident"]).then_inc(s_id, 16)
                sp.wait_ge(s_id, 16)
        layer0_attention(nc, io, xn, stats, consts)
        norm = Norm(nc, ctx, "norm_a", stats)
        invert_spread(nc, norm)
        expert_layer0(nc, io, xn, stats, norm, consts)
        norm = Norm(nc, ctx, "norm_b", stats)
        invert_spread(nc, norm)
        layer1_attention(nc, io, xn, stats, norm, consts)
        norm = Norm(nc, ctx, "norm_c", stats)
        invert_spread(nc, norm)
        gate_act = sb("gate_act", [P, E, NTILE])
        stats_y = sb("stats_y", [P, NTILE, 2])
        picked, kept = sb("picked", [P, E, 4]), sb("kept", [P, E, 4])
        score_tokens(nc, io, xn, stats, stats_y, norm, gate_act, consts)
        norm_y = Norm(nc, ctx, "norm_y", stats_y)
        invert_spread(nc, norm_y)
        sum_d = nc.dram_tensor("sum", [NTOK, C], F32, kind="Internal").ap()
        norm_d = nc.dram_tensor("normed", [NTOK, C], F32, kind="Internal").ap()
        choose_tokens(nc, io, xn, stats_y, norm_y, gate_act, picked, kept, sum_d, norm_d, consts)
        expert_layer1(nc, io, picked, kept, sum_d, norm_d, consts)
        write_output(nc, io, xn, stats, Norm(nc, ctx, "norm_d", stats), sum_d)


def kernel(**inputs):
    import numpy as np
    import concourse.bacc as bacc
    from concourse import mybir as _mybir
    from concourse.bass_utils import run_bass_kernel_spmd as run

    a = {k: np.asarray(v) for k, v in inputs.items()}
    f32 = np.float32

    half = HD // 2
    inv_freq = (f32(1.0) / f32(10000.0) ** (np.arange(half, dtype=f32) / f32(half))).astype(f32)
    freqs = np.arange(T, dtype=f32)[None, :] * inv_freq[:, None]
    cos = np.repeat(np.repeat(np.cos(freqs), 2, axis=0), H, axis=0).astype(f32)
    sin = np.repeat(np.repeat(np.sin(freqs), 2, axis=0), H, axis=0).astype(f32)
    sign = np.where((np.arange(P) // H) % 2 == 0, f32(-1.0), f32(1.0))[:, None]
    rot = np.ascontiguousarray(np.stack([cos, sin * sign], axis=1).astype(f32))

    dh = np.arange(P).reshape(H, HD).T.reshape(-1)
    swap = np.arange(HD) ^ 1
    dh_swap = np.arange(P).reshape(H, HD)[:, swap].T.reshape(-1)
    wqkv = a["L0_attn_Wqkv"]
    wqk = np.stack([wqkv[:, dh], wqkv[:, dh_swap], wqkv[:, P + dh], wqkv[:, P + dh_swap]], axis=1)
    x = a["L0_attn_x"].reshape(NTOK, C)
    host = {
        "x": x, "xT": x.T, "wqk": wqk, "rot": rot, "wv": wqkv[:, 2 * P:], "wo": a["L0_attn_Wo"],
        "bo": np.broadcast_to(a["L0_attn_bo"], (P, C)), "tri": np.where(np.tril(np.ones((P, P), bool)), f32(0), f32(-BIG)),
        "ident": np.eye(P, dtype=f32), "upper": np.triu(np.ones((P, P), f32)),
    }
    gu = a["L0_ffn_gate_up_proj"].reshape(E, C, P, 2)
    sel = np.zeros((32, E, P), f32)
    for part in range(3):
        sel[part * E + np.arange(E), np.arange(E)] = 1
    host.update({
        "wr": a["L0_ffn_router_weight"], "wgu": gu.transpose(1, 0, 3, 2),
        "bgu": a["L0_ffn_gate_up_proj_bias"].reshape(E, P, 2).transpose(1, 0, 2),
        "wd0": a["L0_ffn_down_proj"].transpose(1, 0, 2), "bd0": a["L0_ffn_down_proj_bias"],
        "sel": sel, "desc": np.broadcast_to(np.arange(E, 0, -1).astype(f32), (P, E)),
    })
    dh1 = np.arange(H * FD).reshape(H, FD).T.reshape(2, P)
    wqk1 = np.stack([a[w].T[:, half] for w in ("L1_attn_Wq", "L1_attn_Wk") for half in dh1], axis=1)
    host.update({"wqk1": wqk1, "wv1": a["L1_attn_Wv"].T, "wo1": a["L1_attn_Wo"].T})
    fc1T = a["L1_ffn_fc1s"].transpose(0, 2, 1)
    fc2T = a["L1_ffn_fc2s"].transpose(0, 2, 1).reshape(E, 4, P, C).transpose(0, 2, 1, 3).reshape(E, P, 4 * C)
    b1T = a["L1_ffn_b1s"].reshape(E, 4, P).transpose(0, 2, 1)
    host.update({
        "wg1": a["L1_ffn_gate_w"].T, "w1": np.concatenate([fc1T, fc2T, b1T], axis=2), "b2": a["L1_ffn_b2s"],
        "gb1": np.stack([a["L1_ffn_ln_gamma"], a["L1_ffn_ln_beta"]], axis=1),
        "iota": np.broadcast_to(np.arange(P, dtype=f32), (P, P)),
        "tile0": np.broadcast_to(P * np.arange(NTILE, dtype=f32), (P, NTILE)),
        "not0": np.broadcast_to((np.arange(E * NTILE) % NTILE != 0).astype(f32), (P, E * NTILE)),
        "row": np.arange(P, dtype=f32).reshape(P, 1),
    })
    nc = bacc.Bacc("TRN2", target_bir_lowering=False, num_devices=1)
    arrays, io = {}, {}
    for name, v in host.items():
        v = np.ascontiguousarray(v)
        arrays[f"in_{name}"] = v
        io[name] = nc.dram_tensor(f"in_{name}", v.shape, _mybir.dt.from_np(v.dtype), kind="ExternalInput").ap()
    io["out"] = nc.dram_tensor("out_x", (NTOK, C), F32, kind="ExternalOutput").ap()
    program(nc, io)
    r = run(nc, [arrays], core_ids=[0])
    return r.results[0]["out_x"].reshape(NB, T, C)
```

```python
from contextlib import ExitStack

import concourse.bass as bass
from concourse import mybir

F32 = mybir.dt.float32
BF16 = mybir.dt.bfloat16
ALU = mybir.AluOpType
ACT = mybir.ActivationFunctionType
I32 = mybir.dt.int32
AX_X = mybir.AxisListType.X

P = 128
NB, T, C = 16, 256, 128
NTOK = NB * T
NTILE = NTOK // P
H, HD = 16, 8
HV = HD + 1
VW = 32
F1 = 4 * C
W1 = 2 * F1 + 4 + C
CH = 512
NCH = NTOK // CH
FD = 16
E = 8
ALPHA, LIMIT = 1.702, 7.0
CAP = NTOK // E
ROUNDS = 13
DEN_EPS = 1e-12
NSLOT = 6
SLOT_RUNS = ((0, 3, 0), (3, 2, 1), (5, 1, 2))
UH = 8
NU = NB * H // UH
EPS = 1e-5
BIG = 1e30


def after(eng, sem, n):
    if isinstance(n, int) and n <= 0:
        return
    eng.wait_ge(sem, n)


class Semaphores:

    def __init__(self, nc):
        self.nc, self.taken = nc, []

    def __enter__(self):
        return self

    def take(self, name):
        self.taken.append(self.nc.alloc_semaphore(name))
        return self.taken[-1]

    def __exit__(self, *exc):
        if exc[0] is None:
            self.nc.clear_and_free_semaphores(self.taken)
            self.nc.all_engine_barrier()


def settled(eng, sem, n, gate):
    after(eng, sem, n)
    if not isinstance(n, int):
        eng.sem_inc(gate, 1)


def layer0_attention(nc, io, xn, stats, consts):
    scratch = [nc.dram_tensor(f"scratch0_{n}", [NCH, NSLOT, P, CH], BF16, kind="Internal").ap() for n in "qk"]
    with ExitStack() as keep:
        v_all = keep.enter_context(nc.sbuf_tensor("v_all0", [P, NTILE, H, HV], F32))
        wo = keep.enter_context(nc.sbuf_tensor("wo0", [P, P], F32))
        bo = keep.enter_context(nc.sbuf_tensor("bo0", [P, 1, C], F32))
        project_layer0(nc, io, scratch, v_all, wo, bo, xn, consts)
        attend(nc, "a0", scratch, 6 * HD, v_all, xn, stats, consts, wo, bo, softmax=True)


def project_layer0(nc, io, scratch, v_all, wo, bo, xn, consts):
    with ExitStack() as ctx:
        def sb(name, shape, dt=F32):
            return ctx.enter_context(nc.sbuf_tensor(name, shape, dt))

        def ps(name, shape, dt=F32):
            return ctx.enter_context(nc.psum_tensor(name, shape, dt))

        phase = ctx.enter_context(Semaphores(nc))

        def sem(name):
            return phase.take(name)

        ident, ident_bf, ones_row = consts["ident"], consts["ident_bf"], consts["ones_row"]
        tri4, upper, ones_sq = consts["tri4"], consts["upper"], consts["ones_sq"]
        xc = sb("xc", [P, 2, CH])
        wqk = sb("wqk", [P, 4, P])
        wv = sb("wv", [P, P])
        rot = sb("rot", [P, 2, 1, T])
        tri_f = sb("tri_f", [P, P])
        term = sb("term", [P, 2, 2, CH])
        roped = sb("roped", [P, 2, CH])
        resid = sb("resid", [P, 2, CH])
        parts = sb("parts", [P, 4, 3, CH], BF16)

        ps_b = [ps(f"ps_b{i}", [P, 1024]) for i in range(2)]
        ps_a = [ps(f"ps_a{i}", [P, 512]) for i in range(2)]
        ps_qk = [[ps_b[j][:, 512 * i:512 * i + 512] for i in range(2)] for j in range(2)]
        ps_v = ps_a[0]

        s_w = sem("weights_loaded")
        s_xn = sem("xn_loaded")
        s_xc = [sem(f"xc_loaded{i}") for i in range(2)]
        s_zero = sem("stacks_cleared")
        s_tri = sem("tri_ready")
        s_proj = sem("qk_projected")
        s_rot = sem("qk_psum_read")
        s_rope = sem("qk_roped")
        s_hi = sem("hi_done")
        s_r1 = sem("residual_done")
        s_mid = sem("mid_done")
        s_lo = sem("lo_done")
        s_store = [sem(f"parts_stored{i}") for i in range(4)]
        s_vp = sem("v_projected")
        s_vc = sem("v_copied")

        with nc.Block() as block:
            @block.sync
            def _(sp):
                for dst, src in ((wqk[:, :, :], io["wqk"]), (rot[:, :, 0, :], io["rot"]), (wv[:, :], io["wv"])):
                    sp.dma_start(dst, src).then_inc(s_w, 16)

                def load(c, u):
                    sp.dma_start(xc[:, u, :], io["xT"][:, bass.ds(c * CH, CH)]).then_inc(s_xc[u], 16)

                def store(c, u):
                    for j in range(2):
                        n = 2 * c + j
                        sp.wait_ge(s_lo, n + 1)
                        src = parts[:, 2 * u + j, :, :]
                        dst = scratch[j][bass.ds(c, 1), :, :, :].rearrange("c s p t -> p (c s) t")
                        for s0, m, part in SLOT_RUNS:
                            if j == 0:
                                sp.dma_start(dst[:, s0:s0 + m, :], src[:, 0:m, :]).then_inc(s_store[2 * u + j], 16)
                            else:
                                sp.dma_start(dst[:, s0:s0 + m, :],
                                             src[:, part:part + 1, :].to_broadcast([P, m, CH])).then_inc(s_store[2 * u + j], 16)

                for u in range(2):
                    load(u, u)
                for dst, src in ((wo[:, :], io["wo"]), (bo[:, 0, :], io["bo"]), (tri_f[:, :], io["tri"]), (upper[:, :], io["upper"])):
                    sp.dma_start(dst, src).then_inc(s_w, 16)
                sp.dma_start(xn[:, :, :], io["x"].rearrange("(t p) c -> p t c", p=P)).then_inc(s_xn, 16)
                with sp.Fori(0, NCH // 2 - 1) as k:
                    for u in range(2):
                        store(2 * k + u, u)
                        sp.wait_ge(s_vp, 2 * k + u + 1)
                        load(2 * k + u + 2, u)
                for u in range(2):
                    store(NCH - 2 + u, u)
                for n in range(4):
                    sp.wait_ge(s_store[n], 48 * (NCH // 2))
                sp.wait_ge(s_xn, 16)

            @block.tensor
            def _(pe):
                pe.wait_ge(s_w, 48)

                def chunk(k, u):
                    c = 2 * k + u
                    pe.wait_ge(s_xc[u], 16 * k + 16)
                    for j in range(2):
                        after(pe, s_rot, 2 * c + j - 1)
                        for i in range(2):
                            last = nc.tensor.matmul(ps_qk[j][i], wqk[:, 2 * j + i, :], xc[:, u, :], start=True, stop=True)
                        last.then_inc(s_proj, 1)
                    after(pe, s_vc, c)
                    for t in range(4):
                        last = nc.tensor.matmul(ps_v[:, t * P:(t + 1) * P], xc[:, u, t * P:(t + 1) * P], wv[:, :],
                                                start=True, stop=True)
                    last.then_inc(s_vp, 1)

                for u in range(2):
                    chunk(0, u)
                with pe.Fori(1, NCH // 2) as k:
                    for u in range(2):
                        chunk(k, u)

            @block.vector
            def _(ve):
                nc.vector.memset(v_all[:, :, :, HD:HV], 1.0).then_inc(s_zero, 1)
                nc.vector.memset(ones_row[:, :], 1.0).then_inc(s_zero, 1)
                nc.vector.memset(ones_sq[:, :], 1.0).then_inc(s_zero, 1)
                ve.wait_ge(s_w, 112)
                for i in range(4):
                    nc.vector.tensor_copy(tri4[:, i, :], tri_f[:, :]).then_inc(s_tri, 1)
                nc.vector.tensor_copy(ident_bf[:, :], ident[:, :]).then_inc(s_tri, 1)

                def item(c, j):
                    n = 2 * c + j
                    ve.wait_ge(s_proj, n + 1)
                    for i in range(2):
                        last = nc.vector.tensor_tensor(
                            term[:, j, i, :].rearrange("p (b t) -> p b t", b=2),
                            ps_qk[j][i].rearrange("p (b t) -> p b t", b=2),
                            rot[:, i, :, :].to_broadcast([P, 2, T]), ALU.mult)
                    last.then_inc(s_rot, 1)
                    ve.wait_ge(s_rot, n + 1)
                    after(ve, s_r1, n - 1)
                    nc.vector.tensor_tensor(roped[:, j, :], term[:, j, 0, :], term[:, j, 1, :], ALU.add).then_inc(s_rope, 1)

                for j in range(2):
                    item(0, j)
                with ve.Fori(1, NCH) as c:
                    for j in range(2):
                        item(c, j)

            @block.scalar
            def _(act):
                act.wait_ge(s_zero, 1)

                def chunk(k, u):
                    c = 2 * k + u
                    for j in range(2):
                        n = 2 * c + j
                        act.wait_ge(s_rope, n + 1)
                        after(act, s_store[2 * u + j], 48 * k)
                        nc.scalar.activation(parts[:, 2 * u + j, 0, :], roped[:, j, :], ACT.Copy).then_inc(s_hi, 1)
                        act.wait_ge(s_r1, n + 1)
                        nc.scalar.activation(parts[:, 2 * u + j, 1, :], resid[:, j, :], ACT.Copy).then_inc(s_mid, 1)
                    act.wait_ge(s_vp, c + 1)
                    nc.scalar.activation(v_all[:, bass.ds(4 * c, 4), :, 0:HD],
                                         ps_v[:, :].rearrange("p (t h d) -> p t h d", t=4, h=H), ACT.Copy).then_inc(s_vc, 1)

                for u in range(2):
                    chunk(0, u)
                with act.Fori(1, NCH // 2) as k:
                    for u in range(2):
                        chunk(k, u)

            @block.gpsimd
            def _(pool):
                def item(k, u, j):
                    n = 4 * k + 2 * u + j
                    pool.wait_ge(s_hi, n + 1)
                    after(pool, s_mid, n - 1)
                    nc.gpsimd.tensor_tensor(resid[:, j, :], roped[:, j, :], parts[:, 2 * u + j, 0, :], ALU.subtract).then_inc(s_r1, 1)
                    pool.wait_ge(s_mid, n + 1)
                    nc.gpsimd.tensor_tensor(parts[:, 2 * u + j, 2, :], resid[:, j, :], parts[:, 2 * u + j, 1, :],
                                            ALU.subtract).then_inc(s_lo, 1)

                for u in range(2):
                    for j in range(2):
                        item(0, u, j)
                with pool.Fori(1, NCH // 2) as k:
                    for u in range(2):
                        for j in range(2):
                            item(k, u, j)


def attend(nc, tag, scratch, rows, v_all, xn, stats, consts, wo, bo, softmax):
    depth = 67 if softmax else rows
    scale = HD ** -0.5 if softmax else FD ** -0.5
    ident, ident_bf, ones_row = consts["ident"], consts["ident_bf"], consts["ones_row"]
    tri4, upper, ones_sq = consts["tri4"], consts["upper"], consts["ones_sq"]
    with ExitStack() as ctx:
        def sb(name, shape, dt=F32):
            return ctx.enter_context(nc.sbuf_tensor(f"{tag}_{name}", shape, dt))

        def ps(name, shape, dt=F32):
            return ctx.enter_context(nc.psum_tensor(f"{tag}_{name}", shape, dt))

        phase = ctx.enter_context(Semaphores(nc))

        def sem(name):
            return phase.take(f"{tag}_{name}")

        v_now = sb("v_now", [P, 2, 2, H, VW])
        qst = sb("qst", [P, 4, UH, T], BF16)
        kst = sb("kst", [P, 4, UH, T], BF16)
        prob = sb("prob", [P, 6, 1024])
        mx = sb("mx", [P, 2, UH, 2])
        mres = sb("mres", [P, 2, 16])
        mparts = sb("mparts", [P, 2, 3, 16], BF16)
        mT = sb("mT", [48, 2, P], BF16)
        outT = sb("outT", [P, 2, 2, T])
        vsum = sb("vsum", [P, 2, 2, H, HV])
        total = sb("total", [P, 2, 2, 4, HV])
        rden = sb("rden", [P, 2, 2, 4, 1])
        att = sb("att", [P, 2, H, HD])
        attT = sb("attT", [P, 2, P])
        bns = sb("bns", [P, NTILE, 6])
        den = sb("den", [P, 2, 2, 4, 1])
        ps_b = [ps(f"ps_b{i}", [P, 1024]) for i in range(2)]
        ps_a = [ps(f"ps_a{i}", [P, 512]) for i in range(2)]
        ps_pv = ps("ps_pv", [P, 512])
        ps_m = ps("ps_m", [P, 512])

        s_st = [sem(f"stack_loaded{i}") for i in range(4)]
        s_mrow = [sem(f"max_rows_loaded{i}") for i in range(2)]
        s_gate_pe, s_gate_pool = sem("gate_pe"), sem("gate_pool")
        s_af = sem("max_scores_ready")
        s_mx = sem("max_taken")
        s_mh = sem("max_hi_done")
        s_mr = sem("max_residual_done")
        s_mm = sem("max_mid_done")
        s_mp = sem("max_parts_done")
        s_mT = sem("max_transposed")
        s_mTc = sem("max_rows_copied")
        s_b = sem("scores_ready")
        s_e = sem("exp_done")
        s_k = sem("causal_masked")
        s_pv = sem("weighted_v_done")
        s_vn = sem("v_now_ready")
        s_vz = sem("v_now_cleared")
        s_ev = sem("out_rows_copied")
        s_tp = sem("out_transposed")
        s_vs = sem("v_summed")
        s_vsc = sem("v_sums_copied")
        s_tot = sem("v_sums_added")
        s_bias = sem("bias_added")
        s_rd = sem("denominator_inverted")
        s_on = sem("out_normalised")
        s_aT = sem("attention_transposed")
        s_aTc = sem("attention_rows_copied")
        s_o = sem("output_projected")
        s_y = sem("residual_added")
        s_bn = sem("row_stats_taken")
        s_ag = sem("row_stats_merged")
        s_clear = sem("stacks_cleared")
        s_zero = sem("stack_rows_set")
        s_de = sem("denominator_guarded")

        with nc.Block() as block:
            @block.sync
            def _(sp):
                sp.wait_ge(s_clear, 1)

                def load(c, s):
                    h0, t0 = UH * (s % 2), T * (s // 2)
                    for st, sc in ((qst, scratch[0]), (kst, scratch[1])):
                        src = sc[bass.ds(c, 1), :, :, :].rearrange("c s (d h) t -> (c s d) h t", h=H)[:, h0:h0 + UH, t0:t0 + T]
                        sp.dma_start(st[0:rows, s, :, :], src).then_inc(s_st[s], 16)

                def max_rows(k, s):
                    sp.wait_ge(s_mTc, 4 * k + s + 1)
                    for p in range(3):
                        dst = qst[64 + p:65 + p, s % 4, :, :].rearrange("p h (x q) -> p (h x) q", q=P)
                        sp.dma_start(dst, mT[16 * p:16 * p + 16, s % 2, :]).then_inc(s_mrow[s % 2], 16)

                for s in range(4):
                    load(0, s)
                if softmax:
                    max_rows(0, 0)

                def slot(k, s, next_max=softmax, more=True):
                    if next_max:
                        max_rows(k, s + 1)
                    if more:
                        sp.wait_ge(s_b, 12 * k + 3 * s + 3)
                        load(k + 1, s)

                with sp.Fori(0, NU // 4 - 1) as k:
                    for s in range(4):
                        slot(k, s)
                for s in range(4):
                    slot(NU // 4 - 1, s, next_max=softmax and s < 3, more=False)

            @block.tensor
            def _(pe):
                pe.wait_ge(s_clear, 1)

                def fill(k, s, f):
                    g = 24 * k + 6 * s + f
                    after(pe, s_mx, g - 1)
                    if f >= 4:
                        after(pe, s_on, 2 * (4 * k + s - 3) + f - 3)
                    s = s % 4
                    out = ps_a[f % 2]
                    if f < 4:
                        for i in range(2):
                            nc.tensor.matmul(out[:, 256 * i:256 * i + 256], qst[0:48, s, 2 * f + i, P:2 * P],
                                             kst[0:48, s, 2 * f + i, :], start=i == 0, stop=False, skip_group_check=True)
                        o = out[:, :].rearrange("p (h k) -> p h k", h=2)[:, :, P:2 * P]
                        nc.tensor.matmul(o, ident_bf[:, :], tri4[:, 0:2, :], start=False, stop=True,
                                         skip_group_check=True).then_inc(s_af, 1)
                    else:
                        for i in range(4):
                            h = 4 * (f - 4) + i
                            nc.tensor.matmul(out[:, P * i:P * i + P], qst[0:48, s, h, 0:P], kst[0:48, s, h, 0:P],
                                             start=i == 0, stop=False, skip_group_check=True)
                        nc.tensor.matmul(out[:, :], ident_bf[:, :], tri4[:, :, :], start=False, stop=True,
                                         skip_group_check=True).then_inc(s_af, 1)

                def stack_ready(k, s):
                    pe.wait_ge(s_st[s % 4], 32 * (k + s // 4) + 32)

                def scores(k, s, j):
                    r = 12 * k + 3 * s + j
                    after(pe, s_e, r - 1)
                    out = ps_b[(3 * s + j) % 2]
                    if j < 2:
                        for i in range(4):
                            last = nc.tensor.matmul(out[:, 256 * i:256 * i + 256], kst[0:depth, s, 4 * j + i, 0:P],
                                                    qst[0:depth, s, 4 * j + i, :], start=True, stop=True)
                    else:
                        for i in range(8):
                            last = nc.tensor.matmul(out[:, P * i:P * i + P], kst[0:depth, s, i, P:2 * P],
                                                    qst[0:depth, s, i, P:2 * P], start=True, stop=True)
                    last.then_inc(s_b, 1)

                def weighted(k, s, j):
                    r = 12 * k + 3 * s + j
                    u = 4 * k + s
                    pe.wait_ge(s_k, r + 1)
                    if j == 0:
                        after(pe, s_ev, u)
                        if s % 2 == 0:
                            pe.wait_ge(s_vn, 2 * k + s // 2 + 1)
                    h0, par = UH * (s % 2), s // 2
                    reg = prob[:, (3 * s + j) % 6, :]
                    for i in range(4 if j < 2 else UH):
                        part = slice(VW * (i % 4), VW * (i % 4) + VW)
                        if j < 2:
                            last = nc.tensor.matmul(ps_pv[part, T * j:T * j + T], v_now[:, par, 0, h0 + 4 * j + i, :],
                                                    reg[:, T * i:T * i + T], start=j == 0, stop=False, skip_group_check=True)
                        else:
                            q0 = T * (i // 4) + P
                            last = nc.tensor.matmul(ps_pv[part, q0:q0 + P], v_now[:, par, 1, h0 + i, :],
                                                    reg[:, P * i:P * i + P], start=False, stop=True, skip_group_check=True)
                    last.then_inc(s_pv, 1)

                def turn_out(k, s, fills):
                    w = 4 * k + s
                    after(pe, s_ev, w + 1)
                    for i in range(2):
                        if softmax:
                            pe.wait_ge(s_mx, 6 * (w + 3) + 3 + i if fills else 6 * NU)
                        after(pe, s_on, 2 * w + i - 1)
                        for q in range(2):
                            last = nc.tensor.transpose(ps_a[i][:, q * P:q * P + P], outT[:, s % 2, i, q * P:q * P + P], ident[:, :])
                        last.then_inc(s_tp, 1)

                def sum_v(b, par):
                    pe.wait_ge(s_vn, b + 1)
                    after(pe, s_y, b - 1)
                    vt = [v_now[:, par, t, :, 0:HV] for t in range(2)]
                    out = [ps_m[:, H * HV * t:H * HV * (t + 1)].rearrange("p (h d) -> p h d", h=H) for t in range(2)]
                    nc.tensor.matmul(out[0], upper[:, :], vt[0], start=True, stop=False, skip_group_check=True)
                    nc.tensor.matmul(out[1], ones_sq[:, :], vt[0], start=False, stop=False, skip_group_check=True)
                    nc.tensor.matmul(out[1], upper[:, :], vt[1], start=False, stop=True, skip_group_check=True).then_inc(s_vs, 1)

                def transpose_max(n, s):
                    settled(pe, s_mp, n + 1, s_gate_pe)
                    nc.tensor.transpose(ps_m[0:48, 0:64].bitcast(BF16), mparts[:, s % 2, :, :].rearrange("p a b -> p (a b)"),
                                        ident_bf[:, :]).then_inc(s_mT, 1)

                def transpose_att(b):
                    pe.wait_ge(s_on, 4 * b + 4)
                    for q in range(2):
                        last = nc.tensor.transpose(ps_m[:, q * P:q * P + P], att[:, q, :, :].rearrange("p h d -> p (h d)"),
                                                   ident[:, :])
                    last.then_inc(s_aT, 1)

                def project(b):
                    pe.wait_ge(s_aTc, b + 1)
                    for q in range(2):
                        o = ps_m[:, q * P:q * P + P]
                        last = nc.tensor.matmul(o, attT[:, q, :], wo[:, :], start=q == 0, stop=True, skip_group_check=True)
                    last.then_inc(s_o, 1)

                def slot(k, s, fills=softmax, tr=softmax, prev=True):
                    u = 4 * k + s
                    b = 2 * k + s // 2
                    if softmax:
                        pe.wait_ge(s_mrow[s % 2], 48 * (2 * k + s // 2) + 48)
                    else:
                        stack_ready(k, s)
                    prev1 = prev or s > 0
                    w = (k - 1, 3) if s == 0 else (k, s - 1)
                    for j in range(3):
                        scores(k, s, j)
                        if fills:
                            if j == 0:
                                stack_ready(k, s + 2)
                            fill(k, s + 2, 2 * j)
                            fill(k, s + 2, 2 * j + 1)
                        if j > 0:
                            weighted(k, s, j - 1)
                        elif prev1:
                            weighted(*w, 2)
                        if j == 0 and tr:
                            if s % 2 == 0:
                                after(pe, s_y, b - 1)
                            else:
                                after(pe, s_aTc, b)
                            transpose_max(u + 1, s + 1)
                        if j == 0 and not softmax and s % 2 == 0:
                            sum_v(b, s // 2)
                        if j == 1 and prev1:
                            turn_out(*w, fills)
                        if j == 1 and s % 2 == 1 and (prev or s > 1):
                            if softmax:
                                pe.wait_ge(s_mTc, u + (2 if tr else 1))
                            project(b - 1)
                        if j == 2 and s % 2 == 0 and (prev or s > 1):
                            if softmax:
                                pe.wait_ge(s_mTc, u + (2 if tr else 1))
                            else:
                                pe.wait_ge(s_vsc, b + 1)
                            transpose_att(b - 1)

                if softmax:
                    for s in range(2):
                        stack_ready(0, s)
                        for f in range(6):
                            fill(0, s, f)
                    transpose_max(0, 0)
                    pe.wait_ge(s_mTc, 1)
                for s in range(4):
                    slot(0, s, prev=False)
                with pe.Fori(1, NU // 4 - 1) as k:
                    for s in range(4):
                        slot(k, s)
                for s in range(4):
                    slot(NU // 4 - 1, s, fills=softmax and s < 2, tr=softmax and s < 3)
                weighted(NU // 4 - 1, 3, 2)
                turn_out(NU // 4 - 1, 3, False)
                pe.wait_ge(s_y, NB - 1)
                transpose_att(NB - 1)
                project(NB - 1)

            @block.vector
            def _(ve):
                if softmax:
                    nc.vector.memset(qst[32:64, :, :, :], 0.0).then_inc(s_zero, 1)
                    nc.vector.memset(kst[32:64, :, :, :], 0.0).then_inc(s_zero, 1)
                    nc.vector.memset(kst[64:96, :, :, :], -1.0).then_inc(s_zero, 1)
                    ve.wait_ge(s_zero, 3)
                nc.vector.memset(v_now[:, :, :, :, :], 0.0).then_inc(s_vz, 1)
                nc.vector.memset(den[:, :, :, :, :], 0.0).then_inc(s_clear, 1)
                if bo is not None:
                    nc.vector.tensor_tensor(xn[:, :, :], xn[:, :, :], bo[:, :, :].to_broadcast([P, NTILE, C]),
                                            ALU.add).then_inc(s_bias, 1)
                    ve.wait_ge(s_bias, 1)

                def reduce(k, s, f):
                    g = 24 * k + 6 * s + f
                    if f == 0:
                        after(ve, s_mp, 4 * k + s - 1)
                    ve.wait_ge(s_af, g + 1)
                    if f < 4:
                        nc.vector.reduce_max(mx[:, s % 2, 2 * f:2 * f + 2, 1:2],
                                             ps_a[f % 2][:, :].rearrange("p (h k) -> p h k", h=2), AX_X).then_inc(s_mx, 1)
                    else:
                        h = 4 * (f - 4)
                        nc.vector.reduce_max(mx[:, s % 2, h:h + 4, 0:1],
                                             ps_a[f % 2][:, :].rearrange("p (h k) -> p h k", h=4), AX_X).then_inc(s_mx, 1)

                def normalise(k, s):
                    w = 4 * k + s
                    for i in range(2):
                        src = ps_a[i][:, 0:2 * P].rearrange("p (q h d) -> p q h d", q=2, h=4)
                        h = UH * (s % 2) + 4 * i
                        ve.wait_ge(s_tp, 2 * w + i + 1)
                        if softmax:
                            out, d = src[:, :, :, 0:HD], src[:, :, :, HD:HV]
                        else:
                            tot = total[:, i, :, :, :]
                            out, d = tot[:, :, :, 0:HD], den[:, i, :, :, :]
                            if i == 0 and s % 2 == 0:
                                ve.wait_ge(s_vsc, 2 * k + s // 2 + 1)
                            for q in range(2):
                                last = nc.vector.tensor_tensor(tot[:, q, :, :], src[:, q, :, 0:HV], vsum[:, s // 2, q, h:h + 4, :], ALU.add)
                            last.then_inc(s_tot, 1)
                            ve.wait_ge(s_tot, 2 * w + i + 1)
                            nc.vector.tensor_scalar(d, tot[:, :, :, HD:HV], 2.0 * DEN_EPS, None, ALU.add).then_inc(s_de, 1)
                            ve.wait_ge(s_de, 2 * w + i + 1)
                        nc.vector.reciprocal(rden[:, i, :, :, :], d).then_inc(s_rd, 1)
                        ve.wait_ge(s_rd, 2 * w + i + 1)
                        if i == 0 and s % 2 == 0:
                            after(ve, s_aT, 2 * k + s // 2)
                        for q in range(2):
                            last = nc.vector.tensor_tensor(att[:, q, h:h + 4, :], out[:, q, :, :],
                                                           rden[:, i, q, :, :].to_broadcast([P, 4, HD]), ALU.mult)
                        last.then_inc(s_on, 1)

                def add_residual(b):
                    ve.wait_ge(s_o, b + 1)
                    y = xn[:, bass.ds(2 * b, 2), :]
                    nc.vector.tensor_tensor(y, ps_m[:, 0:2 * P].rearrange("p (t c) -> p t c", t=2), y, ALU.add).then_inc(s_y, 1)
                    ve.wait_ge(s_clear, 1)
                    ve.wait_ge(s_y, b + 1)
                    for q in range(2):
                        nc.vector.bn_stats(bns[:, bass.ds(2 * b + q, 1), :], xn[:, bass.ds(2 * b + q, 1), :]).then_inc(s_bn, 1)

                def slot(k, s, fills=softmax, prev=True):
                    b = 2 * k + s // 2
                    for j in range(3):
                        if fills:
                            reduce(k, s + 2, 2 * j)
                            reduce(k, s + 2, 2 * j + 1)
                        if j == 1 and (prev or s > 0):
                            normalise(*((k - 1, 3) if s == 0 else (k, s - 1)))
                        if j == 1 and s % 2 == 1 and (prev or s > 1):
                            add_residual(b - 1)

                if softmax:
                    for s in range(2):
                        for f in range(6):
                            reduce(0, s, f)
                for s in range(4):
                    slot(0, s, prev=False)
                with ve.Fori(1, NU // 4 - 1) as k:
                    for s in range(4):
                        slot(k, s)
                for s in range(4):
                    slot(NU // 4 - 1, s, fills=softmax and s < 2)
                normalise(NU // 4 - 1, 3)
                add_residual(NB - 1)
                merge_stats(nc, ve, stats, bns, s_bn, s_ag)

            @block.scalar
            def _(act):
                def copy_max(n, s):
                    act.wait_ge(s_mT, n + 1)
                    nc.scalar.activation(mT[:, s % 2, :], ps_m[0:48, 0:64].bitcast(BF16), ACT.Copy).then_inc(s_mTc, 1)

                def copy_att(b):
                    act.wait_ge(s_aT, b + 1)
                    after(act, s_o, b)
                    nc.scalar.activation(attT[:, :, :], ps_m[:, 0:2 * P].rearrange("p (t c) -> p t c", t=2),
                                         ACT.Copy).then_inc(s_aTc, 1)

                def copy_out(w, s):
                    act.wait_ge(s_pv, 3 * w + 3)
                    after(act, s_tp, 2 * w - 2)
                    nc.scalar.activation(outT[:, s % 2, :, :], ps_pv[:, :].rearrange("p (i q) -> p i q", i=2),
                                         ACT.Copy).then_inc(s_ev, 1)

                def copy_vsum(b, par):
                    act.wait_ge(s_vs, b + 1)
                    after(act, s_on, 4 * b - 4)
                    nc.scalar.activation(vsum[:, par, :, :, :].rearrange("p t h d -> p (t h d)"), ps_m[:, 0:2 * H * HV],
                                         ACT.Copy).then_inc(s_vsc, 1)

                def slot(k, s, tr=softmax, prev=True):
                    b = 2 * k + s // 2
                    for j in range(3):
                        r = 12 * k + 3 * s + j
                        act.wait_ge(s_b, r + 1)
                        after(act, s_pv, r - 5)
                        nc.scalar.activation(prob[:, (3 * s + j) % 6, :], ps_b[(3 * s + j) % 2][:, :],
                                             ACT.Exp if softmax else ACT.Square, scale=scale,
                                             bias=0.0 if softmax else 1.0).then_inc(s_e, 1)
                        if j == 0 and (prev or s > 0):
                            copy_out(4 * k + s - 1, (s - 1) % 4)
                        if j == 0 and tr:
                            copy_max(4 * k + s + 1, s + 1)
                        if j == 0 and not softmax and s % 2 == 0:
                            copy_vsum(b, s // 2)
                        if j == 2 and s % 2 == 0 and (prev or s > 1):
                            copy_att(b - 1)

                if softmax:
                    copy_max(0, 0)
                for s in range(4):
                    slot(0, s, prev=False)
                with act.Fori(1, NU // 4 - 1) as k:
                    for s in range(4):
                        slot(k, s)
                for s in range(4):
                    slot(NU // 4 - 1, s, tr=softmax and s < 3)
                copy_out(NU - 1, 3)
                copy_att(NB - 1)

            @block.gpsimd
            def _(pool):
                def mask(k, s, j):
                    r = 12 * k + 3 * s + j
                    settled(pool, s_e, r + 1, s_gate_pool)
                    reg = prob[:, (3 * s + j) % 6, :]
                    if j < 2:
                        blk, n = reg.rearrange("p (h q) -> p h q", h=4)[:, :, 0:P], 4
                    else:
                        blk, n = reg.rearrange("p (h q) -> p h q", h=8), 8
                    nc.gpsimd.affine_select(out=blk, in_=blk, compare_op=ALU.is_ge, fill=0.0, base=0,
                                            pattern=[[0, n], [1, P]], channel_multiplier=-1).then_inc(s_k, 1)

                def split_max(n, s):
                    after(pool, s_mT, n - 1)
                    settled(pool, s_mx, 6 * n + 6, s_gate_pool)
                    m = mx[:, s % 2, :, :].rearrange("p h q -> p (h q)")
                    nc.gpsimd.tensor_copy(mparts[:, s % 2, 0, :], m).then_inc(s_mh, 1)
                    pool.wait_ge(s_mh, n + 1)
                    nc.gpsimd.tensor_tensor(mres[:, s % 2, :], m, mparts[:, s % 2, 0, :], ALU.subtract).then_inc(s_mr, 1)
                    settled(pool, s_mr, n + 1, s_gate_pool)
                    nc.gpsimd.tensor_copy(mparts[:, s % 2, 1, :], mres[:, s % 2, :]).then_inc(s_mm, 1)
                    pool.wait_ge(s_mm, n + 1)
                    nc.gpsimd.tensor_tensor(mparts[:, s % 2, 2, :], mres[:, s % 2, :], mparts[:, s % 2, 1, :],
                                            ALU.subtract).then_inc(s_mp, 1)

                def take_v(b, par):
                    settled(pool, s_pv, 6 * b - 6, s_gate_pool)
                    nc.gpsimd.tensor_copy(v_now[:, par, :, :, 0:HV], v_all[:, bass.ds(2 * b, 2), :, :]).then_inc(s_vn, 1)

                def slot(k, s, fills=softmax, more=True):
                    for j in range(3):
                        mask(k, s, j)
                    if fills:
                        split_max(4 * k + s + 2, s)
                    if s % 2 == 1 and more:
                        take_v(2 * k + s // 2 + 1, (s // 2 + 1) % 2)

                pool.wait_ge(s_vz, 1)
                take_v(0, 0)
                if softmax:
                    for s in range(2):
                        split_max(s, s)
                for s in range(4):
                    slot(0, s)
                with pool.Fori(1, NU // 4 - 1) as k:
                    for s in range(4):
                        slot(k, s)
                for s in range(4):
                    slot(NU // 4 - 1, s, fills=softmax and s < 2, more=s < 3)


def expert_layer0(nc, io, xn, stats, norm, consts):
    ident, ident_bf = consts["ident"], consts["ident_bf"]
    with ExitStack() as ctx:
        def sb(name, shape, dt=F32):
            return ctx.enter_context(nc.sbuf_tensor(f"m0_{name}", shape, dt))

        def ps(name, shape, dt=F32):
            return ctx.enter_context(nc.psum_tensor(f"m0_{name}", shape, dt))

        phase = ctx.enter_context(Semaphores(nc))

        def sem(name):
            return phase.take(f"m0_{name}")

        wr = sb("wr", [P, E])
        wgu = sb("wgu", [P, E, 2, P])
        bgu = sb("bgu", [P, E, 2])
        bup = sb("bup", [P, E])
        wd = sb("wd", [P, E, C])
        wdh = sb("wdh", [P, E, C])
        bd = sb("bd", [32, C])
        bdp = sb("bdp", [32, 3, C], BF16)
        bdr = sb("bdr", [32, 2, C])
        sel_f = sb("sel_f", [32, E, P])
        sel = sb("sel", [32, E, P], BF16)
        desc = sb("desc", [P, 1, E])
        x1_tok = sb("x1_tok", [P, 2, 4, C])
        x1_now = sb("x1_now", [P, 2, CH])
        x1T = sb("x1T", [P, NTOK])
        ra = [sb(f"route{i}", [P, NTILE, E]) for i in range(6)]
        rs = [sb(f"pick{i}", [P, NTILE, 1]) for i in range(8)]
        wt = sb("wt", [P, NTILE, E])
        wtr = sb("wtr", [P, 1, NTILE, E])
        wtp = sb("wtp", [P, NTILE, 32], BF16)
        wt_now = sb("wt_now", [P, 2, 4, 32], BF16)
        wTp = sb("wTp", [32, 2, CH], BF16)
        gate = sb("gate", [P, 2, CH])
        up = sb("up", [P, 2, CH])
        upc = sb("upc", [P, 2, CH])
        th = sb("th", [P, 2, CH])
        prod = sb("prod", [P, 2, CH])
        glu = sb("glu", [P, 2, CH])
        act = sb("act", [P, 2, CH])
        bns = sb("bns", [P, NTILE, 6])
        ps_g = [ps(f"ps_g{i}", [P, CH]) for i in range(2)]
        ps_u = [ps(f"ps_u{i}", [P, CH]) for i in range(2)]
        ps_w = [ps(f"ps_w{i}", [P, CH]) for i in range(2)]
        ps_d = ps("ps_d", [P, CH])
        ps_r = ps("ps_r", [P, CH])
        logits = ps_r[:, 0:NTILE * E].rearrange("p (t e) -> p t e", t=NTILE)

        s_w = sem("weights_loaded")
        s_c = sem("constants_ready")
        s_x1 = sem("tile_normalised")
        s_xp = sem("x_transposed")
        s_xT = sem("x_rows_copied")
        s_xk = sem("x_rows_kept")
        s_xb = sem("x_kept")
        s_wn = sem("weights_staged")
        s_lg = sem("logits_ready")
        s_rt = sem("routing_step")
        s_ra = sem("routing_exp_done")
        s_wtp = sem("weights_transposed")
        s_wT = sem("weight_rows_copied")
        s_g = sem("gate_ready")
        s_u = sem("up_ready")
        s_bc = sem("weight_broadcast")
        s_gc = sem("gate_clipped")
        s_uc = sem("up_copied")
        s_ucl = sem("up_clipped")
        s_th = sem("tanh_done")
        s_pr = sem("product_done")
        s_gl = sem("glu_done")
        s_act = sem("activation_weighted")
        s_dn = sem("expert_summed")
        s_y = sem("residual_added")
        s_bn = sem("row_stats_taken")
        s_ag = sem("row_stats_merged")
        s_gate = sem("gate_pool")
        NR = 22
        NEXP = NCH * E

        with nc.Block() as block:
            @block.sync
            def _(sp):
                for dst, src in ((wr[:, :], io["wr"]), (sel_f[:, :, :], io["sel"]), (desc[:, 0, :], io["desc"]),
                                 (bgu[:, :, :], io["bgu"]), (wgu[:, :, :, :], io["wgu"]), (wd[:, :, :], io["wd0"]),
                                 (bd[:, :], io["bd0"])):
                    sp.dma_start(dst, src).then_inc(s_w, 16)
                sp.wait_ge(s_w, 112)

            @block.tensor
            def _(pe):
                pe.wait_ge(s_c, 9)

                def transpose_x(c, u):
                    after(pe, s_xk, c - 1)
                    pe.wait_ge(s_x1, 4 * c + 4)
                    for t in range(4):
                        last = nc.tensor.transpose(ps_w[u][:, t * P:(t + 1) * P], x1_tok[:, u, t, :], ident[:, :])
                    last.then_inc(s_xp, 1)

                def score(c, u):
                    pe.wait_ge(s_xT, c + 1)
                    for t in range(4):
                        last = nc.tensor.matmul(logits[:, bass.ds(4 * c + t, 1), :], x1_now[:, u, t * P:(t + 1) * P], wr[:, :],
                                                start=True, stop=True, skip_group_check=True)
                    last.then_inc(s_lg, 1)

                def transpose_w(c, u):
                    pe.wait_ge(s_wn, c + 1)
                    after(pe, s_wT, c)
                    for t in range(4):
                        last = nc.tensor.transpose(ps_r[0:32, 64 * t:64 * t + 64].bitcast(BF16), wt_now[:, u, t, :], ident_bf[:, :])
                    last.then_inc(s_wtp, 1)

                def expand(c, e):
                    n = E * c + e
                    after(pe, s_gc, n - 1)
                    nc.tensor.matmul(ps_g[e % 2][:, :], wgu[:, e, 0, :], x1T[:, bass.ds(c * CH, CH)], start=True, stop=True).then_inc(s_g, 1)
                    after(pe, s_uc, n - 1)
                    nc.tensor.matmul(ps_u[e % 2][:, :], wgu[:, e, 1, :], x1T[:, bass.ds(c * CH, CH)], start=True, stop=True).then_inc(s_u, 1)

                def broadcast(c, u, e):
                    n = E * c + e
                    after(pe, s_act, n - 1)
                    if e == 0:
                        pe.wait_ge(s_wT, c + 1)
                    nc.tensor.matmul(ps_w[e % 2][:, :], sel[0:32, e, :], wTp[0:32, u, :], start=True, stop=True).then_inc(s_bc, 1)

                def reduce(c, u, e):
                    n = E * c + e
                    if e == 0:
                        after(pe, s_y, c)
                        for t in range(4):
                            for part in range(3):
                                nc.tensor.matmul(ps_d[:, t * P:(t + 1) * P], wTp[0:32, u, t * P:(t + 1) * P], bdp[0:32, part, :],
                                                 start=t == 0 and part == 0, stop=False, skip_group_check=True)
                    pe.wait_ge(s_act, n + 1)
                    for t in range(4):
                        last = nc.tensor.matmul(ps_d[:, t * P:(t + 1) * P], act[:, e % 2, t * P:(t + 1) * P], wdh[:, e, :],
                                                start=False, stop=e == E - 1, skip_group_check=True)
                    last.then_inc(s_dn, 1)

                def chunk(c, u, prev=True, nxt=True):
                    for e in range(E):
                        expand(c, e)
                        broadcast(c, u, e)
                        if e >= 2:
                            reduce(c, u, e - 2)
                        elif prev:
                            reduce(c - 1, 1 - u, E + e - 2)
                        if nxt and e == 4:
                            transpose_w(c + 1, 1 - u)

                transpose_x(0, 0)
                transpose_x(1, 1)
                score(0, 0)
                score(1, 1)
                with pe.Fori(1, NCH // 2) as k:
                    for u in range(2):
                        transpose_x(2 * k + u, u)
                    for u in range(2):
                        score(2 * k + u, u)
                pe.wait_ge(s_xk, NCH)
                transpose_w(0, 0)
                chunk(0, 0, prev=False)
                chunk(1, 1)
                with pe.Fori(1, NCH // 2 - 1) as k:
                    for u in range(2):
                        chunk(2 * k + u, u)
                chunk(NCH - 2, 0)
                chunk(NCH - 1, 1, nxt=False)
                for e in (E - 2, E - 1):
                    reduce(NCH - 1, 1, e)

            @block.vector
            def _(ve):
                nc.vector.memset(wtp[:, :, :], 0.0).then_inc(s_c, 1)
                ve.wait_ge(s_w, 112)
                nc.vector.tensor_scalar(bup[:, :], bgu[:, :, 1], 1.0, None, ALU.add).then_inc(s_c, 1)
                nc.vector.tensor_copy(sel[:, :, :], sel_f[:, :, :]).then_inc(s_c, 1)
                nc.vector.tensor_scalar(wdh[:, :, :], wd[:, :, :], 0.5, None, ALU.mult).then_inc(s_c, 1)
                nc.vector.tensor_copy(bdp[:, 0, :], bd[:, :]).then_inc(s_c, 1)
                ve.wait_ge(s_c, 5)
                nc.vector.tensor_tensor(bdr[:, 0, :], bd[:, :], bdp[:, 0, :], ALU.subtract).then_inc(s_c, 1)
                ve.wait_ge(s_c, 6)
                nc.vector.tensor_copy(bdp[:, 1, :], bdr[:, 0, :]).then_inc(s_c, 1)
                ve.wait_ge(s_c, 7)
                nc.vector.tensor_tensor(bdr[:, 1, :], bdr[:, 0, :], bdp[:, 1, :], ALU.subtract).then_inc(s_c, 1)
                ve.wait_ge(s_c, 8)
                nc.vector.tensor_copy(bdp[:, 2, :], bdr[:, 1, :]).then_inc(s_c, 1)
                ve.wait_ge(s_c, 9)

                def normalise(c, u):
                    after(ve, s_xp, c - 1)
                    after(ve, s_xb, c - 1)
                    for t in range(4):
                        nc.vector.tensor_scalar(x1_tok[:, u, t, :], xn[:, bass.ds(4 * c + t, 1), :],
                                                stats[:, bass.ds(4 * c + t, 1), 0:1], norm.rstd[:, bass.ds(4 * c + t, 1)],
                                                ALU.subtract, ALU.mult).then_inc(s_x1, 1)
                    ve.wait_ge(s_x1, 4 * c + 4)
                    nc.vector.tensor_scalar(xn[:, bass.ds(4 * c, 4), :], x1_tok[:, u, :, :], 1.0, None, ALU.mult).then_inc(s_xb, 1)

                def route():
                    done = [0]

                    def step(ins):
                        done[0] += 1
                        ins.then_inc(s_rt, 1)
                        ve.wait_ge(s_rt, done[0])

                    def wide(x):
                        return x[:, :, :].to_broadcast([P, NTILE, E])

                    order = desc[:, :, :].to_broadcast([P, NTILE, E])
                    m1, k1, m2, k2, d, s, r, p2 = rs
                    ve.wait_ge(s_lg, NCH)
                    step(nc.vector.reduce_max(m1[:, :, :], logits, AX_X))
                    step(nc.vector.tensor_tensor(ra[0][:, :, :], logits, wide(m1), ALU.is_ge))
                    step(nc.vector.tensor_tensor(ra[0][:, :, :], ra[0][:, :, :], order, ALU.mult))
                    step(nc.vector.reduce_max(k1[:, :, :], ra[0][:, :, :], AX_X))
                    step(nc.vector.tensor_tensor(ra[1][:, :, :], ra[0][:, :, :], wide(k1), ALU.is_equal))
                    step(nc.vector.scalar_tensor_tensor(ra[2][:, :, :], ra[1][:, :, :], -BIG, logits, ALU.mult, ALU.add))
                    step(nc.vector.reduce_max(m2[:, :, :], ra[2][:, :, :], AX_X))
                    step(nc.vector.tensor_tensor(d[:, :, :], m2[:, :, :], m1[:, :, :], ALU.subtract))
                    step(nc.vector.tensor_tensor(ra[3][:, :, :], ra[2][:, :, :], wide(m2), ALU.is_ge))
                    step(nc.vector.tensor_tensor(ra[3][:, :, :], ra[3][:, :, :], order, ALU.mult))
                    step(nc.vector.reduce_max(k2[:, :, :], ra[3][:, :, :], AX_X))
                    step(nc.vector.tensor_tensor(ra[4][:, :, :], ra[3][:, :, :], wide(k2), ALU.is_equal))
                    ve.wait_ge(s_ra, 1)
                    step(nc.vector.tensor_scalar(s[:, :, :], d[:, :, :], 1.0, None, ALU.add))
                    step(nc.vector.reciprocal(r[:, :, :], s[:, :, :]))
                    step(nc.vector.tensor_tensor(p2[:, :, :], d[:, :, :], r[:, :, :], ALU.mult))
                    step(nc.vector.tensor_tensor(ra[5][:, :, :], ra[1][:, :, :], wide(r), ALU.mult))
                    step(nc.vector.tensor_tensor(ra[4][:, :, :], ra[4][:, :, :], wide(p2), ALU.mult))
                    step(nc.vector.tensor_tensor(wt[:, :, :], ra[5][:, :, :], ra[4][:, :, :], ALU.add))
                    step(nc.vector.tensor_copy(wtp[:, :, 0:E], wt[:, :, :]))
                    step(nc.vector.tensor_tensor(wtr[:, 0, :, :], wt[:, :, :], wtp[:, :, 0:E], ALU.subtract))
                    step(nc.vector.tensor_copy(wtp[:, :, E:2 * E], wtr[:, 0, :, :]))
                    step(nc.vector.tensor_tensor(wtp[:, :, 2 * E:3 * E], wtr[:, 0, :, :], wtp[:, :, E:2 * E], ALU.subtract))
                    assert done[0] == NR

                def clip(c, e):
                    n = E * c + e
                    ve.wait_ge(s_g, n + 1)
                    after(ve, s_gl, n - 1)
                    nc.vector.tensor_scalar(gate[:, e % 2, :], ps_g[e % 2][:, :], bgu[:, e, 0:1], LIMIT, ALU.add, ALU.min)\
                        .then_inc(s_gc, 1)
                    ve.wait_ge(s_uc, n + 1)
                    nc.vector.tensor_scalar(upc[:, e % 2, :], up[:, e % 2, :], LIMIT + 1.0, 1.0 - LIMIT, ALU.min, ALU.max)\
                        .then_inc(s_ucl, 1)

                def weigh(c, e):
                    n = E * c + e
                    ve.wait_ge(s_th, n + 1)
                    ve.wait_ge(s_pr, n + 1)
                    nc.vector.scalar_tensor_tensor(glu[:, e % 2, :], th[:, e % 2, :], 1.0, prod[:, e % 2, :],
                                                   ALU.add, ALU.mult).then_inc(s_gl, 1)
                    ve.wait_ge(s_gl, n + 1)
                    ve.wait_ge(s_bc, n + 1)
                    after(ve, s_dn, n - 1)
                    nc.vector.tensor_tensor(act[:, e % 2, :], ps_w[e % 2][:, :], glu[:, e % 2, :], ALU.mult).then_inc(s_act, 1)

                def add_residual(c):
                    ve.wait_ge(s_dn, E * c + E)
                    nc.vector.tensor_tensor(xn[:, bass.ds(4 * c, 4), :], ps_d[:, :].rearrange("p (t c) -> p t c", t=4),
                                            xn[:, bass.ds(4 * c, 4), :], ALU.add).then_inc(s_y, 1)
                    ve.wait_ge(s_c, 9)
                    ve.wait_ge(s_y, c + 1)
                    for t in range(4):
                        nc.vector.bn_stats(bns[:, bass.ds(4 * c + t, 1), :], xn[:, bass.ds(4 * c + t, 1), :]).then_inc(s_bn, 1)

                def chunk(c, prev=True):
                    for e in range(E):
                        clip(c, e)
                        if e >= 1:
                            weigh(c, e - 1)
                        elif prev:
                            weigh(c - 1, E - 1)
                        if e == 2 and prev:
                            add_residual(c - 1)

                for u in range(2):
                    normalise(u, u)
                with ve.Fori(1, NCH // 2) as k:
                    for u in range(2):
                        normalise(2 * k + u, u)
                ve.wait_ge(s_xb, NCH)
                route()
                chunk(0, prev=False)
                with ve.Fori(1, NCH) as c:
                    chunk(c)
                weigh(NCH - 1, E - 1)
                add_residual(NCH - 1)
                merge_stats(nc, ve, stats, bns, s_bn, s_ag)

            @block.scalar
            def _(act_e):
                act_e.wait_ge(s_c, 9)

                def copy_x(c, u):
                    act_e.wait_ge(s_xp, c + 1)
                    after(act_e, s_lg, c - 1)
                    nc.scalar.activation(x1_now[:, u, :], ps_w[u][:, :], ACT.Copy).then_inc(s_xT, 1)
                    nc.scalar.activation(x1T[:, bass.ds(c * CH, CH)], ps_w[u][:, :], ACT.Copy).then_inc(s_xk, 1)

                def copy_w(c, u):
                    act_e.wait_ge(s_wtp, c + 1)
                    nc.scalar.activation(wTp[:, u, :], ps_r[0:32, 0:CH // 2].bitcast(BF16), ACT.Copy).then_inc(s_wT, 1)

                def expert(c, e):
                    n = E * c + e
                    act_e.wait_ge(s_u, n + 1)
                    after(act_e, s_ucl, n - 1)
                    nc.scalar.activation(up[:, e % 2, :], ps_u[e % 2][:, :], ACT.Identity, bias=bup[:, e:e + 1]).then_inc(s_uc, 1)
                    act_e.wait_ge(s_gc, n + 1)
                    after(act_e, s_gl, n - 1)
                    nc.scalar.activation(th[:, e % 2, :], gate[:, e % 2, :], ACT.Tanh, scale=ALPHA / 2).then_inc(s_th, 1)

                def chunk(c, u, nxt=True):
                    for e in range(E):
                        expert(c, e)
                        if nxt and e == 4:
                            copy_w(c + 1, 1 - u)

                for u in range(2):
                    copy_x(u, u)
                with act_e.Fori(1, NCH // 2) as k:
                    for u in range(2):
                        copy_x(2 * k + u, u)
                act_e.wait_ge(s_rt, 8)
                nc.scalar.activation(rs[4][:, :, :], rs[4][:, :, :], ACT.Exp).then_inc(s_ra, 1)
                copy_w(0, 0)
                chunk(0, 0)
                chunk(1, 1)
                with act_e.Fori(1, NCH // 2 - 1) as k:
                    for u in range(2):
                        chunk(2 * k + u, u)
                chunk(NCH - 2, 0)
                chunk(NCH - 1, 1, nxt=False)

            @block.gpsimd
            def _(pool):
                def product(n, e):
                    after(pool, s_gl, n - 1)
                    pool.wait_ge(s_ucl, n + 1)
                    nc.gpsimd.tensor_tensor(prod[:, e % 2, :], upc[:, e % 2, :], gate[:, e % 2, :], ALU.mult).then_inc(s_pr, 1)

                def stage_w(c, u):
                    settled(pool, s_wtp, c - 1, s_gate)
                    nc.gpsimd.tensor_copy(wt_now[:, u, :, :], wtp[:, bass.ds(4 * c, 4), :]).then_inc(s_wn, 1)

                def chunk(c, u, nxt=True):
                    for e in range(E):
                        product(E * c + e, e)
                        if nxt and e == 2:
                            stage_w(c + 1, 1 - u)

                pool.wait_ge(s_rt, NR)
                stage_w(0, 0)
                chunk(0, 0)
                chunk(1, 1)
                with pool.Fori(1, NCH // 2 - 1) as k:
                    for u in range(2):
                        chunk(2 * k + u, u)
                chunk(NCH - 2, 0)
                chunk(NCH - 1, 1, nxt=False)


def layer1_attention(nc, io, xn, stats, norm, consts):
    scratch = [nc.dram_tensor(f"scratch1_{n}", [NCH, NSLOT, 2 * P, CH], BF16, kind="Internal").ap() for n in "qk"]
    with ExitStack() as keep:
        v_all = keep.enter_context(nc.sbuf_tensor("v_all1", [P, NTILE, H, HV], F32))
        wo = keep.enter_context(nc.sbuf_tensor("wo1", [P, P], F32))
        project_layer1(nc, io, scratch, v_all, wo, xn, stats, norm, consts)
        attend(nc, "a1", scratch, 6 * FD, v_all, xn, stats, consts, wo, None, softmax=False)


def project_layer1(nc, io, scratch, v_all, wo, xn, stats, norm, consts):
    ident = consts["ident"]
    with ExitStack() as ctx:
        def sb(name, shape, dt=F32):
            return ctx.enter_context(nc.sbuf_tensor(f"p1_{name}", shape, dt))

        def ps(name, shape, dt=F32):
            return ctx.enter_context(nc.psum_tensor(f"p1_{name}", shape, dt))

        phase = ctx.enter_context(Semaphores(nc))

        def sem(name):
            return phase.take(f"p1_{name}")

        wqk = sb("wqk", [P, 4, P])
        wv = sb("wv", [P, P])
        x2 = sb("x2", [P, 2, 4, C])
        x2T = sb("x2T", [P, 2, CH])
        resid = sb("resid", [P, 2, CH])
        parts = sb("parts", [P, 8, 3, CH], BF16)
        ps_qk = [ps(f"ps_qk{i}", [P, CH]) for i in range(4)]
        ps_x = [ps(f"ps_x{i}", [P, CH]) for i in range(2)]
        ps_v = ps("ps_v", [P, CH])

        s_w = sem("weights_loaded")
        s_ones = sem("ones_set")
        s_x2 = sem("tile_normalised")
        s_back = sem("x2_kept")
        s_xp = sem("x_transposed")
        s_xT = sem("x_rows_copied")
        s_proj = sem("qk_projected")
        s_hi = sem("hi_done")
        s_r1 = sem("residual_done")
        s_mid = sem("mid_done")
        s_lo = sem("lo_done")
        s_store = [sem(f"parts_stored{i}") for i in range(8)]
        s_vp = sem("v_projected")
        s_vc = sem("v_copied")
        s_gate = sem("gate_pool")

        with nc.Block() as block:
            @block.sync
            def _(sp):
                for dst, src in ((wqk[:, :, :], io["wqk1"]), (wv[:, :], io["wv1"]), (wo[:, :], io["wo1"])):
                    sp.dma_start(dst, src).then_inc(s_w, 16)

                def store(c, u):
                    for i in range(4):
                        sp.wait_ge(s_lo, 4 * c + i + 1)
                        src = parts[:, 4 * u + i, :, :]
                        half = P * (i % 2)
                        dst = scratch[i // 2][bass.ds(c, 1), :, half:half + P, :].rearrange("c s p t -> p (c s) t")
                        for s0, m, part in SLOT_RUNS:
                            if i < 2:
                                sp.dma_start(dst[:, s0:s0 + m, :], src[:, 0:m, :]).then_inc(s_store[4 * u + i], 16)
                            else:
                                sp.dma_start(dst[:, s0:s0 + m, :],
                                             src[:, part:part + 1, :].to_broadcast([P, m, CH])).then_inc(s_store[4 * u + i], 16)

                with sp.Fori(0, NCH // 2) as k:
                    for u in range(2):
                        store(2 * k + u, u)
                for n in range(8):
                    sp.wait_ge(s_store[n], 48 * (NCH // 2))

            @block.tensor
            def _(pe):
                pe.wait_ge(s_w, 48)

                def chunk(c, u):
                    pe.wait_ge(s_x2, 4 * c + 4)
                    after(pe, s_xT, c - 1)
                    for t in range(4):
                        last = nc.tensor.transpose(ps_x[u][:, t * P:(t + 1) * P], x2[:, u, t, :], ident[:, :])
                    last.then_inc(s_xp, 1)
                    pe.wait_ge(s_xT, c + 1)
                    for i in range(4):
                        after(pe, s_r1, 4 * c + i - 3)
                        nc.tensor.matmul(ps_qk[i][:, :], wqk[:, i, :], x2T[:, u, :], start=True, stop=True).then_inc(s_proj, 1)
                    after(pe, s_vc, c)
                    for t in range(4):
                        last = nc.tensor.matmul(ps_v[:, t * P:(t + 1) * P], x2T[:, u, t * P:(t + 1) * P], wv[:, :],
                                                start=True, stop=True)
                    last.then_inc(s_vp, 1)

                for u in range(2):
                    chunk(u, u)
                with pe.Fori(1, NCH // 2) as k:
                    for u in range(2):
                        chunk(2 * k + u, u)

            @block.vector
            def _(ve):
                nc.vector.memset(v_all[:, :, :, HD:HV], 1.0).then_inc(s_ones, 1)

                def normalise(c, u):
                    after(ve, s_xp, c - 1)
                    after(ve, s_back, c - 1)
                    for t in range(4):
                        nc.vector.tensor_scalar(x2[:, u, t, :], xn[:, bass.ds(4 * c + t, 1), :],
                                                stats[:, bass.ds(4 * c + t, 1), 0:1], norm.rstd[:, bass.ds(4 * c + t, 1)],
                                                ALU.subtract, ALU.mult).then_inc(s_x2, 1)

                def residuals(c, u):
                    for i in range(4):
                        n = 4 * c + i
                        ve.wait_ge(s_hi, n + 1)
                        after(ve, s_lo, n - 1)
                        nc.vector.tensor_tensor(resid[:, i % 2, :], ps_qk[i][:, :], parts[:, 4 * u + i, 0, :],
                                                ALU.subtract).then_inc(s_r1, 1)

                normalise(0, 0)
                normalise(1, 1)
                residuals(0, 0)
                with ve.Fori(1, NCH // 2) as k:
                    for u in range(2):
                        normalise(2 * k + u, u)
                        residuals(2 * k + u - 1, 1 - u)
                residuals(NCH - 1, 1)

            @block.scalar
            def _(act):
                act.wait_ge(s_ones, 1)

                def copy_x(c, u):
                    act.wait_ge(s_xp, c + 1)
                    after(act, s_vp, c - 1)
                    nc.scalar.activation(x2T[:, u, :], ps_x[u][:, :], ACT.Copy).then_inc(s_xT, 1)

                def chunk(c, k, u):
                    copy_x(c, u)
                    for i in range(4):
                        n = 4 * c + i
                        act.wait_ge(s_proj, n + 1)
                        after(act, s_store[4 * u + i], 48 * k)
                        nc.scalar.activation(parts[:, 4 * u + i, 0, :], ps_qk[i][:, :], ACT.Copy).then_inc(s_hi, 1)
                        act.wait_ge(s_r1, n + 1)
                        nc.scalar.activation(parts[:, 4 * u + i, 1, :], resid[:, i % 2, :], ACT.Copy).then_inc(s_mid, 1)
                    act.wait_ge(s_vp, c + 1)
                    nc.scalar.activation(v_all[:, bass.ds(4 * c, 4), :, 0:HD],
                                         ps_v[:, :].rearrange("p (t h d) -> p t h d", t=4, h=H), ACT.Copy).then_inc(s_vc, 1)

                for u in range(2):
                    chunk(u, 0, u)
                with act.Fori(1, NCH // 2) as k:
                    for u in range(2):
                        chunk(2 * k + u, k, u)

            @block.gpsimd
            def _(pool):
                def chunk(c, u):
                    settled(pool, s_x2, 4 * c + 4, s_gate)
                    nc.gpsimd.tensor_copy(xn[:, bass.ds(4 * c, 4), :], x2[:, u, :, :]).then_inc(s_back, 1)
                    for i in range(4):
                        pool.wait_ge(s_mid, 4 * c + i + 1)
                        nc.gpsimd.tensor_tensor(parts[:, 4 * u + i, 2, :], resid[:, i % 2, :], parts[:, 4 * u + i, 1, :],
                                                ALU.subtract).then_inc(s_lo, 1)

                for u in range(2):
                    chunk(u, u)
                with pool.Fori(1, NCH // 2) as k:
                    for u in range(2):
                        chunk(2 * k + u, u)


def score_tokens(nc, io, xn, stats, stats_y, norm, gate_act, consts):
    ident = consts["ident"]
    with ExitStack() as ctx:
        def sb(name, shape, dt=F32):
            return ctx.enter_context(nc.sbuf_tensor(f"g_{name}", shape, dt))

        phase = ctx.enter_context(Semaphores(nc))

        def sem(name):
            return phase.take(f"g_{name}")

        wg = sb("wg", [P, E])
        x3 = sb("x3", [P, 2, 4, C])
        x3T = sb("x3T", [P, 2, CH])
        bns = sb("bns", [P, NTILE, 6])
        ps_x = [ctx.enter_context(nc.psum_tensor(f"g_ps_x{i}", [P, CH], F32)) for i in range(2)]
        ps_s = [ctx.enter_context(nc.psum_tensor(f"g_ps_s{i}", [P, CH], F32)) for i in range(2)]
        s_w = sem("weights_loaded")
        s_x3 = sem("tile_normalised")
        s_back = sem("x3_kept")
        s_xp = sem("x_transposed")
        s_xT = sem("x_rows_copied")
        s_sc = sem("scores_ready")
        s_th = sem("tanh_done")
        s_bn = sem("row_stats_taken")
        s_ag = sem("row_stats_merged")
        s_gate = sem("gate_pool")
        with nc.Block() as block:
            @block.sync
            def _(sp):
                sp.dma_start(wg[:, :], io["wg1"]).then_inc(s_w, 16)

            @block.tensor
            def _(pe):
                pe.wait_ge(s_w, 16)

                def chunk(c, u):
                    pe.wait_ge(s_x3, 4 * c + 4)
                    after(pe, s_xT, c - 1)
                    for t in range(4):
                        last = nc.tensor.transpose(ps_x[u][:, t * P:(t + 1) * P], x3[:, u, t, :], ident[:, :])
                    last.then_inc(s_xp, 1)

                def score(c, u):
                    pe.wait_ge(s_xT, c + 1)
                    after(pe, s_th, c - 1)
                    for t in range(4):
                        last = nc.tensor.matmul(ps_s[u][:, t * E:(t + 1) * E], x3T[:, u, t * P:(t + 1) * P], wg[:, :],
                                                start=True, stop=True)
                    last.then_inc(s_sc, 1)

                chunk(0, 0)
                chunk(1, 1)
                score(0, 0)
                with pe.Fori(1, NCH // 2) as k:
                    for u in range(2):
                        chunk(2 * k + u, u)
                        score(2 * k + u - 1, 1 - u)
                score(NCH - 1, 1)

            @block.vector
            def _(ve):
                ve.wait_ge(s_w, 16)

                def chunk(c, u):
                    after(ve, s_xp, c - 1)
                    after(ve, s_back, c - 1)
                    for t in range(4):
                        nc.vector.tensor_scalar(x3[:, u, t, :], xn[:, bass.ds(4 * c + t, 1), :],
                                                stats[:, bass.ds(4 * c + t, 1), 0:1], norm.rstd[:, bass.ds(4 * c + t, 1)],
                                                ALU.subtract, ALU.mult).then_inc(s_x3, 1)
                    ve.wait_ge(s_w, 16)
                    ve.wait_ge(s_x3, 4 * c + 4)
                    for t in range(4):
                        nc.vector.bn_stats(bns[:, bass.ds(4 * c + t, 1), :], x3[:, u, t, :]).then_inc(s_bn, 1)

                for u in range(2):
                    chunk(u, u)
                with ve.Fori(1, NCH // 2) as k:
                    for u in range(2):
                        chunk(2 * k + u, u)
                merge_stats(nc, ve, stats_y, bns, s_bn, s_ag)

            @block.scalar
            def _(act):
                def chunk(c, u):
                    act.wait_ge(s_xp, c + 1)
                    after(act, s_sc, c - 1)
                    nc.scalar.activation(x3T[:, u, :], ps_x[u][:, :], ACT.Copy).then_inc(s_xT, 1)
                    act.wait_ge(s_sc, c + 1)
                    nc.scalar.activation(gate_act[:, :, bass.ds(4 * c, 4)],
                                         ps_s[u][:, 0:4 * E].rearrange("p (t e) -> p e t", t=4), ACT.Tanh).then_inc(s_th, 1)

                chunk(0, 0)
                chunk(1, 1)
                with act.Fori(1, NCH // 2) as k:
                    for u in range(2):
                        chunk(2 * k + u, u)

            @block.gpsimd
            def _(pool):
                def chunk(c, u):
                    settled(pool, s_x3, 4 * c + 4, s_gate)
                    nc.gpsimd.tensor_copy(xn[:, bass.ds(4 * c, 4), :], x3[:, u, :, :]).then_inc(s_back, 1)

                for u in range(2):
                    chunk(u, u)
                with pool.Fori(1, NCH // 2) as k:
                    for u in range(2):
                        chunk(2 * k + u, u)


def choose_tokens(nc, io, xn, stats_y, norm_y, gate_act, picked, kept, w1, sum_d, norm_d, consts):
    ident, upper, ones_sq = consts["ident"], consts["upper"], consts["ones_sq"]
    NT, NV = NTILE, 5
    SHARE = 24
    with ExitStack() as ctx:
        def sb(name, shape, dt=F32):
            return ctx.enter_context(nc.sbuf_tensor(f"c_{name}", shape, dt))

        phase = ctx.enter_context(Semaphores(nc))

        def sem(name):
            return phase.take(f"c_{name}")

        score = sb("score", [P, E, NT])
        hit = sb("hit", [P, 3, E, NT])
        more = sb("more", [P, E, NT])
        equal = sb("equal", [P, E, NT])
        sel = sb("sel", [P, E, NT])
        pos = sb("pos", [P, E, NT])
        total = sb("total", [P, E, NT])
        running = sb("running", [P, E, NT])
        quarter = sb("quarter", [P, E, NT])
        in_q = [sb(f"in_q{i}", [P, E, NT]) for i in range(4)]
        wpart = [sb(f"wpart{i}", [P, E, NT], BF16) for i in range(3)]
        wres = sb("wres", [P, E, NT])
        vals = sb("vals", [P, E, NT, NV, 4], BF16)
        onehot = sb("onehot", [P, 2, NT, P], BF16)
        far = sb("far", [P, NT - SHARE, P])
        iota = sb("iota", [P, 1, P])
        tile0 = sb("tile0", [P, 1, NT])
        not0 = sb("not0", [P, E * NT])
        row = sb("row", [P, 1])
        strict = sb("strict", [P, P])
        count, cand, held = [sb(n, [P, 3, E, 1]) for n in ("count", "cand", "held")]
        ahead = sb("ahead", [P, 3, 1])
        thr, best, need = [sb(n, [P, E, 1]) for n in ("thr", "best", "need")]
        found = sb("found", [P, E, NV, 4])
        yn = sb("yn", [P, NT, C])
        twice = sb("twice", [P, NT, C])
        nought = sb("nought", [P, 1, C])
        ps_c = ctx.enter_context(nc.psum_tensor("c_ps_c", [P, 512], F32))
        ps_p = ctx.enter_context(nc.psum_tensor("c_ps_p", [P, 512], F32))
        ps_t = ctx.enter_context(nc.psum_tensor("c_ps_t", [P, 512], F32))
        ps_f = ctx.enter_context(nc.psum_tensor("c_ps_f", [P, 512], F32))
        tot = ps_c[:, 0:3 * E].rearrange("p (j e o) -> p j e o", j=3, o=1)
        before = ps_p[:, 0:E * NT].rearrange("p (e t) -> p e t", e=E)
        tiles = ps_t[:, 0:E * NT].rearrange("p (e t) -> p e t", e=E)
        hits = ps_f[:, 0:E * NV * 4].rearrange("p (e v a) -> p e v a", e=E, v=NV)

        s_w = sem("constants_loaded")
        s_st = sem("vector_step")
        s_cnt = sem("rows_counted")
        s_tot = sem("tokens_counted")
        s_src = sem("flags_ready")
        s_pre = sem("prefixes_ready")
        s_oh = sem("onehot_ready")
        s_ohp = sem("onehot_rest_ready")
        s_pos = sem("positions_ready")
        s_far = sem("distances_ready")
        s_used = sem("onehot_used")
        s_y = sem("tile_normalised")
        s_two = sem("x3_doubled")
        s_w1 = sem("expert_weights_loaded")
        s_d = sem("rows_stored")

        def flat(x):
            return x[:, :, :].rearrange("p e t -> p (e t)")

        with nc.Block() as block:
            @block.sync
            def _(sp):
                for dst, src in ((iota[:, 0, :], io["iota"]), (tile0[:, 0, :], io["tile0"]), (not0[:, :], io["not0"]),
                                 (row[:, :], io["row"])):
                    sp.dma_start(dst, src).then_inc(s_w, 16)
                for e in range(2):
                    sp.dma_start(w1[:, e, :], io["w1"][e, :, :]).then_inc(s_w1, 16)
                sp.wait_ge(s_two, 2)
                sp.dma_start(sum_d[1].rearrange("(t p) c -> p t c", p=P), nought[:, :, :].to_broadcast([P, NT, C])).then_inc(s_d, 16)
                sp.dma_start(sum_d[0].rearrange("(t p) c -> p t c", p=P), twice[:, :, :]).then_inc(s_d, 16)
                sp.wait_ge(s_y, NT)
                sp.dma_start(norm_d.rearrange("(t p) c -> p t c", p=P), yn[:, :, :]).then_inc(s_d, 16)
                sp.wait_ge(s_d, 48)
                sp.wait_ge(s_w1, 32)

            @block.scalar
            def _(act):
                nc.scalar.activation(nought[:, 0, :], xn[:, 0, :], ACT.Copy, scale=0.0).then_inc(s_two, 1)
                nc.scalar.activation(twice[:, :, :], xn[:, :, :], ACT.Copy, scale=2.0).then_inc(s_two, 1)
                act.wait_ge(s_pos, 1)
                for e in range(E):
                    after(act, s_ohp, e)
                    for t in range(SHARE, NT):
                        last = nc.scalar.activation(far[:, t - SHARE, :], iota[:, 0, :], ACT.Square, scale=-1.0,
                                                    bias=pos[:, e, t:t + 1])
                    last.then_inc(s_far, 1)
                    act.wait_ge(s_far, e + 1)
                    after(act, s_used, e - 1)
                    nc.scalar.activation(onehot[:, e % 2, SHARE:NT, :], far[:, :, :], ACT.Relu, scale=-1.0,
                                         bias=1.0).then_inc(s_ohp, 1)

            @block.gpsimd
            def _(pool):
                for t in range(NT):
                    nc.gpsimd.tensor_scalar(yn[:, t, :], xn[:, t, :], stats_y[:, t, 0:1], norm_y.rstd[:, t:t + 1],
                                            ALU.subtract, ALU.mult).then_inc(s_y, 1)

            @block.tensor
            def _(pe):
                def total_counts(i):
                    pe.wait_ge(s_cnt, i + 1)
                    nc.tensor.matmul(ps_c[:, 0:3 * E], ones_sq[:, :], count[:, :, :, :].rearrange("p j e o -> p (j e o)"),
                                     start=True, stop=True).then_inc(s_tot, 1)

                with pe.Fori(0, ROUNDS) as i:
                    total_counts(i)
                total_counts(ROUNDS)
                for n, src in enumerate((equal, sel)):
                    pe.wait_ge(s_src, n + 1)
                    nc.tensor.matmul(ps_t[:, 0:E * NT], ones_sq[:, :], flat(src), start=True, stop=True).then_inc(s_pre, 1)
                    nc.tensor.matmul(ps_p[:, 0:E * NT], strict[:, :], flat(src), start=True, stop=True).then_inc(s_pre, 1)
                for e in range(E):
                    pe.wait_ge(s_oh, e + 1)
                    for t in range(NT):
                        if t == SHARE:
                            pe.wait_ge(s_ohp, e + 1)
                        last = nc.tensor.matmul(hits[:, e, :, :], onehot[:, e % 2, t, :], vals[:, e, t, :, :],
                                                start=e == 0 and t == 0, stop=t == NT - 1, skip_group_check=True)
                    last.then_inc(s_used, 1)

            @block.vector
            def _(ve):
                done = [0]

                def step(ins):
                    done[0] += 1
                    ins.then_inc(s_st, 1)
                    ve.wait_ge(s_st, done[0])

                def wide(x):
                    return x[:, :, :].to_broadcast([P, E, NT])


                v = nc.vector
                ve.wait_ge(s_w, 64)
                step(v.tensor_scalar(score[:, :, :], gate_act[:, :, :], 1.0, 0.5, ALU.add, ALU.mult))
                step(v.memset(thr[:, :, :], 0.0))
                for j in range(3):
                    step(v.memset(ahead[:, j, :], 0.5 * (j + 1)))
                step(v.tensor_tensor(strict[:, :], upper[:, :], ident[:, :], ALU.subtract))
                base0, per = done[0], 6
                with ve.Fori(0, ROUNDS) as i:
                    n = [0]

                    def bit(ins):
                        n[0] += 1
                        ins.then_inc(s_st, 1)
                        ve.wait_ge(s_st, per * i + (base0 + n[0]))

                    for j in range(3):
                        last = v.tensor_scalar(cand[:, j, :, :], thr[:, :, :], ahead[:, j, :], None, ALU.add)
                    bit(last)
                    for j in range(3):
                        last = v.tensor_tensor(hit[:, j, :, :], score[:, :, :], wide(cand[:, j, :, :]), ALU.is_ge)
                    bit(last)
                    v.reduce_sum(count[:, :, :, :].rearrange("p j e o -> p (j e) o"),
                                 hit[:, :, :, :].rearrange("p j e t -> p (j e) t"), AX_X).then_inc(s_cnt, 1)
                    bit(v.tensor_scalar(ahead[:, :, :], ahead[:, :, :], 0.25, None, ALU.mult))
                    ve.wait_ge(s_tot, i + 1)
                    bit(v.scalar_tensor_tensor(held[:, :, :, :], tot, CAP - 0.5, cand[:, :, :, :], ALU.is_ge, ALU.mult))
                    bit(v.reduce_max(best[:, :, :], held[:, :, :, :].rearrange("p j e o -> p e (j o)"), AX_X))
                    bit(v.tensor_tensor(thr[:, :, :], thr[:, :, :], best[:, :, :], ALU.max))
                    assert n[0] == per
                done[0] = base0 + per * ROUNDS

                step(v.tensor_tensor(more[:, :, :], score[:, :, :], wide(thr), ALU.is_gt))
                v.reduce_sum(count[:, 0, :, :], more[:, :, :], AX_X).then_inc(s_cnt, 1)
                v.tensor_tensor(equal[:, :, :], score[:, :, :], wide(thr), ALU.is_equal).then_inc(s_src, 1)
                ve.wait_ge(s_tot, ROUNDS + 1)
                step(v.tensor_scalar(need[:, :, :], tot[:, 0, :, :], -1.0, float(CAP), ALU.mult, ALU.add))

                def prefix(n):
                    ve.wait_ge(s_pre, 2 * n + 1)
                    step(v.tensor_copy(total[:, :, :], tiles))
                    step(v.tensor_tensor_scan(flat(running), not0[:, :], flat(total), 0.0, ALU.mult, ALU.add))
                    step(v.tensor_tensor(running[:, :, :], running[:, :, :], total[:, :, :], ALU.subtract))
                    ve.wait_ge(s_pre, 2 * n + 2)
                    step(v.tensor_tensor(pos[:, :, :], before, running[:, :, :], ALU.add))

                prefix(0)
                step(v.tensor_tensor(sel[:, :, :], pos[:, :, :], wide(need), ALU.is_lt))
                step(v.tensor_tensor(sel[:, :, :], sel[:, :, :], equal[:, :, :], ALU.mult))
                v.tensor_tensor(sel[:, :, :], sel[:, :, :], more[:, :, :], ALU.add).then_inc(s_src, 1)
                step(v.tensor_copy(wpart[0][:, :, :], score[:, :, :]))
                step(v.tensor_tensor(wres[:, :, :], score[:, :, :], wpart[0][:, :, :], ALU.subtract))
                step(v.tensor_copy(wpart[1][:, :, :], wres[:, :, :]))
                step(v.tensor_tensor(wpart[2][:, :, :], wres[:, :, :], wpart[1][:, :, :], ALU.subtract))
                prefix(1)
                step(v.tensor_scalar(quarter[:, :, :], pos[:, :, :], float(P), None, ALU.is_ge))
                for q in (2, 3):
                    step(v.scalar_tensor_tensor(quarter[:, :, :], pos[:, :, :], float(q * P), quarter[:, :, :], ALU.is_ge, ALU.add))
                for q in range(4):
                    step(v.scalar_tensor_tensor(in_q[q][:, :, :], quarter[:, :, :], float(q), sel[:, :, :], ALU.is_equal, ALU.mult))
                step(v.scalar_tensor_tensor(pos[:, :, :], quarter[:, :, :], -float(P), pos[:, :, :], ALU.mult, ALU.add))
                for q in range(4):
                    step(v.tensor_tensor(vals[:, :, :, 0, q], in_q[q][:, :, :], tile0[:, :, :].to_broadcast([P, E, NT]), ALU.mult))
                    step(v.tensor_scalar(vals[:, :, :, 1, q], in_q[q][:, :, :], row[:, 0:1], None, ALU.mult))
                    for i in range(3):
                        step(v.tensor_tensor(vals[:, :, :, 2 + i, q], in_q[q][:, :, :], wpart[i][:, :, :], ALU.mult))
                nc.vector.memset(thr[:, :, :], 0.0).then_inc(s_pos, 1)
                for e in range(E):
                    after(ve, s_used, e - 1)
                    v.tensor_tensor(onehot[:, e % 2, 0:SHARE, :], iota[:, :, :].to_broadcast([P, SHARE, P]),
                                    pos[:, e, 0:SHARE].rearrange("p (t o) -> p t o", o=1).to_broadcast([P, SHARE, P]), ALU.is_equal).then_inc(s_oh, 1)
                ve.wait_ge(s_used, E)
                step(v.tensor_copy(found[:, :, :, :], hits))
                step(v.tensor_tensor(picked[:, :, :], found[:, :, 0, :], found[:, :, 1, :], ALU.add))
                step(v.tensor_tensor(kept[:, :, :, 0], found[:, :, 2, :], found[:, :, 3, :], ALU.add))
                step(v.tensor_tensor(kept[:, :, :, 0], kept[:, :, :, 0], found[:, :, 4, :], ALU.add))


def expert_layer1(nc, io, picked, kept, w, sum_d, norm_d, consts):
    ident, F = consts["ident"], F1
    kept = kept[:, :, :, :].rearrange("p e a o -> p (e a) o")
    with ExitStack() as ctx:
        def sb(name, shape, dt=F32):
            return ctx.enter_context(nc.sbuf_tensor(f"m1_{name}", shape, dt))

        phase = ctx.enter_context(Semaphores(nc))

        def sem(name):
            return phase.take(f"m1_{name}")

        gb = sb("gb", [P, 2])
        idx = sb("idx", [P, E, 4], I32)
        y = sb("y", [P, 2, 4, C])
        yT = sb("yT", [P, 2, CAP])
        hT = sb("hT", [P, 2, 4, CAP])
        ob = sb("ob", [P, 2, 4, C])
        o = sb("o", [P, 2, 4, C])
        ps_x = ctx.enter_context(nc.psum_tensor("m1_ps_x", [P, CAP], F32))
        ps_h = [ctx.enter_context(nc.psum_tensor(f"m1_ps_h{i}", [P, CAP], F32)) for i in range(2)]
        ps_o = [ctx.enter_context(nc.psum_tensor(f"m1_ps_o{i}", [P, CAP], F32)) for i in range(2)]
        s_c = sem("norm_weights_loaded")
        s_w = [sem(f"weights_loaded{i}") for i in range(2)]
        s_ix = sem("indices_ready")
        s_y = [sem(f"rows_gathered{i}") for i in range(2)]
        s_yp = sem("rows_transposed")
        s_yT = sem("rows_scaled")
        s_h = sem("hidden_ready")
        s_g = sem("gelu_done")
        s_o = sem("output_ready")
        s_ow = sem("output_weighted")
        s_ob = sem("bias_added")
        s_sc = [sem(f"rows_added{i}") for i in range(2)]
        s_gate = sem("gate_pool")

        with nc.Block() as block:
            @block.sync
            def _(sp):
                sp.dma_start(gb[:, :], io["gb1"]).then_inc(s_c, 16)

                with sp.Fori(1, E // 2) as k:
                    for u in range(2):
                        sp.wait_ge(s_ob, 2 * k + u - 1)
                        sp.dma_start(w[:, u, :], io["w1"][bass.ds(2 * k + u, 1), :, :].rearrange("e p f -> (e p) f"))\
                            .then_inc(s_w[u], 16)

            @block.gpsimd
            def _(pool):
                def gather(e, a):
                    nc.gpsimd.indirect_dma_start(out=y[:, e % 2, a, :], out_offset=None, in_=norm_d,
                                                 in_offset=bass.IndirectOffsetOnAxis(ap=idx[:, e, a:a + 1], axis=0))\
                        .then_inc(s_y[e % 2], 16)

                pool.wait_ge(s_ix, 1)
                for e in range(2):
                    for a in range(4):
                        gather(e, a)
                for e in range(E):
                    if e + 2 < E:
                        pool.wait_ge(s_yp, e + 1)
                        gather(e + 2, 0)
                        gather(e + 2, 1)
                    pool.wait_ge(s_ow, e + 1)
                    for a in range(4):
                        after(pool, s_sc[a % 2], 32 * e + 16 * (a // 2))
                        nc.gpsimd.indirect_dma_start(out=sum_d[a % 2],
                                                     out_offset=bass.IndirectOffsetOnAxis(ap=idx[:, e, a:a + 1], axis=0),
                                                     in_=o[:, e % 2, a, :], in_offset=None, compute_op=ALU.add)\
                            .then_inc(s_sc[a % 2], 16)
                        if e + 2 < E and a == 1:
                            gather(e + 2, 2)
                            gather(e + 2, 3)
                for i in range(2):
                    pool.wait_ge(s_sc[i], 32 * E)

            @block.tensor
            def _(pe):
                def transpose(e, k, u):
                    pe.wait_ge(s_y[u], 64 * k + 64)
                    after(pe, s_yT, e)
                    for a in range(4):
                        last = nc.tensor.transpose(ps_x[:, a * P:(a + 1) * P], y[:, u, a, :], ident[:, :])
                    last.then_inc(s_yp, 1)

                def expand(e, k, u):
                    after(pe, s_w[u], 16 * k)
                    pe.wait_ge(s_yT, e + 1)
                    for f in range(4):
                        after(pe, s_g, 4 * e + f - 1)
                        nc.tensor.matmul(ps_h[f % 2][:, :], w[:, u, f * P:(f + 1) * P], yT[:, u, :], start=True, stop=True)\
                            .then_inc(s_h, 1)

                def reduce(e, u):
                    after(pe, s_ob, e - 1)
                    pe.wait_ge(s_g, 4 * e + 4)
                    for a in range(4):
                        out = ps_o[u][:, a * P:(a + 1) * P]
                        for f in range(4):
                            last = nc.tensor.matmul(out, hT[:, u, f, a * P:(a + 1) * P], w[:, u, F + f * P:F + (f + 1) * P],
                                                    start=a == 0 and f == 0, stop=f == 3, skip_group_check=True)
                    last.then_inc(s_o, 1)

                def pair(k, more=True):
                    expand(2 * k, k, 0)
                    reduce(2 * k, 0)
                    transpose(2 * k + 1, k, 1)
                    expand(2 * k + 1, k, 1)
                    reduce(2 * k + 1, 1)
                    if more:
                        transpose(2 * k + 2, k + 1, 0)

                transpose(0, 0, 0)
                pair(0)
                with pe.Fori(1, E // 2 - 1) as k:
                    pair(k)
                pair(E // 2 - 1, more=False)

            @block.scalar
            def _(act):
                def gelu(e, k, u):
                    after(act, s_o, e - 1)
                    for f in range(4):
                        act.wait_ge(s_h, 4 * e + f + 1)
                        nc.scalar.activation(hT[:, u, f, :], ps_h[f % 2][:, :], ACT.Gelu_apprx_tanh,
                                             bias=w[:, u, 2 * F + f:2 * F + f + 1]).then_inc(s_g, 1)

                for u in range(2):
                    gelu(u, 0, u)
                with act.Fori(1, E // 2) as k:
                    for u in range(2):
                        gelu(2 * k + u, k, u)

            @block.vector
            def _(ve):
                ve.wait_ge(s_c, 16)

                nc.vector.tensor_copy(idx[:, :, :], picked[:, :, :]).then_inc(s_ix, 1)

                def scale(e, u):
                    ve.wait_ge(s_yp, e + 1)
                    after(ve, s_h, 4 * (e - 1))
                    nc.vector.tensor_scalar(yT[:, u, :], ps_x[:, :], gb[:, 0:1], gb[:, 1:2], ALU.mult, ALU.add).then_inc(s_yT, 1)

                def add_bias(e, u):
                    ve.wait_ge(s_o, e + 1)
                    after(ve, s_ow, e - 1)
                    nc.vector.tensor_tensor(ob[:, u, :, :], ps_o[u][:, :].rearrange("p (a c) -> p a c", a=4),
                                            w[:, u:u + 1, 2 * F + 4:W1].to_broadcast([P, 4, C]), ALU.add).then_inc(s_ob, 1)

                def weigh(e, u):
                    ve.wait_ge(s_ob, e + 1)
                    for i in range(2):
                        after(ve, s_sc[i], 32 * (e - 1))
                    nc.vector.tensor_tensor(o[:, u, :, :], ob[:, u, :, :],
                                            kept[:, bass.ds(4 * e, 4), :].to_broadcast([P, 4, C]), ALU.mult).then_inc(s_ow, 1)

                scale(0, 0)
                add_bias(0, 0)
                scale(1, 1)
                weigh(0, 0)
                with ve.Fori(1, E // 2) as k:
                    add_bias(2 * k - 1, 1)
                    scale(2 * k, 0)
                    weigh(2 * k - 1, 1)
                    add_bias(2 * k, 0)
                    scale(2 * k + 1, 1)
                    weigh(2 * k, 0)
                add_bias(E - 1, 1)
                weigh(E - 1, 1)


def write_output(nc, io, xn, stats, norm, sum_d):
    with ExitStack() as ctx:
        phase = ctx.enter_context(Semaphores(nc))

        def sem(name):
            return phase.take(f"w_{name}")

        bns = ctx.enter_context(nc.sbuf_tensor("w_bns", [P, NTILE, 6], F32))
        other = ctx.enter_context(nc.sbuf_tensor("w_other", [P, NTILE, C], F32))
        s_add = sem("sums_joined")
        s_x = [sem(f"sum_loaded{i}") for i in range(4)]
        s_bn = sem("row_stats_taken")
        s_ag = sem("row_stats_merged")
        s_n = sem("tile_normalised")
        s_out = sem("output_stored")
        part = NTILE // 4
        src = [d.rearrange("(t p) c -> p t c", p=P) for d in sum_d]
        dst = io["out"].rearrange("(t p) c -> p t c", p=P)
        with nc.Block() as block:
            @block.sync
            def _(sp):
                for i in range(4):
                    for dst_i, src_i in zip((xn, other), src):
                        sp.dma_start(dst_i[:, i * part:(i + 1) * part, :], src_i[:, i * part:(i + 1) * part, :]).then_inc(s_x[i], 16)

            @block.vector
            def _(ve):
                for t in range(NTILE):
                    if t % part == 0:
                        ve.wait_ge(s_x[t // part], 32)
                        nc.vector.tensor_tensor(xn[:, t:t + part, :], xn[:, t:t + part, :], other[:, t:t + part, :], ALU.add)\
                            .then_inc(s_add, 1)
                        ve.wait_ge(s_add, t // part + 1)
                    nc.vector.bn_stats(bns[:, t, :], xn[:, t, :]).then_inc(s_bn, 1)
                merge_stats(nc, ve, stats, bns, s_bn, s_ag)
                norm.vector(ve)
                for t in range(NTILE):
                    nc.vector.tensor_scalar(xn[:, t, :], xn[:, t, :], stats[:, t, 0:1], norm.rstd[:, t:t + 1],
                                            ALU.subtract, ALU.mult).then_inc(s_n, 1)

            @block.scalar
            def _(act):
                norm.scalar(act)
                for i in range(4):
                    act.wait_ge(s_n, part * (i + 1))
                    act.dma_start(dst[:, i * part:(i + 1) * part, :], xn[:, i * part:(i + 1) * part, :]).then_inc(s_out, 16)
                act.wait_ge(s_out, 64)


def merge_stats(nc, ve, stats, bns, s_bn, s_ag):
    ve.wait_ge(s_bn, NTILE)
    for t in range(NTILE):
        nc.vector.bn_aggr(stats[:, t, :], bns[:, t, :]).then_inc(s_ag, 1)
    ve.wait_ge(s_ag, NTILE)


def invert_spread(nc, norm):
    with nc.Block() as block:
        @block.vector
        def _(ve):
            norm.vector(ve)

        @block.scalar
        def _(act):
            norm.scalar(act)


class Norm:

    def __init__(self, nc, ctx, name, stats, n=NTILE):
        self.nc, self.stats, self.n, self.name = nc, stats, n, name
        self.ve = ctx.enter_context(nc.sbuf_tensor(f"{name}_ve", [P, n], F32))
        self.sq = ctx.enter_context(nc.sbuf_tensor(f"{name}_sq", [P, n], F32))
        self.t = ctx.enter_context(nc.sbuf_tensor(f"{name}_t", [P, n], F32))
        self.rstd = ctx.enter_context(nc.sbuf_tensor(f"{name}_rstd", [P, n], F32))
        phase = ctx.enter_context(Semaphores(nc))
        self.s_v = phase.take(f"{name}_variance")
        self.s_q = phase.take(f"{name}_root")
        self.s_r = phase.take(f"{name}_rstd")

    def vector(self, ve, base=0):
        nc = self.nc
        steps = [0]

        def step(ins):
            steps[0] += 1
            ins.then_inc(self.s_r, 1)
            ve.wait_ge(self.s_r, steps[0])

        nc.vector.tensor_scalar(self.ve[:, :], self.stats[:, :, 1], EPS, None, ALU.add).then_inc(self.s_v, 1)
        ve.wait_ge(self.s_q, 1)
        step(nc.vector.reciprocal(self.rstd[:, :], self.sq[:, :]))
        step(nc.vector.tensor_tensor(self.t[:, :], self.rstd[:, :], self.rstd[:, :], ALU.mult))
        step(nc.vector.tensor_tensor(self.t[:, :], self.t[:, :], self.ve[:, :], ALU.mult))
        step(nc.vector.tensor_scalar(self.t[:, :], self.t[:, :], -0.5, 1.5, ALU.mult, ALU.add))
        step(nc.vector.tensor_tensor(self.rstd[:, :], self.rstd[:, :], self.t[:, :], ALU.mult))

    STEPS = 5

    def scalar(self, act):
        act.wait_ge(self.s_v, 1)
        self.nc.scalar.activation(self.sq[:, :], self.ve[:, :], ACT.Sqrt).then_inc(self.s_q, 1)


def program(nc, io):
    with ExitStack() as ctx:
        def sb(name, shape, dt=F32):
            return ctx.enter_context(nc.sbuf_tensor(name, shape, dt))

        phase = ctx.enter_context(Semaphores(nc))

        def sem(name):
            return phase.take(name)

        xn = sb("xn", [P, NTILE, C])
        stats = sb("stats", [P, NTILE, 2])
        consts = {"ident": sb("ident", [P, P]), "ident_bf": sb("ident_bf", [P, P], BF16), "ones_row": sb("ones_row", [1, P]),
                  "tri4": sb("tri4", [P, 4, P], BF16), "upper": sb("upper", [P, P]), "ones_sq": sb("ones_sq", [P, P])}
        s_id = sem("ident_loaded")
        with nc.Block() as block:
            @block.sync
            def _(sp):
                sp.dma_start(consts["ident"][:, :], io["ident"]).then_inc(s_id, 16)
                sp.wait_ge(s_id, 16)
        layer0_attention(nc, io, xn, stats, consts)
        norm = Norm(nc, ctx, "norm_a", stats)
        invert_spread(nc, norm)
        expert_layer0(nc, io, xn, stats, norm, consts)
        norm = Norm(nc, ctx, "norm_b", stats)
        invert_spread(nc, norm)
        layer1_attention(nc, io, xn, stats, norm, consts)
        norm = Norm(nc, ctx, "norm_c", stats)
        invert_spread(nc, norm)
        gate_act = sb("gate_act", [P, E, NTILE])
        stats_y = sb("stats_y", [P, NTILE, 2])
        picked, kept = sb("picked", [P, E, 4]), sb("kept", [P, E, 4, 1])
        w1 = sb("w1", [P, 2, W1])
        score_tokens(nc, io, xn, stats, stats_y, norm, gate_act, consts)
        norm_y = Norm(nc, ctx, "norm_y", stats_y)
        invert_spread(nc, norm_y)
        sum_d = [nc.dram_tensor(f"sum{i}", [NTOK, C], F32, kind="Internal").ap() for i in range(2)]
        norm_d = nc.dram_tensor("normed", [NTOK, C], F32, kind="Internal").ap()
        choose_tokens(nc, io, xn, stats_y, norm_y, gate_act, picked, kept, w1, sum_d, norm_d, consts)
        expert_layer1(nc, io, picked, kept, w1, sum_d, norm_d, consts)
        write_output(nc, io, xn, stats, Norm(nc, ctx, "norm_d", stats), sum_d)


def kernel(**inputs):
    import numpy as np
    import concourse.bacc as bacc
    from concourse import mybir as _mybir
    from concourse.bass_utils import run_bass_kernel_spmd as run

    a = {k: np.asarray(v) for k, v in inputs.items()}
    f32 = np.float32

    half = HD // 2
    inv_freq = (f32(1.0) / f32(10000.0) ** (np.arange(half, dtype=f32) / f32(half))).astype(f32)
    freqs = np.arange(T, dtype=f32)[None, :] * inv_freq[:, None]
    cos = np.repeat(np.repeat(np.cos(freqs), 2, axis=0), H, axis=0).astype(f32)
    sin = np.repeat(np.repeat(np.sin(freqs), 2, axis=0), H, axis=0).astype(f32)
    sign = np.where((np.arange(P) // H) % 2 == 0, f32(-1.0), f32(1.0))[:, None]
    rot = np.ascontiguousarray(np.stack([cos, sin * sign], axis=1).astype(f32))

    dh = np.arange(P).reshape(H, HD).T.reshape(-1)
    swap = np.arange(HD) ^ 1
    dh_swap = np.arange(P).reshape(H, HD)[:, swap].T.reshape(-1)
    wqkv = a["L0_attn_Wqkv"]
    wqk = np.stack([wqkv[:, dh], wqkv[:, dh_swap], wqkv[:, P + dh], wqkv[:, P + dh_swap]], axis=1)
    x = a["L0_attn_x"].reshape(NTOK, C)
    host = {
        "x": x, "xT": x.T, "wqk": wqk, "rot": rot, "wv": wqkv[:, 2 * P:], "wo": a["L0_attn_Wo"],
        "bo": np.broadcast_to(a["L0_attn_bo"], (P, C)), "tri": np.where(np.tril(np.ones((P, P), bool)), f32(0), f32(-BIG)),
        "ident": np.eye(P, dtype=f32), "upper": np.triu(np.ones((P, P), f32)),
    }
    gu = a["L0_ffn_gate_up_proj"].reshape(E, C, P, 2)
    sel = np.zeros((32, E, P), f32)
    for part in range(3):
        sel[part * E + np.arange(E), np.arange(E)] = 1
    host.update({
        "wr": a["L0_ffn_router_weight"], "wgu": gu.transpose(1, 0, 3, 2),
        "bgu": a["L0_ffn_gate_up_proj_bias"].reshape(E, P, 2).transpose(1, 0, 2),
        "wd0": a["L0_ffn_down_proj"].transpose(1, 0, 2), "bd0": np.concatenate([a["L0_ffn_down_proj_bias"]] * 3 + [np.zeros((32 - 3 * E, C), f32)]),
        "sel": sel, "desc": np.broadcast_to(np.arange(E, 0, -1).astype(f32), (P, E)),
    })
    dh1 = np.arange(H * FD).reshape(H, FD).T.reshape(2, P)
    wqk1 = np.stack([a[w].T[:, half] for w in ("L1_attn_Wq", "L1_attn_Wk") for half in dh1], axis=1)
    host.update({"wqk1": wqk1, "wv1": a["L1_attn_Wv"].T, "wo1": a["L1_attn_Wo"].T})
    fc1T = a["L1_ffn_fc1s"].transpose(0, 2, 1)
    fc2T = a["L1_ffn_fc2s"].transpose(0, 2, 1).reshape(E, 4, P, C).transpose(0, 2, 1, 3).reshape(E, P, 4 * C)
    b1T = a["L1_ffn_b1s"].reshape(E, 4, P).transpose(0, 2, 1)
    host.update({
        "wg1": a["L1_ffn_gate_w"].T, "w1": np.concatenate(
            [fc1T, fc2T, b1T, np.broadcast_to(a["L1_ffn_b2s"][:, None, :], (E, P, C))], axis=2),
        "gb1": np.stack([a["L1_ffn_ln_gamma"], a["L1_ffn_ln_beta"]], axis=1),
        "iota": np.broadcast_to(np.arange(P, dtype=f32), (P, P)),
        "tile0": np.broadcast_to(P * np.arange(NTILE, dtype=f32), (P, NTILE)),
        "not0": np.broadcast_to((np.arange(E * NTILE) % NTILE != 0).astype(f32), (P, E * NTILE)),
        "row": np.arange(P, dtype=f32).reshape(P, 1),
    })
    nc = bacc.Bacc("TRN2", target_bir_lowering=False, num_devices=1)
    arrays, io = {}, {}
    for name, v in host.items():
        v = np.ascontiguousarray(v)
        arrays[f"in_{name}"] = v
        io[name] = nc.dram_tensor(f"in_{name}", v.shape, _mybir.dt.from_np(v.dtype), kind="ExternalInput").ap()
    io["out"] = nc.dram_tensor("out_x", (NTOK, C), F32, kind="ExternalOutput").ap()
    program(nc, io)
    r = run(nc, [arrays], core_ids=[0])
    return r.results[0]["out_x"].reshape(NB, T, C)
```

```python
from contextlib import ExitStack

import concourse.bass as bass
from concourse import mybir

F32 = mybir.dt.float32
BF16 = mybir.dt.bfloat16
ALU = mybir.AluOpType
ACT = mybir.ActivationFunctionType
I32 = mybir.dt.int32
AX_X = mybir.AxisListType.X

P = 128
NB, T, C = 16, 256, 128
NTOK = NB * T
NTILE = NTOK // P
H, HD = 16, 8
HV = HD + 1
VW = 32
F1 = 4 * C
W1 = 2 * F1 + 4 + C
CH = 512
NCH = NTOK // CH
FD = 16
E = 8
ALPHA, LIMIT = 1.702, 7.0
CAP = NTOK // E
ROUNDS = 13
DEN_EPS = 1e-12
NPART = 3
PART_ORDER = ((0, 1, 2), (2, 1, 0))
SLOT_RUNS = {"q": ((0, 0, 3), (3, 0, 2), (5, 0, 1)), "k": ((0, 0, 3), (3, 1, 2), (5, 2, 1))}
UH = 8
NU = NB * H // UH
EPS = 1e-5
BIG = 1e30


def after(eng, sem, n):
    if isinstance(n, int) and n <= 0:
        return
    eng.wait_ge(sem, n)


class Semaphores:

    def __init__(self, nc):
        self.nc, self.taken = nc, []

    def __enter__(self):
        return self

    def take(self, name):
        self.taken.append(self.nc.alloc_semaphore(name))
        return self.taken[-1]

    def __exit__(self, *exc):
        if exc[0] is None:
            self.nc.clear_and_free_semaphores(self.taken)
            self.nc.all_engine_barrier()


def settled(eng, sem, n, gate):
    after(eng, sem, n)
    if not isinstance(n, int):
        eng.sem_inc(gate, 1)


def layer0_attention(nc, io, xn, stats, consts):
    scratch = [nc.dram_tensor(f"scratch0_{n}", [NCH, NPART, P, CH], BF16, kind="Internal").ap() for n in "qk"]
    with ExitStack() as keep:
        v_all = keep.enter_context(nc.sbuf_tensor("v_all0", [P, NTILE, H, HV], F32))
        wo = keep.enter_context(nc.sbuf_tensor("wo0", [P, P], F32))
        bo = keep.enter_context(nc.sbuf_tensor("bo0", [P, 1, C], F32))
        stacks = [keep.enter_context(nc.sbuf_tensor(f"{n}st0", [P, 4, UH, T], BF16)) for n in "qk"]
        project_layer0(nc, io, scratch, stacks, v_all, wo, bo, xn, consts)
        attend(nc, io, "a0", stacks, scratch, 6 * HD, v_all, xn, stats, consts, wo, bo, softmax=True)


def project_layer0(nc, io, scratch, stacks, v_all, wo, bo, xn, consts):
    with ExitStack() as ctx:
        def sb(name, shape, dt=F32):
            return ctx.enter_context(nc.sbuf_tensor(name, shape, dt))

        def ps(name, shape, dt=F32):
            return ctx.enter_context(nc.psum_tensor(name, shape, dt))

        phase = ctx.enter_context(Semaphores(nc))

        def sem(name):
            return phase.take(name)

        ident, ident_bf = consts["ident"], consts["ident_bf"]
        tri4, upper, ones_sq = consts["tri4"], consts["upper"], consts["ones_sq"]
        kst = stacks[1]
        xc = sb("xc", [P, 2, CH])
        wqk = sb("wqk", [P, 4, P])
        wv = sb("wv", [P, P])
        rot = sb("rot", [P, 2, 1, T])
        tri_f = sb("tri_f", [P, P])
        term = sb("term", [P, 2, 2, CH])
        roped = sb("roped", [P, 2, CH])
        resid = sb("resid", [P, 2, CH])
        parts = sb("parts", [P, 4, 3, CH], BF16)

        ps_b = [ps(f"ps_b{i}", [P, 1024]) for i in range(2)]
        ps_a = [ps(f"ps_a{i}", [P, 512]) for i in range(2)]
        ps_qk = [[ps_b[j][:, 512 * i:512 * i + 512] for i in range(2)] for j in range(2)]
        ps_v = ps_a[0]

        s_w = sem("weights_loaded")
        s_xn = sem("xn_loaded")
        s_xc = [sem(f"xc_loaded{i}") for i in range(2)]
        s_zero = sem("stacks_cleared")
        s_tri = sem("tri_ready")
        s_proj = sem("qk_projected")
        s_rot = sem("qk_psum_read")
        s_rope = sem("qk_roped")
        s_hi = sem("hi_done")
        s_r1 = sem("residual_done")
        s_mid = sem("mid_done")
        s_lo = sem("lo_done")
        s_store = [sem(f"parts_stored{i}") for i in range(4)]
        s_vp = sem("v_projected")
        s_vc = sem("v_copied")

        with nc.Block() as block:
            @block.sync
            def _(sp):
                for dst, src in ((wqk[:, :, :], io["wqk"]), (rot[:, :, 0, :], io["rot"]), (wv[:, :], io["wv"])):
                    sp.dma_start(dst, src).then_inc(s_w, 16)

                def load(c, u):
                    sp.dma_start(xc[:, u, :], io["xT"][:, bass.ds(c * CH, CH)]).then_inc(s_xc[u], 16)

                def store(c, u):
                    for j in range(2):
                        n = 2 * c + j
                        sp.wait_ge(s_lo, n + 1)
                        src = parts[:, 2 * u + j, :, :]
                        dst = scratch[j][bass.ds(c, 1), :, :, :].rearrange("c s p t -> p (c s) t")
                        sp.dma_start(dst, src).then_inc(s_store[2 * u + j], 16)

                for u in range(2):
                    load(u, u)
                for dst, src in ((wo[:, :], io["wo"]), (bo[:, 0, :], io["bo"]), (tri_f[:, :], io["tri"]), (upper[:, :], io["upper"])):
                    sp.dma_start(dst, src).then_inc(s_w, 16)
                sp.dma_start(xn[:, :, :], io["x"].rearrange("(t p) c -> p t c", p=P)).then_inc(s_xn, 16)
                with sp.Fori(0, NCH // 2 - 1) as k:
                    for u in range(2):
                        sp.wait_ge(s_vp, 2 * k + u + 1)
                        load(2 * k + u + 2, u)
                        store(2 * k + u, u)
                for u in range(2):
                    store(NCH - 2 + u, u)
                for n in range(4):
                    sp.wait_ge(s_store[n], 16 * (NCH // 2))
                sp.wait_ge(s_xn, 16)

            @block.tensor
            def _(pe):
                pe.wait_ge(s_w, 48)

                def chunk(k, u):
                    c = 2 * k + u
                    pe.wait_ge(s_xc[u], 16 * k + 16)
                    for j in range(2):
                        after(pe, s_rot, 2 * c + j - 1)
                        for i in range(2):
                            last = nc.tensor.matmul(ps_qk[j][i], wqk[:, 2 * j + i, :], xc[:, u, :], start=True, stop=True)
                        last.then_inc(s_proj, 1)
                    after(pe, s_vc, c)
                    for t in range(4):
                        last = nc.tensor.matmul(ps_v[:, t * P:(t + 1) * P], xc[:, u, t * P:(t + 1) * P], wv[:, :],
                                                start=True, stop=True)
                    last.then_inc(s_vp, 1)

                for u in range(2):
                    chunk(0, u)
                with pe.Fori(1, NCH // 2) as k:
                    for u in range(2):
                        chunk(k, u)

            @block.vector
            def _(ve):
                nc.vector.memset(v_all[:, :, :, HD:HV], 1.0).then_inc(s_zero, 1)
                nc.vector.memset(kst[32:64, :, :, :], -1.0).then_inc(s_zero, 1)
                nc.vector.memset(ones_sq[:, :], 1.0).then_inc(s_zero, 1)
                ve.wait_ge(s_w, 112)
                for i in range(4):
                    nc.vector.tensor_copy(tri4[:, i, :], tri_f[:, :]).then_inc(s_tri, 1)
                nc.vector.tensor_copy(ident_bf[:, :], ident[:, :]).then_inc(s_tri, 1)

                def item(c, j):
                    n = 2 * c + j
                    ve.wait_ge(s_proj, n + 1)
                    for i in range(2):
                        last = nc.vector.tensor_tensor(
                            term[:, j, i, :].rearrange("p (b t) -> p b t", b=2),
                            ps_qk[j][i].rearrange("p (b t) -> p b t", b=2),
                            rot[:, i, :, :].to_broadcast([P, 2, T]), ALU.mult)
                    last.then_inc(s_rot, 1)
                    ve.wait_ge(s_rot, n + 1)
                    after(ve, s_r1, n - 1)
                    nc.vector.tensor_tensor(roped[:, j, :], term[:, j, 0, :], term[:, j, 1, :], ALU.add).then_inc(s_rope, 1)

                for j in range(2):
                    item(0, j)
                with ve.Fori(1, NCH) as c:
                    for j in range(2):
                        item(c, j)

            @block.scalar
            def _(act):
                act.wait_ge(s_zero, 1)

                def chunk(k, u):
                    c = 2 * k + u
                    for j in range(2):
                        n = 2 * c + j
                        act.wait_ge(s_rope, n + 1)
                        after(act, s_store[2 * u + j], 16 * k)
                        nc.scalar.activation(parts[:, 2 * u + j, PART_ORDER[j][0], :], roped[:, j, :], ACT.Copy).then_inc(s_hi, 1)
                    for j in range(2):
                        act.wait_ge(s_r1, 2 * c + j + 1)
                        nc.scalar.activation(parts[:, 2 * u + j, PART_ORDER[j][1], :], resid[:, j, :], ACT.Copy).then_inc(s_mid, 1)
                    act.wait_ge(s_vp, c + 1)
                    nc.scalar.activation(v_all[:, bass.ds(4 * c, 4), :, 0:HD],
                                         ps_v[:, :].rearrange("p (t h d) -> p t h d", t=4, h=H), ACT.Copy).then_inc(s_vc, 1)

                for u in range(2):
                    chunk(0, u)
                with act.Fori(1, NCH // 2) as k:
                    for u in range(2):
                        chunk(k, u)

            @block.gpsimd
            def _(pool):
                def chunk(k, u):
                    for j in range(2):
                        n = 4 * k + 2 * u + j
                        pool.wait_ge(s_hi, n + 1)
                        after(pool, s_mid, n - 1)
                        after(pool, s_lo, n - 1)
                        nc.gpsimd.tensor_tensor(resid[:, j, :], roped[:, j, :], parts[:, 2 * u + j, PART_ORDER[j][0], :], ALU.subtract)\
                            .then_inc(s_r1, 1)
                    for j in range(2):
                        pool.wait_ge(s_mid, 4 * k + 2 * u + j + 1)
                        nc.gpsimd.tensor_tensor(parts[:, 2 * u + j, PART_ORDER[j][2], :], resid[:, j, :],
                                                parts[:, 2 * u + j, PART_ORDER[j][1], :],
                                                ALU.subtract).then_inc(s_lo, 1)

                for u in range(2):
                    chunk(0, u)
                with pool.Fori(1, NCH // 2) as k:
                    for u in range(2):
                        chunk(k, u)


def attend(nc, io, tag, stacks, scratch, rows, v_all, xn, stats, consts, wo, bo, softmax):
    depth = rows + 3 if softmax else rows
    scale = HD ** -0.5 if softmax else FD ** -0.5
    ident, ident_bf = consts["ident"], consts["ident_bf"]
    tri4, upper, ones_sq = consts["tri4"], consts["upper"], consts["ones_sq"]
    with ExitStack() as ctx:
        def sb(name, shape, dt=F32):
            return ctx.enter_context(nc.sbuf_tensor(f"{tag}_{name}", shape, dt))

        def ps(name, shape, dt=F32):
            return ctx.enter_context(nc.psum_tensor(f"{tag}_{name}", shape, dt))

        phase = ctx.enter_context(Semaphores(nc))

        def sem(name):
            return phase.take(f"{tag}_{name}")

        v_now = sb("v_now", [P, 2, 2, H, VW])
        qst, kst = stacks
        prob = sb("prob", [P, 6, 1024])
        mx = sb("mx", [P, 2, UH, 2])
        mres = sb("mres", [P, 2, 16])
        mparts = sb("mparts", [P, 2, 3, 16], BF16)
        mT = sb("mT", [48, 2, P], BF16)
        outT = sb("outT", [P, 2, 2, T])
        vsum = sb("vsum", [P, 2, 2, H, HV])
        total = sb("total", [P, 2, 2, 4, HV])
        rden = sb("rden", [P, 2, 2, 4, 1])
        att = sb("att", [P, 2, H, HD])
        attT = sb("attT", [P, 2, P])
        bns = sb("bns", [P, NTILE, 6])
        den = sb("den", [P, 2, 2, 4, 1])
        ps_b = [ps(f"ps_b{i}", [P, 1024]) for i in range(2)]
        ps_a = [ps(f"ps_a{i}", [P, 512]) for i in range(2)]
        ps_pv = ps("ps_pv", [P, 512])
        ps_m = ps("ps_m", [P, 512])

        s_st = [sem(f"stack_loaded{i}") for i in range(4)]
        s_mrow = [sem(f"max_rows_loaded{i}") for i in range(2)]
        s_gate_pe, s_gate_pool, s_gate_act = sem("gate_pe"), sem("gate_pool"), sem("gate_act")
        s_af = sem("max_scores_ready")
        s_mx = sem("max_taken")
        s_mh = sem("max_hi_done")
        s_mr = sem("max_residual_done")
        s_mm = sem("max_mid_done")
        s_mp = sem("max_parts_done")
        s_mT = sem("max_transposed")
        s_mTc = sem("max_rows_copied")
        s_b = sem("scores_ready")
        s_e = sem("exp_done")
        s_k = sem("causal_masked")
        s_pv = sem("weighted_v_done")
        s_vn = sem("v_now_ready")
        s_vz = sem("v_now_cleared")
        s_ev = sem("out_rows_copied")
        s_tp = sem("out_transposed")
        s_vs = sem("v_summed")
        s_vsc = sem("v_sums_copied")
        s_tot = sem("v_sums_added")
        s_bias = sem("bias_added")
        s_later = sem("later_weights_loaded")
        s_rd = sem("denominator_inverted")
        s_on = sem("out_normalised")
        s_aT = sem("attention_transposed")
        s_aTc = sem("attention_rows_copied")
        s_o = sem("output_projected")
        s_y = sem("residual_added")
        s_bn = sem("row_stats_taken")
        s_ag = sem("row_stats_merged")
        s_clear = sem("stacks_cleared")
        s_de = sem("denominator_guarded")

        with nc.Block() as block:
            @block.sync
            def _(sp):
                def load(c, s):
                    h0, t0 = UH * (s % 2), T * (s // 2)
                    dims = rows // 6
                    for name, st, sc in (("q", qst, scratch[0]), ("k", kst, scratch[1])):
                        src = sc[bass.ds(c, 1), :, :, :].rearrange("c s (d h) t -> (c s d) h t", h=H)[:, h0:h0 + UH, t0:t0 + T]
                        for s0, part, n in SLOT_RUNS[name]:
                            sp.dma_start(st[dims * s0:dims * (s0 + n), s, :, :],
                                         src[dims * part:dims * (part + n), :, :]).then_inc(s_st[s], 16)

                def max_rows(k, s):
                    sp.wait_ge(s_mTc, 4 * k + s + 1)
                    for p in range(3):
                        dst = qst[rows + p:rows + p + 1, s % 4, :, :].rearrange("p h (x q) -> p (h x) q", q=P)
                        sp.dma_start(dst, mT[16 * p:16 * p + 16, s % 2, :]).then_inc(s_mrow[s % 2], 16)

                for s in range(4):
                    load(0, s)
                if softmax:
                    max_rows(0, 0)
                    for name, dst in consts["later"].items():
                        sp.dma_start(dst[tuple(slice(None) for _ in dst.shape)], io[name]).then_inc(s_later, 16)

                def slot(k, s, next_max=softmax, more=True):
                    if next_max:
                        max_rows(k, s + 1)
                    if more:
                        sp.wait_ge(s_b, 12 * k + 3 * s + 3)
                        load(k + 1, s)

                for s in range(4):
                    slot(0, s)
                with sp.Fori(1, NU // 4 - 1) as k:
                    for s in range(4):
                        slot(k, s)
                for s in range(4):
                    slot(NU // 4 - 1, s, next_max=softmax and s < 3, more=False)
                if softmax:
                    sp.wait_ge(s_later, 16 * len(consts["later"]))

            @block.tensor
            def _(pe):
                def fill(k, s, f):
                    g = 24 * k + 6 * s + f
                    after(pe, s_mx, g - 1)
                    if f == 1:
                        after(pe, s_on, 4 * k + s - 3)
                    s = s % 4
                    out = ps_a[f % 2]
                    if f < 4:
                        for i in range(2):
                            nc.tensor.matmul(out[:, 256 * i:256 * i + 256], qst[0:48, s, 2 * f + i, P:2 * P],
                                             kst[0:48, s, 2 * f + i, :], start=i == 0, stop=False, skip_group_check=True)
                        o = out[:, :].rearrange("p (h k) -> p h k", h=2)[:, :, P:2 * P]
                        nc.tensor.matmul(o, ident_bf[:, :], tri4[:, 0:2, :], start=False, stop=True,
                                         skip_group_check=True).then_inc(s_af, 1)
                    else:
                        for i in range(4):
                            h = 4 * (f - 4) + i
                            nc.tensor.matmul(out[:, P * i:P * i + P], qst[0:48, s, h, 0:P], kst[0:48, s, h, 0:P],
                                             start=i == 0, stop=False, skip_group_check=True)
                        nc.tensor.matmul(out[:, :], ident_bf[:, :], tri4[:, :, :], start=False, stop=True,
                                         skip_group_check=True).then_inc(s_af, 1)

                def stack_ready(k, s):
                    pe.wait_ge(s_st[s % 4], 96 * (k + s // 4) + 96)

                def scores(k, s, j):
                    r = 12 * k + 3 * s + j
                    after(pe, s_e, r - 1)
                    out = ps_b[(3 * s + j) % 2]
                    if j < 2:
                        for i in range(4):
                            last = nc.tensor.matmul(out[:, 256 * i:256 * i + 256], kst[0:depth, s, 4 * j + i, 0:P],
                                                    qst[0:depth, s, 4 * j + i, :], start=True, stop=True)
                    else:
                        for i in range(8):
                            last = nc.tensor.matmul(out[:, P * i:P * i + P], kst[0:depth, s, i, P:2 * P],
                                                    qst[0:depth, s, i, P:2 * P], start=True, stop=True)
                    last.then_inc(s_b, 1)

                def weighted(k, s, j):
                    r = 12 * k + 3 * s + j
                    u = 4 * k + s
                    pe.wait_ge(s_k, r + 1)
                    if j == 0:
                        after(pe, s_ev, u)
                        if s % 2 == 0:
                            pe.wait_ge(s_vn, 2 * k + s // 2 + 1)
                    h0, par = UH * (s % 2), s // 2
                    reg = prob[:, (3 * s + j) % 6, :]
                    for i in range(4 if j < 2 else UH):
                        part = slice(VW * (i % 4), VW * (i % 4) + VW)
                        if j < 2:
                            last = nc.tensor.matmul(ps_pv[part, T * j:T * j + T], v_now[:, par, 0, h0 + 4 * j + i, :],
                                                    reg[:, T * i:T * i + T], start=j == 0, stop=False, skip_group_check=True)
                        else:
                            q0 = T * (i // 4) + P
                            last = nc.tensor.matmul(ps_pv[part, q0:q0 + P], v_now[:, par, 1, h0 + i, :],
                                                    reg[:, P * i:P * i + P], start=False, stop=True, skip_group_check=True)
                    last.then_inc(s_pv, 1)

                def turn_out(k, s, fills):
                    w = 4 * k + s
                    after(pe, s_ev, w + 1)
                    if softmax:
                        pe.wait_ge(s_mx, 6 * (w + 3) + 6 if fills else 6 * NU)
                    after(pe, s_on, w)
                    for i in range(2):
                        for q in range(2):
                            last = nc.tensor.transpose(ps_a[1][:, (2 * i + q) * P:(2 * i + q + 1) * P],
                                                       outT[:, s % 2, i, q * P:q * P + P], ident[:, :])
                    last.then_inc(s_tp, 1)

                def sum_v(b, par):
                    pe.wait_ge(s_vn, b + 1)
                    after(pe, s_y, b - 1)
                    vt = [v_now[:, par, t, :, 0:HV] for t in range(2)]
                    out = [ps_m[:, H * HV * t:H * HV * (t + 1)].rearrange("p (h d) -> p h d", h=H) for t in range(2)]
                    nc.tensor.matmul(out[0], upper[:, :], vt[0], start=True, stop=False, skip_group_check=True)
                    nc.tensor.matmul(out[1], ones_sq[:, :], vt[0], start=False, stop=False, skip_group_check=True)
                    nc.tensor.matmul(out[1], upper[:, :], vt[1], start=False, stop=True, skip_group_check=True).then_inc(s_vs, 1)

                def transpose_max(n, s):
                    settled(pe, s_mp, n + 1, s_gate_pe)
                    nc.tensor.transpose(ps_m[0:48, 0:64].bitcast(BF16), mparts[:, s % 2, :, :].rearrange("p a b -> p (a b)"),
                                        ident_bf[:, :]).then_inc(s_mT, 1)

                def transpose_att(b):
                    pe.wait_ge(s_on, 2 * b + 2)
                    for q in range(2):
                        last = nc.tensor.transpose(ps_m[:, q * P:q * P + P], att[:, q, :, :].rearrange("p h d -> p (h d)"),
                                                   ident[:, :])
                    last.then_inc(s_aT, 1)

                def project(b):
                    pe.wait_ge(s_aTc, b + 1)
                    for q in range(2):
                        o = ps_m[:, q * P:q * P + P]
                        last = nc.tensor.matmul(o, attT[:, q, :], wo[:, :], start=q == 0, stop=True, skip_group_check=True)
                    last.then_inc(s_o, 1)

                def slot(k, s, fills=softmax, tr=softmax, prev=True):
                    u = 4 * k + s
                    b = 2 * k + s // 2
                    if softmax:
                        pe.wait_ge(s_mrow[s % 2], 48 * (2 * k + s // 2) + 48)
                    else:
                        stack_ready(k, s)
                    prev1 = prev or s > 0
                    w = (k - 1, 3) if s == 0 else (k, s - 1)
                    for j in range(3):
                        scores(k, s, j)
                        if j < 2 and prev1:
                            weighted(*w, j + 1)
                        if fills:
                            if j == 0:
                                stack_ready(k, s + 2)
                            fill(k, s + 2, 2 * j)
                            fill(k, s + 2, 2 * j + 1)
                        if j == 2:
                            weighted(k, s, 0)
                        if j == 0 and tr:
                            if s % 2 == 0:
                                after(pe, s_y, b - 1)
                            pe.wait_ge(s_mTc, u + 1)
                            transpose_max(u + 1, s + 1)
                        if j == 0 and not softmax and s % 2 == 0:
                            sum_v(b, s // 2)
                        if j == 1 and s % 2 == 1 and (prev or s > 1):
                            if softmax:
                                pe.wait_ge(s_mTc, u + (2 if tr else 1))
                            else:
                                pe.wait_ge(s_vsc, b + 1)
                            transpose_att(b - 1)
                        if j == 2 and s % 2 == 1 and (prev or s > 1):
                            project(b - 1)
                        if j == 2 and prev1:
                            turn_out(*w, fills)

                if softmax:
                    for s in range(2):
                        stack_ready(0, s)
                        for f in range(6):
                            if (s, f) == (1, 4):
                                transpose_max(0, 0)
                            fill(0, s, f)
                    pe.wait_ge(s_mTc, 1)
                for s in range(4):
                    slot(0, s, prev=False)
                with pe.Fori(1, NU // 4 - 1) as k:
                    for s in range(4):
                        slot(k, s)
                for s in range(4):
                    slot(NU // 4 - 1, s, fills=softmax and s < 2, tr=softmax and s < 3)
                weighted(NU // 4 - 1, 3, 1)
                weighted(NU // 4 - 1, 3, 2)
                turn_out(NU // 4 - 1, 3, False)
                pe.wait_ge(s_y, NB - 1)
                transpose_att(NB - 1)
                project(NB - 1)

            @block.vector
            def _(ve):
                nc.vector.memset(den[:, :, :, :, :], 0.0).then_inc(s_clear, 1)
                nc.vector.memset(v_now[:, :, :, :, :], 0.0).then_inc(s_vz, 1)

                def reduce(k, s, f):
                    g = 24 * k + 6 * s + f
                    if f == 0:
                        after(ve, s_mp, 4 * k + s - 1)
                    ve.wait_ge(s_af, g + 1)
                    if f < 4:
                        nc.vector.reduce_max(mx[:, s % 2, 2 * f:2 * f + 2, 1:2],
                                             ps_a[f % 2][:, :].rearrange("p (h k) -> p h k", h=2), AX_X).then_inc(s_mx, 1)
                    else:
                        h = 4 * (f - 4)
                        nc.vector.reduce_max(mx[:, s % 2, h:h + 4, 0:1],
                                             ps_a[f % 2][:, :].rearrange("p (h k) -> p h k", h=4), AX_X).then_inc(s_mx, 1)

                def normalise(k, s):
                    w = 4 * k + s
                    src = ps_a[1][:, :].rearrange("p (i q h d) -> p i q h d", i=2, q=2, h=4)
                    h0 = UH * (s % 2)
                    ve.wait_ge(s_tp, w + 1)
                    if softmax:
                        out = src
                        nc.vector.reciprocal(rden[:, :, :, :, :].rearrange("p i q h o -> p (i q) h o"),
                                             src[:, :, :, :, HD:HV].rearrange("p i q h o -> p (i q) h o")).then_inc(s_rd, 1)
                    else:
                        out = total
                        if s % 2 == 0:
                            ve.wait_ge(s_vsc, 2 * k + s // 2 + 1)
                        for q in range(2):
                            last = nc.vector.tensor_tensor(total[:, :, q, :, :], src[:, :, q, :, 0:HV],
                                                           vsum[:, s // 2, q, h0:h0 + UH, :].rearrange("p (i h) d -> p i h d", i=2),
                                                           ALU.add)
                        last.then_inc(s_tot, 1)
                        ve.wait_ge(s_tot, w + 1)
                        nc.vector.tensor_scalar(den[:, :, :, :, :].rearrange("p i q h o -> p (i q) h o"),
                                                total[:, :, :, :, HD:HV].rearrange("p i q h o -> p (i q) h o"),
                                                2.0 * DEN_EPS, None, ALU.add).then_inc(s_de, 1)
                        ve.wait_ge(s_de, w + 1)
                        nc.vector.reciprocal(rden[:, :, :, :, :], den[:, :, :, :, :]).then_inc(s_rd, 1)
                    ve.wait_ge(s_rd, w + 1)
                    if s % 2 == 0:
                        after(ve, s_aT, 2 * k + s // 2)
                    for q in range(2):
                        last = nc.vector.tensor_tensor(att[:, q, h0:h0 + UH, :].rearrange("p (i h) d -> p i h d", i=2),
                                                       out[:, :, q, :, 0:HD],
                                                       rden[:, :, q, :, :].to_broadcast([P, 2, 4, HD]), ALU.mult)
                    last.then_inc(s_on, 1)

                def add_residual(b):
                    ve.wait_ge(s_o, b + 1)
                    y = xn[:, bass.ds(2 * b, 2), :]
                    nc.vector.tensor_tensor(y, ps_m[:, 0:2 * P].rearrange("p (t c) -> p t c", t=2), y, ALU.add).then_inc(s_y, 1)

                def row_stats(b):
                    ve.wait_ge(s_clear, 1)
                    ve.wait_ge(s_y, b + 1)
                    for q in range(2):
                        nc.vector.bn_stats(bns[:, bass.ds(2 * b + q, 1), :], xn[:, bass.ds(2 * b + q, 1), :]).then_inc(s_bn, 1)

                def slot(k, s, fills=softmax, prev=True):
                    b = 2 * k + s // 2
                    for j in range(3):
                        if fills:
                            reduce(k, s + 2, 2 * j)
                            reduce(k, s + 2, 2 * j + 1)
                        if j == 2 and s % 2 == 1 and (prev or s > 1):
                            add_residual(b - 1)
                        if j == 2 and (prev or s > 0):
                            normalise(*((k - 1, 3) if s == 0 else (k, s - 1)))
                        if j == 2 and s % 2 == 1 and (prev or s > 1):
                            row_stats(b - 1)

                if softmax:
                    for s in range(2):
                        for f in range(6):
                            reduce(0, s, f)
                if bo is not None:
                    nc.vector.tensor_tensor(xn[:, :, :], xn[:, :, :], bo[:, :, :].to_broadcast([P, NTILE, C]),
                                            ALU.add).then_inc(s_bias, 1)
                    ve.wait_ge(s_bias, 1)
                for s in range(4):
                    slot(0, s, prev=False)
                with ve.Fori(1, NU // 4 - 1) as k:
                    for s in range(4):
                        slot(k, s)
                for s in range(4):
                    slot(NU // 4 - 1, s, fills=softmax and s < 2)
                normalise(NU // 4 - 1, 3)
                add_residual(NB - 1)
                row_stats(NB - 1)
                merge_stats(nc, ve, stats, bns, s_bn, s_ag)

            @block.scalar
            def _(act):
                def copy_max(n, s):
                    act.wait_ge(s_mT, n + 1)
                    nc.scalar.activation(mT[:, s % 2, :], ps_m[0:48, 0:64].bitcast(BF16), ACT.Copy).then_inc(s_mTc, 1)

                def copy_att(b):
                    act.wait_ge(s_aT, b + 1)
                    after(act, s_o, b)
                    nc.scalar.activation(attT[:, :, :], ps_m[:, 0:2 * P].rearrange("p (t c) -> p t c", t=2),
                                         ACT.Copy).then_inc(s_aTc, 1)

                def copy_out(w, s):
                    act.wait_ge(s_pv, 3 * w + 3)
                    after(act, s_tp, w - 1)
                    nc.scalar.activation(outT[:, s % 2, :, :], ps_pv[:, :].rearrange("p (i q) -> p i q", i=2),
                                         ACT.Copy).then_inc(s_ev, 1)

                def copy_vsum(b, par):
                    act.wait_ge(s_vs, b + 1)
                    after(act, s_on, 2 * b - 2)
                    nc.scalar.activation(vsum[:, par, :, :, :].rearrange("p t h d -> p (t h d)"), ps_m[:, 0:2 * H * HV],
                                         ACT.Copy).then_inc(s_vsc, 1)

                def take_v(b, par):
                    settled(act, s_pv, 6 * b - 6, s_gate_act)
                    nc.scalar.activation(v_now[:, par, :, :, 0:HV], v_all[:, bass.ds(2 * b, 2), :, :], ACT.Copy).then_inc(s_vn, 1)

                def slot(k, s, tr=softmax, prev=True, more=True):
                    b = 2 * k + s // 2
                    for j in range(3):
                        r = 12 * k + 3 * s + j
                        act.wait_ge(s_b, r + 1)
                        after(act, s_pv, r - 5)
                        nc.scalar.activation(prob[:, (3 * s + j) % 6, :], ps_b[(3 * s + j) % 2][:, :],
                                             ACT.Exp if softmax else ACT.Square, scale=scale,
                                             bias=0.0 if softmax else 1.0).then_inc(s_e, 1)
                        if j == 1 and (prev or s > 0):
                            copy_out(4 * k + s - 1, (s - 1) % 4)
                        if j == 0 and tr:
                            copy_max(4 * k + s + 1, s + 1)
                        if j == 0 and not softmax and s % 2 == 0:
                            copy_vsum(b, s // 2)
                        if j == 1 and s % 2 == 1 and (prev or s > 1):
                            copy_att(b - 1)
                        if j == 2 and s % 2 == 1 and more:
                            take_v(b + 1, (s // 2 + 1) % 2)

                act.wait_ge(s_vz, 1)
                take_v(0, 0)
                if softmax:
                    copy_max(0, 0)
                for s in range(4):
                    slot(0, s, prev=False)
                with act.Fori(1, NU // 4 - 1) as k:
                    for s in range(4):
                        slot(k, s)
                for s in range(4):
                    slot(NU // 4 - 1, s, tr=softmax and s < 3, more=s < 3)
                copy_out(NU - 1, 3)
                copy_att(NB - 1)

            @block.gpsimd
            def _(pool):
                def mask(k, s, j):
                    r = 12 * k + 3 * s + j
                    settled(pool, s_e, r + 1, s_gate_pool)
                    reg = prob[:, (3 * s + j) % 6, :]
                    if j < 2:
                        blk, n = reg.rearrange("p (h q) -> p h q", h=4)[:, :, 0:P], 4
                    else:
                        blk, n = reg.rearrange("p (h q) -> p h q", h=8), 8
                    nc.gpsimd.affine_select(out=blk, in_=blk, compare_op=ALU.is_ge, fill=0.0, base=0,
                                            pattern=[[0, n], [1, P]], channel_multiplier=-1).then_inc(s_k, 1)

                def split_max(n, s):
                    after(pool, s_mT, n - 1)
                    settled(pool, s_mx, 6 * n + 6, s_gate_pool)
                    m = mx[:, s % 2, :, :].rearrange("p h q -> p (h q)")
                    nc.gpsimd.tensor_copy(mparts[:, s % 2, 0, :], m).then_inc(s_mh, 1)
                    pool.wait_ge(s_mh, n + 1)
                    nc.gpsimd.tensor_tensor(mres[:, s % 2, :], m, mparts[:, s % 2, 0, :], ALU.subtract).then_inc(s_mr, 1)
                    settled(pool, s_mr, n + 1, s_gate_pool)
                    nc.gpsimd.tensor_copy(mparts[:, s % 2, 1, :], mres[:, s % 2, :]).then_inc(s_mm, 1)
                    pool.wait_ge(s_mm, n + 1)
                    nc.gpsimd.tensor_tensor(mparts[:, s % 2, 2, :], mres[:, s % 2, :], mparts[:, s % 2, 1, :],
                                            ALU.subtract).then_inc(s_mp, 1)

                def slot(k, s, fills=softmax):
                    for j in range(3):
                        mask(k, s, j)
                    if fills:
                        split_max(4 * k + s + 2, s)

                if softmax:
                    for s in range(2):
                        split_max(s, s)
                for s in range(4):
                    slot(0, s)
                with pool.Fori(1, NU // 4 - 1) as k:
                    for s in range(4):
                        slot(k, s)
                for s in range(4):
                    slot(NU // 4 - 1, s, fills=softmax and s < 2)


def expert_layer0(nc, xn, stats, norm, consts):
    ident, ident_bf = consts["ident"], consts["ident_bf"]
    with ExitStack() as ctx:
        def sb(name, shape, dt=F32):
            return ctx.enter_context(nc.sbuf_tensor(f"m0_{name}", shape, dt))

        def ps(name, shape, dt=F32):
            return ctx.enter_context(nc.psum_tensor(f"m0_{name}", shape, dt))

        phase = ctx.enter_context(Semaphores(nc))

        def sem(name):
            return phase.take(f"m0_{name}")

        wr, wgu, bgu, wd, bd, sel_f, desc = [consts["later"][n] for n in ("wr", "wgu", "bgu", "wd0", "bd0", "sel", "desc")]
        bup = sb("bup", [P, E])
        wdh = sb("wdh", [P, E, C])
        bdp = sb("bdp", [32, 3, C], BF16)
        bdr = sb("bdr", [32, 2, C])
        sel = sb("sel", [32, E, P], BF16)
        x1_tok = sb("x1_tok", [P, 2, 4, C])
        x1_now = sb("x1_now", [P, 2, CH])
        x1T = sb("x1T", [P, NTOK])
        ra = [sb(f"route{i}", [P, NTILE, E]) for i in range(6)]
        rs = [sb(f"pick{i}", [P, NTILE, 1]) for i in range(8)]
        wt = sb("wt", [P, NTILE, E])
        wtr = sb("wtr", [P, 1, NTILE, E])
        wtp = sb("wtp", [P, NTILE, 32], BF16)
        wt_now = sb("wt_now", [P, 2, 4, 32], BF16)
        wTp = sb("wTp", [32, 2, CH], BF16)
        gate = sb("gate", [P, 2, CH])
        up = sb("up", [P, 2, CH])
        upc = sb("upc", [P, 2, CH])
        th = sb("th", [P, 2, CH])
        prod = sb("prod", [P, 2, CH])
        glu = sb("glu", [P, 2, CH])
        act = sb("act", [P, 2, CH])
        bns = sb("bns", [P, NTILE, 6])
        ps_g = [ps(f"ps_g{i}", [P, CH]) for i in range(2)]
        ps_u = [ps(f"ps_u{i}", [P, CH]) for i in range(2)]
        ps_w = [ps(f"ps_w{i}", [P, CH]) for i in range(2)]
        ps_d = ps("ps_d", [P, CH])
        ps_r = ps("ps_r", [P, CH])
        logits = ps_r[:, 0:NTILE * E].rearrange("p (t e) -> p t e", t=NTILE)

        s_c = sem("constants_ready")
        s_x1 = sem("tile_normalised")
        s_xp = sem("x_transposed")
        s_xT = sem("x_rows_copied")
        s_xk = sem("x_rows_kept")
        s_xb = sem("x_kept")
        s_wn = sem("weights_staged")
        s_lg = sem("logits_ready")
        s_rt = sem("routing_step")
        s_ra = sem("routing_exp_done")
        s_wtp = sem("weights_transposed")
        s_wT = sem("weight_rows_copied")
        s_g = sem("gate_ready")
        s_u = sem("up_ready")
        s_bc = sem("weight_broadcast")
        s_gc = sem("gate_clipped")
        s_uc = sem("up_copied")
        s_ucl = sem("up_clipped")
        s_th = sem("tanh_done")
        s_pr = sem("product_done")
        s_gl = sem("glu_done")
        s_act = sem("activation_weighted")
        s_dn = sem("expert_summed")
        s_y = sem("residual_added")
        s_bn = sem("row_stats_taken")
        s_ag = sem("row_stats_merged")
        s_gate = sem("gate_pool")
        NR = 22

        with nc.Block() as block:
            @block.tensor
            def _(pe):
                def transpose_x(c, u):
                    after(pe, s_xk, c - 1)
                    pe.wait_ge(s_x1, 4 * c + 4)
                    for t in range(4):
                        last = nc.tensor.transpose(ps_w[u][:, t * P:(t + 1) * P], x1_tok[:, u, t, :], ident[:, :])
                    last.then_inc(s_xp, 1)

                def score(c, u):
                    pe.wait_ge(s_xT, c + 1)
                    for t in range(4):
                        last = nc.tensor.matmul(logits[:, bass.ds(4 * c + t, 1), :], x1_now[:, u, t * P:(t + 1) * P], wr[:, :],
                                                start=True, stop=True, skip_group_check=True)
                    last.then_inc(s_lg, 1)

                def transpose_w(c, u):
                    pe.wait_ge(s_wn, c + 1)
                    after(pe, s_wT, c)
                    for t in range(4):
                        last = nc.tensor.transpose(ps_r[0:32, 64 * t:64 * t + 64].bitcast(BF16), wt_now[:, u, t, :], ident_bf[:, :])
                    last.then_inc(s_wtp, 1)

                def expand(c, e):
                    n = E * c + e
                    after(pe, s_gc, n - 1)
                    nc.tensor.matmul(ps_g[e % 2][:, :], wgu[:, e, 0, :], x1T[:, bass.ds(c * CH, CH)], start=True, stop=True).then_inc(s_g, 1)
                    after(pe, s_uc, n - 1)
                    nc.tensor.matmul(ps_u[e % 2][:, :], wgu[:, e, 1, :], x1T[:, bass.ds(c * CH, CH)], start=True, stop=True).then_inc(s_u, 1)

                def broadcast(c, u, e):
                    n = E * c + e
                    after(pe, s_act, n - 1)
                    if e == 0:
                        pe.wait_ge(s_wT, c + 1)
                    nc.tensor.matmul(ps_w[e % 2][:, :], sel[0:32, e, :], wTp[0:32, u, :], start=True, stop=True).then_inc(s_bc, 1)

                def reduce(c, u, e):
                    n = E * c + e
                    if e == 0:
                        after(pe, s_y, c)
                        for t in range(4):
                            for part in range(3):
                                nc.tensor.matmul(ps_d[:, t * P:(t + 1) * P], wTp[0:32, u, t * P:(t + 1) * P], bdp[0:32, part, :],
                                                 start=t == 0 and part == 0, stop=False, skip_group_check=True)
                    pe.wait_ge(s_act, n + 1)
                    for t in range(4):
                        last = nc.tensor.matmul(ps_d[:, t * P:(t + 1) * P], act[:, e % 2, t * P:(t + 1) * P], wdh[:, e, :],
                                                start=False, stop=e == E - 1, skip_group_check=True)
                    last.then_inc(s_dn, 1)

                def chunk(c, u, prev=True, nxt=True):
                    for e in range(E):
                        if prev or e >= 2:
                            expand(c, e)
                        broadcast(c, u, e)
                        if e >= 2:
                            reduce(c, u, e - 2)
                        elif prev:
                            reduce(c - 1, 1 - u, E + e - 2)
                        if nxt and e == 4:
                            transpose_w(c + 1, 1 - u)

                transpose_x(0, 0)
                transpose_x(1, 1)
                score(0, 0)
                score(1, 1)
                with pe.Fori(1, NCH // 2) as k:
                    for u in range(2):
                        transpose_x(2 * k + u, u)
                    for u in range(2):
                        score(2 * k + u, u)
                pe.wait_ge(s_xk, NCH)
                for e in range(2):
                    expand(0, e)
                pe.wait_ge(s_c, 9)
                transpose_w(0, 0)
                chunk(0, 0, prev=False)
                chunk(1, 1)
                with pe.Fori(1, NCH // 2 - 1) as k:
                    for u in range(2):
                        chunk(2 * k + u, u)
                chunk(NCH - 2, 0)
                chunk(NCH - 1, 1, nxt=False)
                for e in (E - 2, E - 1):
                    reduce(NCH - 1, 1, e)

            @block.vector
            def _(ve):
                nc.vector.memset(wtp[:, :, :], 0.0).then_inc(s_c, 1)
                def normalise(c, u):
                    after(ve, s_xp, c - 1)
                    after(ve, s_xb, c - 1)
                    for t in range(4):
                        nc.vector.tensor_scalar(x1_tok[:, u, t, :], xn[:, bass.ds(4 * c + t, 1), :],
                                                stats[:, bass.ds(4 * c + t, 1), 0:1], norm.rstd[:, bass.ds(4 * c + t, 1)],
                                                ALU.subtract, ALU.mult).then_inc(s_x1, 1)
                    ve.wait_ge(s_x1, 4 * c + 4)
                    nc.vector.tensor_scalar(xn[:, bass.ds(4 * c, 4), :], x1_tok[:, u, :, :], 1.0, None, ALU.mult).then_inc(s_xb, 1)

                def route():
                    done = [0]

                    def step(ins):
                        done[0] += 1
                        ins.then_inc(s_rt, 1)
                        ve.wait_ge(s_rt, done[0])

                    def wide(x):
                        return x[:, :, :].to_broadcast([P, NTILE, E])

                    order = desc[:, :].rearrange("p (o e) -> p o e", o=1).to_broadcast([P, NTILE, E])
                    m1, k1, m2, k2, d, s, r, p2 = rs
                    ve.wait_ge(s_lg, NCH)
                    step(nc.vector.reduce_max(m1[:, :, :], logits, AX_X))
                    step(nc.vector.tensor_tensor(ra[0][:, :, :], logits, wide(m1), ALU.is_ge))
                    step(nc.vector.tensor_tensor(ra[0][:, :, :], ra[0][:, :, :], order, ALU.mult))
                    step(nc.vector.reduce_max(k1[:, :, :], ra[0][:, :, :], AX_X))
                    step(nc.vector.tensor_tensor(ra[1][:, :, :], ra[0][:, :, :], wide(k1), ALU.is_equal))
                    step(nc.vector.scalar_tensor_tensor(ra[2][:, :, :], ra[1][:, :, :], -BIG, logits, ALU.mult, ALU.add))
                    step(nc.vector.reduce_max(m2[:, :, :], ra[2][:, :, :], AX_X))
                    step(nc.vector.tensor_tensor(d[:, :, :], m2[:, :, :], m1[:, :, :], ALU.subtract))
                    step(nc.vector.tensor_tensor(ra[3][:, :, :], ra[2][:, :, :], wide(m2), ALU.is_ge))
                    step(nc.vector.tensor_tensor(ra[3][:, :, :], ra[3][:, :, :], order, ALU.mult))
                    step(nc.vector.reduce_max(k2[:, :, :], ra[3][:, :, :], AX_X))
                    step(nc.vector.tensor_tensor(ra[4][:, :, :], ra[3][:, :, :], wide(k2), ALU.is_equal))
                    ve.wait_ge(s_ra, 1)
                    step(nc.vector.tensor_scalar(s[:, :, :], d[:, :, :], 1.0, None, ALU.add))
                    step(nc.vector.reciprocal(r[:, :, :], s[:, :, :]))
                    step(nc.vector.tensor_tensor(p2[:, :, :], d[:, :, :], r[:, :, :], ALU.mult))
                    step(nc.vector.tensor_tensor(ra[5][:, :, :], ra[1][:, :, :], wide(r), ALU.mult))
                    step(nc.vector.tensor_tensor(ra[4][:, :, :], ra[4][:, :, :], wide(p2), ALU.mult))
                    step(nc.vector.tensor_tensor(wt[:, :, :], ra[5][:, :, :], ra[4][:, :, :], ALU.add))
                    step(nc.vector.tensor_copy(wtp[:, :, 0:E], wt[:, :, :]))
                    step(nc.vector.tensor_tensor(wtr[:, 0, :, :], wt[:, :, :], wtp[:, :, 0:E], ALU.subtract))
                    step(nc.vector.tensor_copy(wtp[:, :, E:2 * E], wtr[:, 0, :, :]))
                    step(nc.vector.tensor_tensor(wtp[:, :, 2 * E:3 * E], wtr[:, 0, :, :], wtp[:, :, E:2 * E], ALU.subtract))
                    assert done[0] == NR

                def clip(c, e):
                    n = E * c + e
                    ve.wait_ge(s_g, n + 1)
                    after(ve, s_gl, n - 1)
                    nc.vector.tensor_scalar(gate[:, e % 2, :], ps_g[e % 2][:, :], bgu[:, e, 0:1], LIMIT, ALU.add, ALU.min)\
                        .then_inc(s_gc, 1)
                    ve.wait_ge(s_uc, n + 1)
                    nc.vector.tensor_scalar(upc[:, e % 2, :], up[:, e % 2, :], LIMIT + 1.0, 1.0 - LIMIT, ALU.min, ALU.max)\
                        .then_inc(s_ucl, 1)

                def weigh(c, e):
                    n = E * c + e
                    ve.wait_ge(s_th, n + 1)
                    ve.wait_ge(s_pr, n + 1)
                    nc.vector.scalar_tensor_tensor(glu[:, e % 2, :], th[:, e % 2, :], 1.0, prod[:, e % 2, :],
                                                   ALU.add, ALU.mult).then_inc(s_gl, 1)
                    ve.wait_ge(s_gl, n + 1)
                    ve.wait_ge(s_bc, n + 1)
                    after(ve, s_dn, n - 1)
                    nc.vector.tensor_tensor(act[:, e % 2, :], ps_w[e % 2][:, :], glu[:, e % 2, :], ALU.mult).then_inc(s_act, 1)

                def add_residual(c):
                    ve.wait_ge(s_dn, E * c + E)
                    nc.vector.tensor_tensor(xn[:, bass.ds(4 * c, 4), :], ps_d[:, :].rearrange("p (t c) -> p t c", t=4),
                                            xn[:, bass.ds(4 * c, 4), :], ALU.add).then_inc(s_y, 1)

                def row_stats(c):
                    ve.wait_ge(s_c, 9)
                    ve.wait_ge(s_y, c + 1)
                    for t in range(4):
                        nc.vector.bn_stats(bns[:, bass.ds(4 * c + t, 1), :], xn[:, bass.ds(4 * c + t, 1), :]).then_inc(s_bn, 1)

                def chunk(c, prev=True):
                    for e in range(E):
                        if e == 2 and prev:
                            add_residual(c - 1)
                        clip(c, e)
                        if e >= 1:
                            weigh(c, e - 1)
                        elif prev:
                            weigh(c - 1, E - 1)
                        if e == 2 and prev:
                            row_stats(c - 1)

                for u in range(2):
                    normalise(u, u)
                with ve.Fori(1, NCH // 2) as k:
                    for u in range(2):
                        normalise(2 * k + u, u)
                nc.vector.tensor_scalar(bup[:, :], bgu[:, :, 1], 1.0, None, ALU.add).then_inc(s_c, 1)
                nc.vector.tensor_copy(sel[:, :, :], sel_f[:, :, :]).then_inc(s_c, 1)
                nc.vector.tensor_scalar(wdh[:, :, :], wd[:, :, :], 0.5, None, ALU.mult).then_inc(s_c, 1)
                nc.vector.tensor_copy(bdp[:, 0, :], bd[:, :]).then_inc(s_c, 1)
                ve.wait_ge(s_c, 5)
                nc.vector.tensor_tensor(bdr[:, 0, :], bd[:, :], bdp[:, 0, :], ALU.subtract).then_inc(s_c, 1)
                ve.wait_ge(s_c, 6)
                nc.vector.tensor_copy(bdp[:, 1, :], bdr[:, 0, :]).then_inc(s_c, 1)
                ve.wait_ge(s_c, 7)
                nc.vector.tensor_tensor(bdr[:, 1, :], bdr[:, 0, :], bdp[:, 1, :], ALU.subtract).then_inc(s_c, 1)
                ve.wait_ge(s_c, 8)
                nc.vector.tensor_copy(bdp[:, 2, :], bdr[:, 1, :]).then_inc(s_c, 1)
                ve.wait_ge(s_c, 9)
                ve.wait_ge(s_xb, NCH)
                route()
                chunk(0, prev=False)
                with ve.Fori(1, NCH) as c:
                    chunk(c)
                weigh(NCH - 1, E - 1)
                add_residual(NCH - 1)
                row_stats(NCH - 1)
                merge_stats(nc, ve, stats, bns, s_bn, s_ag)

            @block.scalar
            def _(act_e):
                def copy_x(c, u):
                    act_e.wait_ge(s_xp, c + 1)
                    after(act_e, s_lg, c - 1)
                    nc.scalar.activation(x1_now[:, u, :], ps_w[u][:, :], ACT.Copy).then_inc(s_xT, 1)
                    nc.scalar.activation(x1T[:, bass.ds(c * CH, CH)], ps_w[u][:, :], ACT.Copy).then_inc(s_xk, 1)

                def copy_w(c, u):
                    act_e.wait_ge(s_wtp, c + 1)
                    nc.scalar.activation(wTp[:, u, :], ps_r[0:32, 0:CH // 2].bitcast(BF16), ACT.Copy).then_inc(s_wT, 1)

                def expert(c, e):
                    n = E * c + e
                    act_e.wait_ge(s_u, n + 1)
                    after(act_e, s_ucl, n - 1)
                    nc.scalar.activation(up[:, e % 2, :], ps_u[e % 2][:, :], ACT.Identity, bias=bup[:, e:e + 1]).then_inc(s_uc, 1)
                    act_e.wait_ge(s_gc, n + 1)
                    after(act_e, s_gl, n - 1)
                    nc.scalar.activation(th[:, e % 2, :], gate[:, e % 2, :], ACT.Tanh, scale=ALPHA / 2).then_inc(s_th, 1)

                def chunk(c, u, nxt=True):
                    for e in range(E):
                        expert(c, e)
                        if nxt and e == 4:
                            copy_w(c + 1, 1 - u)

                for u in range(2):
                    copy_x(u, u)
                with act_e.Fori(1, NCH // 2) as k:
                    for u in range(2):
                        copy_x(2 * k + u, u)
                act_e.wait_ge(s_rt, 8)
                nc.scalar.activation(rs[4][:, :, :], rs[4][:, :, :], ACT.Exp).then_inc(s_ra, 1)
                act_e.wait_ge(s_c, 9)
                copy_w(0, 0)
                chunk(0, 0)
                chunk(1, 1)
                with act_e.Fori(1, NCH // 2 - 1) as k:
                    for u in range(2):
                        chunk(2 * k + u, u)
                chunk(NCH - 2, 0)
                chunk(NCH - 1, 1, nxt=False)

            @block.gpsimd
            def _(pool):
                def product(n, e):
                    after(pool, s_gl, n - 1)
                    pool.wait_ge(s_ucl, n + 1)
                    nc.gpsimd.tensor_tensor(prod[:, e % 2, :], upc[:, e % 2, :], gate[:, e % 2, :], ALU.mult).then_inc(s_pr, 1)

                def stage_w(c, u):
                    settled(pool, s_wtp, c - 1, s_gate)
                    nc.gpsimd.tensor_copy(wt_now[:, u, :, :], wtp[:, bass.ds(4 * c, 4), :]).then_inc(s_wn, 1)

                def chunk(c, u, nxt=True):
                    for e in range(E):
                        product(E * c + e, e)
                        if nxt and e == 2:
                            stage_w(c + 1, 1 - u)

                pool.wait_ge(s_rt, NR)
                stage_w(0, 0)
                chunk(0, 0)
                chunk(1, 1)
                with pool.Fori(1, NCH // 2 - 1) as k:
                    for u in range(2):
                        chunk(2 * k + u, u)
                chunk(NCH - 2, 0)
                chunk(NCH - 1, 1, nxt=False)


def layer1_attention(nc, io, xn, stats, norm, consts):
    scratch = [nc.dram_tensor(f"scratch1_{n}", [NCH, NPART, 2 * P, CH], BF16, kind="Internal").ap() for n in "qk"]
    with ExitStack() as keep:
        v_all = keep.enter_context(nc.sbuf_tensor("v_all1", [P, NTILE, H, HV], F32))
        stacks = [keep.enter_context(nc.sbuf_tensor(f"{n}st1", [P, 4, UH, T], BF16)) for n in "qk"]
        wo = consts["later"]["wo1"]
        project_layer1(nc, scratch, v_all, xn, stats, norm, consts)
        attend(nc, io, "a1", stacks, scratch, 6 * FD, v_all, xn, stats, consts, wo, None, softmax=False)


def project_layer1(nc, scratch, v_all, xn, stats, norm, consts):
    ident = consts["ident"]
    with ExitStack() as ctx:
        def sb(name, shape, dt=F32):
            return ctx.enter_context(nc.sbuf_tensor(f"p1_{name}", shape, dt))

        def ps(name, shape, dt=F32):
            return ctx.enter_context(nc.psum_tensor(f"p1_{name}", shape, dt))

        phase = ctx.enter_context(Semaphores(nc))

        def sem(name):
            return phase.take(f"p1_{name}")

        wqk, wv = consts["later"]["wqk1"], consts["later"]["wv1"]
        x2 = sb("x2", [P, 2, 4, C])
        x2T = sb("x2T", [P, 2, CH])
        resid = sb("resid", [P, 2, CH])
        parts = sb("parts", [P, 8, 3, CH], BF16)
        ps_qk = [ps(f"ps_qk{i}", [P, CH]) for i in range(4)]
        ps_x = [ps(f"ps_x{i}", [P, CH]) for i in range(2)]
        ps_v = ps("ps_v", [P, CH])

        s_ones = sem("ones_set")
        s_x2 = sem("tile_normalised")
        s_back = sem("x2_kept")
        s_xp = sem("x_transposed")
        s_xT = sem("x_rows_copied")
        s_proj = sem("qk_projected")
        s_hi = sem("hi_done")
        s_r1 = sem("residual_done")
        s_mid = sem("mid_done")
        s_lo = sem("lo_done")
        s_store = [sem(f"parts_stored{i}") for i in range(8)]
        s_vp = sem("v_projected")
        s_vc = sem("v_copied")

        with nc.Block() as block:
            @block.sync
            def _(sp):
                def store(c, u):
                    for i in range(4):
                        sp.wait_ge(s_lo, 4 * c + i + 1)
                        src = parts[:, 4 * u + i, :, :]
                        half = P * (i % 2)
                        dst = scratch[i // 2][bass.ds(c, 1), :, half:half + P, :].rearrange("c s p t -> p (c s) t")
                        sp.dma_start(dst, src).then_inc(s_store[4 * u + i], 16)

                with sp.Fori(0, NCH // 2) as k:
                    for u in range(2):
                        store(2 * k + u, u)
                for n in range(8):
                    sp.wait_ge(s_store[n], 16 * (NCH // 2))

            @block.tensor
            def _(pe):
                def turn(c, u):
                    pe.wait_ge(s_x2, 4 * c + 4)
                    after(pe, s_xT, c - 1)
                    for t in range(4):
                        last = nc.tensor.transpose(ps_x[u][:, t * P:(t + 1) * P], x2[:, u, t, :], ident[:, :])
                    last.then_inc(s_xp, 1)

                def chunk(c, u, more=True):
                    if more:
                        turn(c + 1, 1 - u)
                    pe.wait_ge(s_xT, c + 1)
                    for i in range(4):
                        after(pe, s_r1, 4 * c + i - 3)
                        nc.tensor.matmul(ps_qk[i][:, :], wqk[:, i, :], x2T[:, u, :], start=True, stop=True).then_inc(s_proj, 1)
                    after(pe, s_vc, c)
                    for t in range(4):
                        last = nc.tensor.matmul(ps_v[:, t * P:(t + 1) * P], x2T[:, u, t * P:(t + 1) * P], wv[:, :],
                                                start=True, stop=True)
                    last.then_inc(s_vp, 1)

                turn(0, 0)
                for u in range(2):
                    chunk(u, u)
                with pe.Fori(1, NCH // 2 - 1) as k:
                    for u in range(2):
                        chunk(2 * k + u, u)
                chunk(NCH - 2, 0)
                chunk(NCH - 1, 1, more=False)

            @block.vector
            def _(ve):
                nc.vector.memset(v_all[:, :, :, HD:HV], 1.0).then_inc(s_ones, 1)

                def normalise(c, u):
                    after(ve, s_xp, c - 1)
                    after(ve, s_back, c - 1)
                    for t in range(4):
                        nc.vector.tensor_scalar(x2[:, u, t, :], xn[:, bass.ds(4 * c + t, 1), :],
                                                stats[:, bass.ds(4 * c + t, 1), 0:1], norm.rstd[:, bass.ds(4 * c + t, 1)],
                                                ALU.subtract, ALU.mult).then_inc(s_x2, 1)
                    ve.wait_ge(s_x2, 4 * c + 4)
                    nc.vector.tensor_scalar(xn[:, bass.ds(4 * c, 4), :], x2[:, u, :, :], 1.0, None, ALU.mult).then_inc(s_back, 1)

                def residuals(c, u):
                    for i in range(4):
                        n = 4 * c + i
                        ve.wait_ge(s_hi, n + 1)
                        after(ve, s_lo, n - 1)
                        nc.vector.tensor_tensor(resid[:, i % 2, :], ps_qk[i][:, :], parts[:, 4 * u + i, PART_ORDER[i // 2][0], :],
                                                ALU.subtract).then_inc(s_r1, 1)

                for u in range(2):
                    normalise(u, u)
                for u in range(2):
                    normalise(2 + u, u)
                    residuals(u, u)
                with ve.Fori(2, NCH // 2) as k:
                    for u in range(2):
                        normalise(2 * k + u, u)
                        residuals(2 * k + u - 2, u)
                for u in range(2):
                    residuals(NCH - 2 + u, u)

            @block.scalar
            def _(act):
                act.wait_ge(s_ones, 1)

                def copy_x(c, u):
                    act.wait_ge(s_xp, c + 1)
                    after(act, s_vp, c - 1)
                    nc.scalar.activation(x2T[:, u, :], ps_x[u][:, :], ACT.Copy).then_inc(s_xT, 1)

                def chunk(c, k, u, more=True):
                    for i in range(5):
                        n = 4 * c + i
                        if i < 4:
                            act.wait_ge(s_proj, n + 1)
                            after(act, s_store[4 * u + i], 16 * k)
                            nc.scalar.activation(parts[:, 4 * u + i, PART_ORDER[i // 2][0], :], ps_qk[i][:, :], ACT.Copy).then_inc(s_hi, 1)
                        if i == 1 and more:
                            copy_x(c + 1, 1 - u)
                        if i > 0:
                            act.wait_ge(s_r1, n)
                            nc.scalar.activation(parts[:, 4 * u + i - 1, PART_ORDER[(i - 1) // 2][1], :],
                                                 resid[:, (i - 1) % 2, :], ACT.Copy).then_inc(s_mid, 1)
                    act.wait_ge(s_vp, c + 1)
                    nc.scalar.activation(v_all[:, bass.ds(4 * c, 4), :, 0:HD],
                                         ps_v[:, :].rearrange("p (t h d) -> p t h d", t=4, h=H), ACT.Copy).then_inc(s_vc, 1)

                copy_x(0, 0)
                for u in range(2):
                    chunk(u, 0, u)
                with act.Fori(1, NCH // 2 - 1) as k:
                    for u in range(2):
                        chunk(2 * k + u, k, u)
                for u in range(2):
                    chunk(NCH - 2 + u, NCH // 2 - 1, u, more=u == 0)

            @block.gpsimd
            def _(pool):
                def chunk(c, u):
                    for i in range(4):
                        pool.wait_ge(s_mid, 4 * c + i + 1)
                        nc.gpsimd.tensor_tensor(parts[:, 4 * u + i, PART_ORDER[i // 2][2], :], resid[:, i % 2, :],
                                                parts[:, 4 * u + i, PART_ORDER[i // 2][1], :],
                                                ALU.subtract).then_inc(s_lo, 1)

                for u in range(2):
                    chunk(u, u)
                with pool.Fori(1, NCH // 2) as k:
                    for u in range(2):
                        chunk(2 * k + u, u)


def score_tokens(nc, xn, stats, stats_y, norm, gate_act, consts):
    ident = consts["ident"]
    with ExitStack() as ctx:
        def sb(name, shape, dt=F32):
            return ctx.enter_context(nc.sbuf_tensor(f"g_{name}", shape, dt))

        phase = ctx.enter_context(Semaphores(nc))

        def sem(name):
            return phase.take(f"g_{name}")

        wg = consts["later"]["wg1"]
        x3 = sb("x3", [P, 2, 4, C])
        x3T = sb("x3T", [P, 2, CH])
        bns = sb("bns", [P, NTILE, 6])
        ps_x = [ctx.enter_context(nc.psum_tensor(f"g_ps_x{i}", [P, CH], F32)) for i in range(2)]
        ps_s = [ctx.enter_context(nc.psum_tensor(f"g_ps_s{i}", [P, CH], F32)) for i in range(2)]
        s_x3 = sem("tile_normalised")
        s_back = sem("x3_kept")
        s_xp = sem("x_transposed")
        s_xT = sem("x_rows_copied")
        s_sc = sem("scores_ready")
        s_th = sem("tanh_done")
        s_bn = sem("row_stats_taken")
        s_ag = sem("row_stats_merged")
        with nc.Block() as block:
            @block.tensor
            def _(pe):

                def chunk(c, u):
                    pe.wait_ge(s_x3, 4 * c + 4)
                    after(pe, s_xT, c - 1)
                    for t in range(4):
                        last = nc.tensor.transpose(ps_x[u][:, t * P:(t + 1) * P], x3[:, u, t, :], ident[:, :])
                    last.then_inc(s_xp, 1)

                def score(c, u):
                    pe.wait_ge(s_xT, c + 1)
                    after(pe, s_th, c - 1)
                    for t in range(4):
                        last = nc.tensor.matmul(ps_s[u][:, t * E:(t + 1) * E], x3T[:, u, t * P:(t + 1) * P], wg[:, :],
                                                start=True, stop=True)
                    last.then_inc(s_sc, 1)

                chunk(0, 0)
                chunk(1, 1)
                score(0, 0)
                with pe.Fori(1, NCH // 2) as k:
                    for u in range(2):
                        chunk(2 * k + u, u)
                        score(2 * k + u - 1, 1 - u)
                score(NCH - 1, 1)

            @block.vector
            def _(ve):

                def chunk(c, u):
                    after(ve, s_xp, c - 1)
                    after(ve, s_back, c - 1)
                    for t in range(4):
                        nc.vector.tensor_scalar(x3[:, u, t, :], xn[:, bass.ds(4 * c + t, 1), :],
                                                stats[:, bass.ds(4 * c + t, 1), 0:1], norm.rstd[:, bass.ds(4 * c + t, 1)],
                                                ALU.subtract, ALU.mult).then_inc(s_x3, 1)
                    ve.wait_ge(s_x3, 4 * c + 4)
                    nc.vector.tensor_scalar(xn[:, bass.ds(4 * c, 4), :], x3[:, u, :, :], 1.0, None, ALU.mult).then_inc(s_back, 1)
                    for t in range(4):
                        nc.vector.bn_stats(bns[:, bass.ds(4 * c + t, 1), :], x3[:, u, t, :]).then_inc(s_bn, 1)

                for u in range(2):
                    chunk(u, u)
                with ve.Fori(1, NCH // 2) as k:
                    for u in range(2):
                        chunk(2 * k + u, u)
                merge_stats(nc, ve, stats_y, bns, s_bn, s_ag)

            @block.scalar
            def _(act):
                def chunk(c, u):
                    act.wait_ge(s_xp, c + 1)
                    after(act, s_sc, c - 1)
                    nc.scalar.activation(x3T[:, u, :], ps_x[u][:, :], ACT.Copy).then_inc(s_xT, 1)
                    act.wait_ge(s_sc, c + 1)
                    nc.scalar.activation(gate_act[:, :, bass.ds(4 * c, 4)],
                                         ps_s[u][:, 0:4 * E].rearrange("p (t e) -> p e t", t=4), ACT.Tanh).then_inc(s_th, 1)

                chunk(0, 0)
                chunk(1, 1)
                with act.Fori(1, NCH // 2) as k:
                    for u in range(2):
                        chunk(2 * k + u, u)


def choose_tokens(nc, io, xn, stats_y, norm_y, gate_act, picked, kept, w1, sum_d, norm_d, consts):
    ident, upper, ones_sq = consts["ident"], consts["upper"], consts["ones_sq"]
    NT, NV = NTILE, 5
    SHARE = 24
    with ExitStack() as ctx:
        def sb(name, shape, dt=F32):
            return ctx.enter_context(nc.sbuf_tensor(f"c_{name}", shape, dt))

        phase = ctx.enter_context(Semaphores(nc))

        def sem(name):
            return phase.take(f"c_{name}")

        score = sb("score", [P, E, NT])
        hit = sb("hit", [P, 3, E, NT])
        more = sb("more", [P, E, NT])
        equal = sb("equal", [P, E, NT])
        sel = sb("sel", [P, E, NT])
        pos = sb("pos", [P, E, NT])
        total = sb("total", [P, E, NT])
        running = sb("running", [P, E, NT])
        quarter = sb("quarter", [P, E, NT])
        in_q = [sb(f"in_q{i}", [P, E, NT]) for i in range(4)]
        wpart = [sb(f"wpart{i}", [P, E, NT], BF16) for i in range(3)]
        wres = sb("wres", [P, E, NT])
        vals = sb("vals", [P, E, NT, NV, 4], BF16)
        onehot = sb("onehot", [P, 2, NT, P], BF16)
        far = sb("far", [P, NT - SHARE, P])
        iota, tile0, not0, row = [consts["later"][n] for n in ("iota", "tile0", "not0", "row")]
        strict = sb("strict", [P, P])
        count, cand, held = [sb(n, [P, 3, E, 1]) for n in ("count", "cand", "held")]
        ahead = sb("ahead", [P, 3, 1])
        thr, best, need = [sb(n, [P, E, 1]) for n in ("thr", "best", "need")]
        found = sb("found", [P, E, NV, 4])
        yn = sb("yn", [P, NT, C])
        twice = sb("twice", [P, NT, C])
        nought = sb("nought", [P, 1, C])
        ps_c = ctx.enter_context(nc.psum_tensor("c_ps_c", [P, 512], F32))
        ps_p = ctx.enter_context(nc.psum_tensor("c_ps_p", [P, 512], F32))
        ps_t = ctx.enter_context(nc.psum_tensor("c_ps_t", [P, 512], F32))
        ps_f = ctx.enter_context(nc.psum_tensor("c_ps_f", [P, 512], F32))
        tot = ps_c[:, 0:3 * E].rearrange("p (j e o) -> p j e o", j=3, o=1)
        before = ps_p[:, 0:E * NT].rearrange("p (e t) -> p e t", e=E)
        tiles = ps_t[:, 0:E * NT].rearrange("p (e t) -> p e t", e=E)
        hits = ps_f[:, 0:E * NV * 4].rearrange("p (e v a) -> p e v a", e=E, v=NV)

        s_st = sem("vector_step")
        s_cnt = sem("rows_counted")
        s_tot = sem("tokens_counted")
        s_src = sem("flags_ready")
        s_pre = sem("prefixes_ready")
        s_oh = sem("onehot_ready")
        s_ohp = sem("onehot_rest_ready")
        s_pos = sem("positions_ready")
        s_far = sem("distances_ready")
        s_used = sem("onehot_used")
        s_y = sem("tile_normalised")
        s_two = sem("x3_doubled")
        s_w1 = sem("expert_weights_loaded")
        s_d = sem("rows_stored")

        def flat(x):
            return x[:, :, :].rearrange("p e t -> p (e t)")

        with nc.Block() as block:
            @block.sync
            def _(sp):
                for e in range(2):
                    sp.dma_start(w1[:, e, :], io["w1"][e, :, :]).then_inc(s_w1, 16)
                sp.wait_ge(s_two, 2)
                sp.dma_start(sum_d[1].rearrange("(t p) c -> p t c", p=P), nought[:, :, :].to_broadcast([P, NT, C])).then_inc(s_d, 16)
                sp.dma_start(sum_d[0].rearrange("(t p) c -> p t c", p=P), twice[:, :, :]).then_inc(s_d, 16)
                sp.wait_ge(s_y, NT)
                sp.dma_start(norm_d.rearrange("(t p) c -> p t c", p=P), yn[:, :, :]).then_inc(s_d, 16)
                sp.wait_ge(s_d, 48)
                sp.wait_ge(s_w1, 32)

            @block.scalar
            def _(act):
                nc.scalar.activation(nought[:, 0, :], xn[:, 0, :], ACT.Copy, scale=0.0).then_inc(s_two, 1)
                nc.scalar.activation(twice[:, :, :], xn[:, :, :], ACT.Copy, scale=2.0).then_inc(s_two, 1)
                act.wait_ge(s_pos, 1)
                for e in range(E):
                    after(act, s_ohp, e)
                    for t in range(SHARE, NT):
                        last = nc.scalar.activation(far[:, t - SHARE, :], iota[:, :], ACT.Square, scale=-1.0,
                                                    bias=pos[:, e, t:t + 1])
                    last.then_inc(s_far, 1)
                    act.wait_ge(s_far, e + 1)
                    after(act, s_used, e - 1)
                    nc.scalar.activation(onehot[:, e % 2, SHARE:NT, :], far[:, :, :], ACT.Relu, scale=-1.0,
                                         bias=1.0).then_inc(s_ohp, 1)

            @block.gpsimd
            def _(pool):
                for t in range(NT):
                    nc.gpsimd.tensor_scalar(yn[:, t, :], xn[:, t, :], stats_y[:, t, 0:1], norm_y.rstd[:, t:t + 1],
                                            ALU.subtract, ALU.mult).then_inc(s_y, 1)

            @block.tensor
            def _(pe):
                def total_counts(i):
                    pe.wait_ge(s_cnt, i + 1)
                    nc.tensor.matmul(ps_c[:, 0:3 * E], ones_sq[:, :], count[:, :, :, :].rearrange("p j e o -> p (j e o)"),
                                     start=True, stop=True).then_inc(s_tot, 1)

                with pe.Fori(0, ROUNDS) as i:
                    total_counts(i)
                total_counts(ROUNDS)
                for n, src in enumerate((equal, sel)):
                    pe.wait_ge(s_src, n + 1)
                    nc.tensor.matmul(ps_t[:, 0:E * NT], ones_sq[:, :], flat(src), start=True, stop=True).then_inc(s_pre, 1)
                    nc.tensor.matmul(ps_p[:, 0:E * NT], strict[:, :], flat(src), start=True, stop=True).then_inc(s_pre, 1)
                for e in range(E):
                    pe.wait_ge(s_oh, e + 1)
                    for t in range(NT):
                        if t == SHARE:
                            pe.wait_ge(s_ohp, e + 1)
                        last = nc.tensor.matmul(hits[:, e, :, :], onehot[:, e % 2, t, :], vals[:, e, t, :, :],
                                                start=e == 0 and t == 0, stop=t == NT - 1, skip_group_check=True)
                    last.then_inc(s_used, 1)

            @block.vector
            def _(ve):
                done = [0]

                def step(ins):
                    done[0] += 1
                    ins.then_inc(s_st, 1)
                    ve.wait_ge(s_st, done[0])

                def side(ins):
                    done[0] += 1
                    ins.then_inc(s_st, 1)

                def wide(x):
                    return x[:, :, :].to_broadcast([P, E, NT])


                v = nc.vector
                step(v.tensor_scalar(score[:, :, :], gate_act[:, :, :], 1.0, 0.5, ALU.add, ALU.mult))
                step(v.memset(thr[:, :, :], 0.0))
                for j in range(3):
                    step(v.memset(ahead[:, j, :], 0.5 * (j + 1)))
                step(v.tensor_tensor(strict[:, :], upper[:, :], ident[:, :], ALU.subtract))
                base0, per = done[0], 6
                def search_round(i):
                    n = [0]

                    def bit(ins):
                        n[0] += 1
                        ins.then_inc(s_st, 1)
                        ve.wait_ge(s_st, per * i + (base0 + n[0]))

                    for j in range(3):
                        last = v.tensor_scalar(cand[:, j, :, :], thr[:, :, :], ahead[:, j, :], None, ALU.add)
                    bit(last)
                    for j in range(3):
                        last = v.tensor_tensor(hit[:, j, :, :], score[:, :, :], wide(cand[:, j, :, :]), ALU.is_ge)
                    bit(last)
                    v.reduce_sum(count[:, :, :, :].rearrange("p j e o -> p (j e) o"),
                                 hit[:, :, :, :].rearrange("p j e t -> p (j e) t"), AX_X).then_inc(s_cnt, 1)
                    bit(v.tensor_scalar(ahead[:, :, :], ahead[:, :, :], 0.25, None, ALU.mult))
                    ve.wait_ge(s_tot, i + 1)
                    bit(v.scalar_tensor_tensor(held[:, :, :, :], tot, CAP - 0.5, cand[:, :, :, :], ALU.is_ge, ALU.mult))
                    bit(v.reduce_max(best[:, :, :], held[:, :, :, :].rearrange("p j e o -> p e (j o)"), AX_X))
                    bit(v.tensor_tensor(thr[:, :, :], thr[:, :, :], best[:, :, :], ALU.max))
                    assert n[0] == per

                search_round(0)
                with ve.Fori(0, ROUNDS // 2) as k:
                    for i in range(2):
                        search_round(2 * k + i + 1)
                done[0] = base0 + per * ROUNDS

                step(v.tensor_tensor(more[:, :, :], score[:, :, :], wide(thr), ALU.is_gt))
                v.reduce_sum(count[:, 0, :, :], more[:, :, :], AX_X).then_inc(s_cnt, 1)
                v.tensor_tensor(equal[:, :, :], score[:, :, :], wide(thr), ALU.is_equal).then_inc(s_src, 1)
                ve.wait_ge(s_tot, ROUNDS + 1)
                step(v.tensor_scalar(need[:, :, :], tot[:, 0, :, :], -1.0, float(CAP), ALU.mult, ALU.add))

                def prefix(n):
                    ve.wait_ge(s_pre, 2 * n + 1)
                    step(v.tensor_copy(total[:, :, :], tiles))
                    step(v.tensor_tensor_scan(flat(running), not0[:, :], flat(total), 0.0, ALU.mult, ALU.add))
                    step(v.tensor_tensor(running[:, :, :], running[:, :, :], total[:, :, :], ALU.subtract))
                    ve.wait_ge(s_pre, 2 * n + 2)
                    step(v.tensor_tensor(pos[:, :, :], before, running[:, :, :], ALU.add))

                prefix(0)
                step(v.tensor_tensor(sel[:, :, :], pos[:, :, :], wide(need), ALU.is_lt))
                step(v.tensor_tensor(sel[:, :, :], sel[:, :, :], equal[:, :, :], ALU.mult))
                v.tensor_tensor(sel[:, :, :], sel[:, :, :], more[:, :, :], ALU.add).then_inc(s_src, 1)
                step(v.tensor_copy(wpart[0][:, :, :], score[:, :, :]))
                step(v.tensor_tensor(wres[:, :, :], score[:, :, :], wpart[0][:, :, :], ALU.subtract))
                step(v.tensor_copy(wpart[1][:, :, :], wres[:, :, :]))
                step(v.tensor_tensor(wpart[2][:, :, :], wres[:, :, :], wpart[1][:, :, :], ALU.subtract))
                prefix(1)
                step(v.tensor_scalar(quarter[:, :, :], pos[:, :, :], float(P), None, ALU.is_ge))
                for q in (2, 3):
                    step(v.scalar_tensor_tensor(quarter[:, :, :], pos[:, :, :], float(q * P), quarter[:, :, :], ALU.is_ge, ALU.add))
                for q in range(4):
                    (side if q < 3 else step)(v.scalar_tensor_tensor(in_q[q][:, :, :], quarter[:, :, :], float(q), sel[:, :, :], ALU.is_equal, ALU.mult))
                step(v.scalar_tensor_tensor(pos[:, :, :], quarter[:, :, :], -float(P), pos[:, :, :], ALU.mult, ALU.add))
                for q in range(4):
                    side(v.tensor_tensor(vals[:, :, :, 0, q], in_q[q][:, :, :],
                                         tile0[:, :].rearrange("p (o t) -> p o t", o=1).to_broadcast([P, E, NT]), ALU.mult))
                    side(v.tensor_scalar(vals[:, :, :, 1, q], in_q[q][:, :, :], row[:, 0:1], None, ALU.mult))
                    for i in range(3):
                        (step if (q, i) == (3, 2) else side)(v.tensor_tensor(vals[:, :, :, 2 + i, q], in_q[q][:, :, :], wpart[i][:, :, :], ALU.mult))
                nc.vector.memset(thr[:, :, :], 0.0).then_inc(s_pos, 1)
                for e in range(E):
                    after(ve, s_used, e - 1)
                    v.tensor_tensor(onehot[:, e % 2, 0:SHARE, :], iota[:, :].rearrange("p (o n) -> p o n", o=1).to_broadcast([P, SHARE, P]),
                                    pos[:, e, 0:SHARE].rearrange("p (t o) -> p t o", o=1).to_broadcast([P, SHARE, P]), ALU.is_equal).then_inc(s_oh, 1)
                ve.wait_ge(s_used, E)
                step(v.tensor_copy(found[:, :, :, :], hits))
                step(v.tensor_tensor(picked[:, :, :], found[:, :, 0, :], found[:, :, 1, :], ALU.add))
                step(v.tensor_tensor(kept[:, :, :, 0], found[:, :, 2, :], found[:, :, 3, :], ALU.add))
                step(v.tensor_tensor(kept[:, :, :, 0], kept[:, :, :, 0], found[:, :, 4, :], ALU.add))


def expert_layer1(nc, io, picked, kept, w, sum_d, norm_d, consts):
    ident, F = consts["ident"], F1
    kept = kept[:, :, :, :].rearrange("p e a o -> p (e a) o")
    with ExitStack() as ctx:
        def sb(name, shape, dt=F32):
            return ctx.enter_context(nc.sbuf_tensor(f"m1_{name}", shape, dt))

        phase = ctx.enter_context(Semaphores(nc))

        def sem(name):
            return phase.take(f"m1_{name}")

        gb = consts["later"]["gb1"]
        idx = sb("idx", [P, E, 4], I32)
        y = sb("y", [P, 2, 4, C])
        yT = sb("yT", [P, 2, CAP])
        hT = sb("hT", [P, 2, 4, CAP])
        ob = sb("ob", [P, 2, 4, C])
        o = sb("o", [P, 2, 4, C])
        ps_x = ctx.enter_context(nc.psum_tensor("m1_ps_x", [P, CAP], F32))
        ps_h = [ctx.enter_context(nc.psum_tensor(f"m1_ps_h{i}", [P, CAP], F32)) for i in range(2)]
        ps_o = [ctx.enter_context(nc.psum_tensor(f"m1_ps_o{i}", [P, CAP], F32)) for i in range(2)]
        s_w = [sem(f"weights_loaded{i}") for i in range(2)]
        s_ix = sem("indices_ready")
        s_y = [sem(f"rows_gathered{i}") for i in range(2)]
        s_yp = sem("rows_transposed")
        s_yT = sem("rows_scaled")
        s_h = sem("hidden_ready")
        s_g = sem("gelu_done")
        s_o = sem("output_ready")
        s_ow = sem("output_weighted")
        s_ob = sem("bias_added")
        s_sc = [sem(f"rows_added{i}") for i in range(2)]

        with nc.Block() as block:
            @block.sync
            def _(sp):

                with sp.Fori(1, E // 2) as k:
                    for u in range(2):
                        sp.wait_ge(s_ob, 2 * k + u - 1)
                        sp.dma_start(w[:, u, :], io["w1"][bass.ds(2 * k + u, 1), :, :].rearrange("e p f -> (e p) f"))\
                            .then_inc(s_w[u], 16)

            @block.gpsimd
            def _(pool):
                def gather(e, a):
                    nc.gpsimd.indirect_dma_start(out=y[:, e % 2, a, :], out_offset=None, in_=norm_d,
                                                 in_offset=bass.IndirectOffsetOnAxis(ap=idx[:, e, a:a + 1], axis=0))\
                        .then_inc(s_y[e % 2], 16)

                pool.wait_ge(s_ix, 1)
                for e in range(2):
                    for a in range(4):
                        gather(e, a)
                for e in range(E):
                    if e + 2 < E:
                        pool.wait_ge(s_yp, e + 1)
                        for a in range(4):
                            gather(e + 2, a)
                    pool.wait_ge(s_ow, e + 1)
                    for a in range(4):
                        after(pool, s_sc[a % 2], 32 * e + 16 * (a // 2))
                        nc.gpsimd.indirect_dma_start(out=sum_d[a % 2],
                                                     out_offset=bass.IndirectOffsetOnAxis(ap=idx[:, e, a:a + 1], axis=0),
                                                     in_=o[:, e % 2, a, :], in_offset=None, compute_op=ALU.add)\
                            .then_inc(s_sc[a % 2], 16)
                for i in range(2):
                    pool.wait_ge(s_sc[i], 32 * E)

            @block.tensor
            def _(pe):
                def transpose(e, k, u):
                    pe.wait_ge(s_y[u], 64 * k + 64)
                    after(pe, s_yT, e)
                    for a in range(4):
                        last = nc.tensor.transpose(ps_x[:, a * P:(a + 1) * P], y[:, u, a, :], ident[:, :])
                    last.then_inc(s_yp, 1)

                def expand(e, k, u):
                    after(pe, s_w[u], 16 * k)
                    pe.wait_ge(s_yT, e + 1)
                    for f in range(4):
                        after(pe, s_g, 4 * e + f - 1)
                        nc.tensor.matmul(ps_h[f % 2][:, :], w[:, u, f * P:(f + 1) * P], yT[:, u, :], start=True, stop=True)\
                            .then_inc(s_h, 1)

                def reduce(e, u, half):
                    if half == 0:
                        after(pe, s_ob, e - 1)
                        pe.wait_ge(s_g, 4 * e + 4)
                    for a in (2 * half, 2 * half + 1):
                        out = ps_o[u][:, a * P:(a + 1) * P]
                        for f in range(4):
                            last = nc.tensor.matmul(out, hT[:, u, f, a * P:(a + 1) * P], w[:, u, F + f * P:F + (f + 1) * P],
                                                    start=a == 0 and f == 0, stop=f == 3, skip_group_check=True)
                    if half:
                        last.then_inc(s_o, 1)

                def pair(k, more=True):
                    expand(2 * k, k, 0)
                    reduce(2 * k, 0, 0)
                    transpose(2 * k + 1, k, 1)
                    reduce(2 * k, 0, 1)
                    expand(2 * k + 1, k, 1)
                    reduce(2 * k + 1, 1, 0)
                    if more:
                        transpose(2 * k + 2, k + 1, 0)
                    reduce(2 * k + 1, 1, 1)

                transpose(0, 0, 0)
                pair(0)
                with pe.Fori(1, E // 2 - 1) as k:
                    pair(k)
                pair(E // 2 - 1, more=False)

            @block.scalar
            def _(act):
                def gelu(e, k, u):
                    after(act, s_o, e - 1)
                    for f in range(4):
                        act.wait_ge(s_h, 4 * e + f + 1)
                        nc.scalar.activation(hT[:, u, f, :], ps_h[f % 2][:, :], ACT.Gelu_apprx_tanh,
                                             bias=w[:, u, 2 * F + f:2 * F + f + 1]).then_inc(s_g, 1)

                for u in range(2):
                    gelu(u, 0, u)
                with act.Fori(1, E // 2) as k:
                    for u in range(2):
                        gelu(2 * k + u, k, u)

            @block.vector
            def _(ve):

                nc.vector.tensor_copy(idx[:, :, :], picked[:, :, :]).then_inc(s_ix, 1)

                def scale(e, u):
                    ve.wait_ge(s_yp, e + 1)
                    after(ve, s_h, 4 * (e - 1))
                    nc.vector.tensor_scalar(yT[:, u, :], ps_x[:, :], gb[:, 0:1], gb[:, 1:2], ALU.mult, ALU.add).then_inc(s_yT, 1)

                def add_bias(e, u):
                    ve.wait_ge(s_o, e + 1)
                    after(ve, s_ow, e - 1)
                    nc.vector.tensor_tensor(ob[:, u, :, :], ps_o[u][:, :].rearrange("p (a c) -> p a c", a=4),
                                            w[:, u:u + 1, 2 * F + 4:W1].to_broadcast([P, 4, C]), ALU.add).then_inc(s_ob, 1)

                def weigh(e, u):
                    ve.wait_ge(s_ob, e + 1)
                    for i in range(2):
                        after(ve, s_sc[i], 32 * (e - 1))
                    nc.vector.tensor_tensor(o[:, u, :, :], ob[:, u, :, :],
                                            kept[:, bass.ds(4 * e, 4), :].to_broadcast([P, 4, C]), ALU.mult).then_inc(s_ow, 1)

                scale(0, 0)
                scale(1, 1)
                add_bias(0, 0)
                weigh(0, 0)
                with ve.Fori(1, E // 2) as k:
                    scale(2 * k, 0)
                    add_bias(2 * k - 1, 1)
                    weigh(2 * k - 1, 1)
                    scale(2 * k + 1, 1)
                    add_bias(2 * k, 0)
                    weigh(2 * k, 0)
                add_bias(E - 1, 1)
                weigh(E - 1, 1)


def write_output(nc, io, xn, stats, norm, sum_d):
    with ExitStack() as ctx:
        phase = ctx.enter_context(Semaphores(nc))

        def sem(name):
            return phase.take(f"w_{name}")

        bns = ctx.enter_context(nc.sbuf_tensor("w_bns", [P, NTILE, 6], F32))
        other = ctx.enter_context(nc.sbuf_tensor("w_other", [P, NTILE, C], F32))
        s_add = sem("sums_joined")
        s_x = [sem(f"sum_loaded{i}") for i in range(4)]
        s_bn = sem("row_stats_taken")
        s_ag = sem("row_stats_merged")
        s_n = sem("tile_normalised")
        s_na = sem("tile_normalised_by_act")
        s_join = sem("sums_joined_by_pool")
        s_shift = sem("shift_ready")
        shift = ctx.enter_context(nc.sbuf_tensor("w_shift", [P, NTILE], F32))
        s_out = sem("output_stored")
        part = NTILE // 4
        src = [d.rearrange("(t p) c -> p t c", p=P) for d in sum_d]
        dst = io["out"].rearrange("(t p) c -> p t c", p=P)

        def join(eng, i):
            here = slice(i * part, (i + 1) * part)
            return eng.tensor_tensor(xn[:, here, :], xn[:, here, :], other[:, here, :], ALU.add)

        with nc.Block() as block:
            @block.sync
            def _(sp):
                for i in range(4):
                    for dst_i, src_i in zip((xn, other), src):
                        sp.dma_start(dst_i[:, i * part:(i + 1) * part, :], src_i[:, i * part:(i + 1) * part, :]).then_inc(s_x[i], 16)
                for n in range(2):
                    for i, done in ((n, s_n), (n + 2, s_na)):
                        sp.wait_ge(done, part * (n + 1))
                        sp.dma_start(dst[:, i * part:(i + 1) * part, :], xn[:, i * part:(i + 1) * part, :]).then_inc(s_out, 16)
                sp.wait_ge(s_out, 64)

            @block.gpsimd
            def _(pool):
                for i in (1, 3):
                    pool.wait_ge(s_x[i], 32)
                    join(nc.gpsimd, i).then_inc(s_join, 1)

            @block.vector
            def _(ve):
                for i in range(4):
                    if i % 2 == 0:
                        ve.wait_ge(s_x[i], 32)
                        join(nc.vector, i).then_inc(s_add, 1)
                        ve.wait_ge(s_add, i // 2 + 1)
                    else:
                        ve.wait_ge(s_join, i // 2 + 1)
                    for t in range(part * i, part * (i + 1)):
                        nc.vector.bn_stats(bns[:, t, :], xn[:, t, :]).then_inc(s_bn, 1)
                merge_stats(nc, ve, stats, bns, s_bn, s_ag)
                norm.vector(ve)
                nc.vector.scalar_tensor_tensor(shift[:, :], stats[:, :, 0], -1.0, norm.rstd[:, :], ALU.mult, ALU.mult).then_inc(s_shift, 1)
                for t in range(NTILE // 2):
                    nc.vector.tensor_scalar(xn[:, t, :], xn[:, t, :], stats[:, t, 0:1], norm.rstd[:, t:t + 1],
                                            ALU.subtract, ALU.mult).then_inc(s_n, 1)

            @block.scalar
            def _(act):
                norm.scalar(act)
                act.wait_ge(s_shift, 1)
                for t in range(NTILE // 2, NTILE):
                    nc.scalar.activation(xn[:, t, :], xn[:, t, :], ACT.Identity, scale=norm.rstd[:, t:t + 1],
                                         bias=shift[:, t:t + 1]).then_inc(s_na, 1)


def merge_stats(nc, ve, stats, bns, s_bn, s_ag):
    ve.wait_ge(s_bn, NTILE)
    for t in range(NTILE):
        nc.vector.bn_aggr(stats[:, t, :], bns[:, t, :]).then_inc(s_ag, 1)
    ve.wait_ge(s_ag, NTILE)


def invert_spread(nc, norm):
    with nc.Block() as block:
        @block.vector
        def _(ve):
            norm.vector(ve)

        @block.scalar
        def _(act):
            norm.scalar(act)


class Norm:

    def __init__(self, nc, ctx, name, stats, n=NTILE):
        self.nc, self.stats, self.n, self.name = nc, stats, n, name
        self.ve = ctx.enter_context(nc.sbuf_tensor(f"{name}_ve", [P, n], F32))
        self.sq = ctx.enter_context(nc.sbuf_tensor(f"{name}_sq", [P, n], F32))
        self.t = ctx.enter_context(nc.sbuf_tensor(f"{name}_t", [P, n], F32))
        self.rstd = ctx.enter_context(nc.sbuf_tensor(f"{name}_rstd", [P, n], F32))
        phase = ctx.enter_context(Semaphores(nc))
        self.s_v = phase.take(f"{name}_variance")
        self.s_q = phase.take(f"{name}_root")
        self.s_r = phase.take(f"{name}_rstd")

    def vector(self, ve, base=0):
        nc = self.nc
        steps = [0]

        def step(ins):
            steps[0] += 1
            ins.then_inc(self.s_r, 1)
            ve.wait_ge(self.s_r, steps[0])

        nc.vector.tensor_scalar(self.ve[:, :], self.stats[:, :, 1], EPS, None, ALU.add).then_inc(self.s_v, 1)
        ve.wait_ge(self.s_q, 1)
        step(nc.vector.reciprocal(self.rstd[:, :], self.sq[:, :]))
        step(nc.vector.tensor_tensor(self.t[:, :], self.rstd[:, :], self.rstd[:, :], ALU.mult))
        step(nc.vector.tensor_tensor(self.t[:, :], self.t[:, :], self.ve[:, :], ALU.mult))
        step(nc.vector.tensor_scalar(self.t[:, :], self.t[:, :], -0.5, 1.5, ALU.mult, ALU.add))
        step(nc.vector.tensor_tensor(self.rstd[:, :], self.rstd[:, :], self.t[:, :], ALU.mult))

    def scalar(self, act):
        act.wait_ge(self.s_v, 1)
        self.nc.scalar.activation(self.sq[:, :], self.ve[:, :], ACT.Sqrt).then_inc(self.s_q, 1)


def program(nc, io):
    with ExitStack() as ctx:
        def sb(name, shape, dt=F32):
            return ctx.enter_context(nc.sbuf_tensor(name, shape, dt))

        phase = ctx.enter_context(Semaphores(nc))

        def sem(name):
            return phase.take(name)

        xn = sb("xn", [P, NTILE, C])
        stats = sb("stats", [P, NTILE, 2])
        consts = {"ident": sb("ident", [P, P]), "ident_bf": sb("ident_bf", [P, P], BF16), 
                  "tri4": sb("tri4", [P, 4, P], BF16), "upper": sb("upper", [P, P]), "ones_sq": sb("ones_sq", [P, P])}
        consts["later"] = {
            "wr": sb("wr", [P, E]), "sel": sb("sel_f", [32, E, P]), "desc": sb("desc", [P, E]), "bgu": sb("bgu", [P, E, 2]),
            "wgu": sb("wgu", [P, E, 2, P]), "wd0": sb("wd", [P, E, C]), "bd0": sb("bd", [32, C]),
            "wqk1": sb("wqk1", [P, 4, P]), "wv1": sb("wv1", [P, P]), "wo1": sb("wo1", [P, P]), "wg1": sb("wg1", [P, E]),
            "iota": sb("iota", [P, P]), "tile0": sb("tile0", [P, NTILE]), "not0": sb("not0", [P, E * NTILE]),
            "row": sb("row", [P, 1]), "gb1": sb("gb1", [P, 2]),
        }
        s_id = sem("ident_loaded")
        with nc.Block() as block:
            @block.sync
            def _(sp):
                sp.dma_start(consts["ident"][:, :], io["ident"]).then_inc(s_id, 16)
                sp.wait_ge(s_id, 16)
        layer0_attention(nc, io, xn, stats, consts)
        norm = Norm(nc, ctx, "norm_a", stats)
        invert_spread(nc, norm)
        expert_layer0(nc, xn, stats, norm, consts)
        norm = Norm(nc, ctx, "norm_b", stats)
        invert_spread(nc, norm)
        layer1_attention(nc, io, xn, stats, norm, consts)
        norm = Norm(nc, ctx, "norm_c", stats)
        invert_spread(nc, norm)
        gate_act = sb("gate_act", [P, E, NTILE])
        stats_y = sb("stats_y", [P, NTILE, 2])
        picked, kept = sb("picked", [P, E, 4]), sb("kept", [P, E, 4, 1])
        w1 = sb("w1", [P, 2, W1])
        score_tokens(nc, xn, stats, stats_y, norm, gate_act, consts)
        norm_y = Norm(nc, ctx, "norm_y", stats_y)
        invert_spread(nc, norm_y)
        sum_d = [nc.dram_tensor(f"sum{i}", [NTOK, C], F32, kind="Internal").ap() for i in range(2)]
        norm_d = nc.dram_tensor("normed", [NTOK, C], F32, kind="Internal").ap()
        choose_tokens(nc, io, xn, stats_y, norm_y, gate_act, picked, kept, w1, sum_d, norm_d, consts)
        expert_layer1(nc, io, picked, kept, w1, sum_d, norm_d, consts)
        write_output(nc, io, xn, stats, Norm(nc, ctx, "norm_d", stats), sum_d)


def kernel(**inputs):
    import numpy as np
    import concourse.bacc as bacc
    from concourse import mybir as _mybir
    from concourse.bass_utils import run_bass_kernel_spmd as run

    a = {k: np.asarray(v) for k, v in inputs.items()}
    f32 = np.float32

    half = HD // 2
    inv_freq = (f32(1.0) / f32(10000.0) ** (np.arange(half, dtype=f32) / f32(half))).astype(f32)
    freqs = np.arange(T, dtype=f32)[None, :] * inv_freq[:, None]
    cos = np.repeat(np.repeat(np.cos(freqs), 2, axis=0), H, axis=0).astype(f32)
    sin = np.repeat(np.repeat(np.sin(freqs), 2, axis=0), H, axis=0).astype(f32)
    sign = np.where((np.arange(P) // H) % 2 == 0, f32(-1.0), f32(1.0))[:, None]
    rot = np.ascontiguousarray(np.stack([cos, sin * sign], axis=1).astype(f32))

    dh = np.arange(P).reshape(H, HD).T.reshape(-1)
    swap = np.arange(HD) ^ 1
    dh_swap = np.arange(P).reshape(H, HD)[:, swap].T.reshape(-1)
    wqkv = a["L0_attn_Wqkv"]
    wqk = np.stack([wqkv[:, dh], wqkv[:, dh_swap], wqkv[:, P + dh], wqkv[:, P + dh_swap]], axis=1)
    x = a["L0_attn_x"].reshape(NTOK, C)
    host = {
        "x": x, "xT": x.T, "wqk": wqk, "rot": rot, "wv": wqkv[:, 2 * P:], "wo": a["L0_attn_Wo"],
        "bo": np.broadcast_to(a["L0_attn_bo"], (P, C)), "tri": np.where(np.tril(np.ones((P, P), bool)), f32(0), f32(-BIG)),
        "ident": np.eye(P, dtype=f32), "upper": np.triu(np.ones((P, P), f32)),
    }
    gu = a["L0_ffn_gate_up_proj"].reshape(E, C, P, 2)
    sel = np.zeros((32, E, P), f32)
    for part in range(3):
        sel[part * E + np.arange(E), np.arange(E)] = 1
    host.update({
        "wr": a["L0_ffn_router_weight"], "wgu": gu.transpose(1, 0, 3, 2),
        "bgu": a["L0_ffn_gate_up_proj_bias"].reshape(E, P, 2).transpose(1, 0, 2),
        "wd0": a["L0_ffn_down_proj"].transpose(1, 0, 2), "bd0": np.concatenate([a["L0_ffn_down_proj_bias"]] * 3 + [np.zeros((32 - 3 * E, C), f32)]),
        "sel": sel, "desc": np.broadcast_to(np.arange(E, 0, -1).astype(f32), (P, E)),
    })
    dh1 = np.arange(H * FD).reshape(H, FD).T.reshape(2, P)
    wqk1 = np.stack([a[w].T[:, half] for w in ("L1_attn_Wq", "L1_attn_Wk") for half in dh1], axis=1)
    host.update({"wqk1": wqk1, "wv1": a["L1_attn_Wv"].T, "wo1": a["L1_attn_Wo"].T})
    fc1T = a["L1_ffn_fc1s"].transpose(0, 2, 1)
    fc2T = a["L1_ffn_fc2s"].transpose(0, 2, 1).reshape(E, 4, P, C).transpose(0, 2, 1, 3).reshape(E, P, 4 * C)
    b1T = a["L1_ffn_b1s"].reshape(E, 4, P).transpose(0, 2, 1)
    host.update({
        "wg1": a["L1_ffn_gate_w"].T, "w1": np.concatenate(
            [fc1T, fc2T, b1T, np.broadcast_to(a["L1_ffn_b2s"][:, None, :], (E, P, C))], axis=2),
        "gb1": np.stack([a["L1_ffn_ln_gamma"], a["L1_ffn_ln_beta"]], axis=1),
        "iota": np.broadcast_to(np.arange(P, dtype=f32), (P, P)),
        "tile0": np.broadcast_to(P * np.arange(NTILE, dtype=f32), (P, NTILE)),
        "not0": np.broadcast_to((np.arange(E * NTILE) % NTILE != 0).astype(f32), (P, E * NTILE)),
        "row": np.arange(P, dtype=f32).reshape(P, 1),
    })
    nc = bacc.Bacc("TRN2", target_bir_lowering=False, num_devices=1)
    arrays, io = {}, {}
    for name, v in host.items():
        v = np.ascontiguousarray(v)
        arrays[f"in_{name}"] = v
        io[name] = nc.dram_tensor(f"in_{name}", v.shape, _mybir.dt.from_np(v.dtype), kind="ExternalInput").ap()
    io["out"] = nc.dram_tensor("out_x", (NTOK, C), F32, kind="ExternalOutput").ap()
    program(nc, io)
    r = run(nc, [arrays], core_ids=[0])
    return r.results[0]["out_x"].reshape(NB, T, C)
```
